# Optimizing a Trainium2 kernel written in Bass

```python
import numpy as np
import jax
import jax.numpy as jnp

def _softmax(x, axis=-1):
    return jax.nn.softmax(x, axis=axis)

def _gelu(x):
    return jax.nn.gelu(x, approximate=True)

def _silu(x):
    return jax.nn.silu(x)

def _sigmoid(x):
    return jax.nn.sigmoid(x)

def _layernorm(x, axis=-1, eps=1e-05):
    m = jnp.mean(x, axis=axis, keepdims=True)
    v = jnp.var(x, axis=axis, keepdims=True)
    return (x - m) / jnp.sqrt(v + eps)

def _scatter_add(tgt, idx, src, axis=0):
    return tgt.at[idx].add(src)

def _segment_sum(src, seg, n):
    return jax.ops.segment_sum(src, seg, n)
kernel_name = 'mk_xattn_ffn_d1_seqx_r4_c22534'

def setup_inputs(seed: int=0):
    np.random.seed(seed)
    _w = jnp.asarray

    def _rec_inputs():
        import jax
        import jax.numpy as jnp
        _rk = jax.random.key(seed)
        x = -0.0002928 + 1 * jax.random.normal(jax.random.fold_in(_rk, 1), (8, 512, 256), jnp.float32)
        _lenS = 512 - jax.random.randint(jax.random.fold_in(_rk, 7), (8,), 0, max(1, 512 // 4) + 1, jnp.int32)
        _lenS2 = 1024 - jax.random.randint(jax.random.fold_in(_rk, 8), (8,), 0, max(1, 1024 // 4) + 1, jnp.int32)
        _ctx_1024P = jax.random.normal(jax.random.fold_in(_rk, 11), (8, 16, 256), jnp.float32)
        _ctx_1024c = jax.random.dirichlet(jax.random.fold_in(_rk, 511), 0.3 * jnp.ones((16,), jnp.float32), (8, 1024))
        _ctx_1024t = jnp.einsum('bsk,bkd->bsd', _ctx_1024c, _ctx_1024P)
        _ctx_1024t = _ctx_1024t * jax.lax.rsqrt(jnp.mean(jnp.square(_ctx_1024t)) + 1e-12) * 0.953939
        ctx_1024 = -1.39393e-06 + 0.999914 * (_ctx_1024t + 0.3 * jax.random.normal(jax.random.fold_in(_rk, 611), (8, 1024, 256), jnp.float32))
        _validS = jnp.arange(512)[None, :] < _lenS[:, None]
        _validS2 = jnp.arange(1024)[None, :] < _lenS2[:, None]
        _causal = jnp.tril(jnp.ones((512, 512), dtype=bool))
        mask_BxSxS2_bk0 = jnp.logical_not(jnp.broadcast_to(_validS2[:, None, :], (8, 512, 1024)))
        return (x, ctx_1024, mask_BxSxS2_bk0)
    x, ctx_1024, mask_BxSxS2_bk0 = _rec_inputs()

    def _L0_xattn_setup():
        import jax, jax.numpy as jnp
        import numpy as np
        D_MODEL = 256
        N_HEADS = 16
        HEAD_DIM = D_MODEL // N_HEADS
        BATCH = 2
        SEQ = 512
        key = jax.random.key(seed)
        ks = jax.random.split(key, 8)
        scale = 1.0 / np.sqrt(D_MODEL)
        q = jax.random.normal(ks[0], (BATCH, SEQ, D_MODEL), dtype=jnp.float32)
        k = jax.random.normal(ks[1], (BATCH, SEQ, D_MODEL), dtype=jnp.float32)
        v = jax.random.normal(ks[2], (BATCH, SEQ, D_MODEL), dtype=jnp.float32)
        mask = jax.random.bernoulli(ks[3], 0.1, (BATCH, SEQ, SEQ))
        w_q = jax.random.normal(ks[4], (D_MODEL, D_MODEL), dtype=jnp.float32) * scale
        w_k = jax.random.normal(ks[5], (D_MODEL, D_MODEL), dtype=jnp.float32) * scale
        w_v = jax.random.normal(ks[6], (D_MODEL, D_MODEL), dtype=jnp.float32) * scale
        w_o = jax.random.normal(ks[7], (D_MODEL, D_MODEL), dtype=jnp.float32) * scale
        return {'q': q, 'k': k, 'v': v, 'mask': mask, 'w_q': w_q, 'w_k': w_k, 'w_v': w_v, 'w_o': w_o}
    _L0_xattn_all = _L0_xattn_setup()
    _L0_xattn_in = {k: v for k, v in _L0_xattn_all.items() if k in ('w_q', 'w_k', 'w_v', 'w_o')}
    del _L0_xattn_all

    def _L0_ffn_setup():
        import math
        import jax, jax.numpy as jnp
        import numpy as np
        B, T, D = (4, 1024, 256)
        H = 16
        HD = D // H
        CAP = int(1024 * 0.125)
        DFF = int(D * 4 * 2 / 3)
        EPS = 1e-06

        def rmsnorm(x, g):
            return x * jax.lax.rsqrt(jnp.mean(x * x, axis=-1, keepdims=True) + EPS) * g
        key = jax.random.key(seed)
        ks = jax.random.split(key, 9)
        s = lambda k, shape: jax.random.normal(k, shape, jnp.float32) * 0.02
        return {'x': jax.random.normal(ks[0], (B, T, D), jnp.float32), 'w_router': s(ks[1], (D,)), 'W_qkv': s(ks[2], (3 * D, D)), 'W_out': s(ks[3], (D, D)), 'g1': jnp.ones((D,), jnp.float32), 'g2': jnp.ones((D,), jnp.float32), 'W1': s(ks[4], (DFF, D)), 'W2': s(ks[5], (DFF, D)), 'W3': s(ks[6], (D, DFF))}
    _L0_ffn_all = _L0_ffn_setup()
    _L0_ffn_in = {k: v for k, v in _L0_ffn_all.items() if k in ('w_router', 'W_qkv', 'W_out', 'g1', 'g2', 'W1', 'W2', 'W3')}
    del _L0_ffn_all
    return {'x': x, 'ctx_1024': ctx_1024, 'mask_BxSxS2_bk0': mask_BxSxS2_bk0, 'L0_xattn_w_q': _L0_xattn_in['w_q'], 'L0_xattn_w_k': _L0_xattn_in['w_k'], 'L0_xattn_w_v': _L0_xattn_in['w_v'], 'L0_xattn_w_o': _L0_xattn_in['w_o'], 'L0_ffn_w_router': _L0_ffn_in['w_router'], 'L0_ffn_W_qkv': _L0_ffn_in['W_qkv'], 'L0_ffn_W_out': _L0_ffn_in['W_out'], 'L0_ffn_g1': _L0_ffn_in['g1'], 'L0_ffn_g2': _L0_ffn_in['g2'], 'L0_ffn_W1': _L0_ffn_in['W1'], 'L0_ffn_W2': _L0_ffn_in['W2'], 'L0_ffn_W3': _L0_ffn_in['W3']}

def reference(x, ctx_1024, mask_BxSxS2_bk0, L0_xattn_w_q, L0_xattn_w_k, L0_xattn_w_v, L0_xattn_w_o, L0_ffn_w_router, L0_ffn_W_qkv, L0_ffn_W_out, L0_ffn_g1, L0_ffn_g2, L0_ffn_W1, L0_ffn_W2, L0_ffn_W3):
    import jax
    import jax.numpy as jnp

    def _L0_xattn_ref(q, k, v, mask, w_q, w_k, w_v, w_o):
        import jax, jax.numpy as jnp
        import numpy as np
        D_MODEL = 256
        N_HEADS = 16
        HEAD_DIM = D_MODEL // N_HEADS
        BATCH = 2
        SEQ = 512
        B, S, _ = q.shape

        def split_heads(x, w):
            y = x @ w.T
            return y.reshape(B, -1, N_HEADS, HEAD_DIM).transpose(0, 2, 1, 3)
        query = split_heads(q, w_q)
        key_ = split_heads(k, w_k)
        value = split_heads(v, w_v)
        scores = jnp.einsum('bhqd,bhkd->bhqk', query, key_) / np.sqrt(HEAD_DIM)
        scores = jnp.where(mask[:, None, :, :], jnp.float32(-1000000000.0), scores)
        attention = jax.nn.softmax(scores, axis=-1)
        out = jnp.einsum('bhqk,bhkd->bhqd', attention, value)
        out = out.transpose(0, 2, 1, 3).reshape(B, -1, N_HEADS * HEAD_DIM)
        return out @ w_o.T

    def _L0_ffn_ref(x, w_router, W_qkv, W_out, g1, g2, W1, W2, W3):
        import math
        import jax, jax.numpy as jnp
        import numpy as np
        B, T, D = (4, 1024, 256)
        H = 16
        HD = D // H
        CAP = int(1024 * 0.125)
        DFF = int(D * 4 * 2 / 3)
        EPS = 1e-06

        def rmsnorm(x, g):
            return x * jax.lax.rsqrt(jnp.mean(x * x, axis=-1, keepdims=True) + EPS) * g
        Bq, Tq, Dq = x.shape
        scores = x @ w_router
        _, idx = jax.lax.top_k(scores, CAP)
        x_sel = jnp.take_along_axis(x, idx[:, :, None], axis=1)
        h = rmsnorm(x_sel, g1)
        qkv = (h @ W_qkv.T).reshape(Bq, CAP, 3, H, HD)
        q, k, v = jnp.moveaxis(qkv, 2, 0)
        att = jnp.einsum('bqhd,bkhd->bhqk', q, k) / math.sqrt(HD)
        mask = jnp.triu(jnp.ones((CAP, CAP), bool), 1)
        att = jnp.where(mask, -jnp.inf, att)
        att = jax.nn.softmax(att, axis=-1)
        o = jnp.einsum('bhqk,bkhd->bqhd', att, v).reshape(Bq, CAP, Dq)
        x_attn = o @ W_out.T
        h2 = rmsnorm(x_sel + x_attn, g2)
        x_ff = jax.nn.silu(h2 @ W1.T) * (h2 @ W2.T) @ W3.T
        x_proc = x_sel + x_attn + x_ff
        out = x.at[jnp.arange(Bq)[:, None], idx].set(x_proc)
        return out
    x = x + _L0_xattn_ref(_layernorm(x, axis=-1), ctx_1024, ctx_1024, mask_BxSxS2_bk0, L0_xattn_w_q, L0_xattn_w_k, L0_xattn_w_v, L0_xattn_w_o)
    x = x + _L0_ffn_ref(_layernorm(x, axis=-1), L0_ffn_w_router, L0_ffn_W_qkv, L0_ffn_W_out, L0_ffn_g1, L0_ffn_g2, L0_ffn_W1, L0_ffn_W2, L0_ffn_W3)
    return x

_drawn_inputs = setup_inputs


def setup_inputs(seed=0):
    import zlib

    import numpy as np

    out = dict(_drawn_inputs(seed))
    spreads = {'L0_ffn_g1': (1.0, 0.6), 'L0_ffn_g2': (1.0, 0.6)}
    factors = {'L0_ffn_w_router': 4.586,
     'L0_ffn_W_qkv': 4.941,
     'L0_ffn_W_out': 4.664,
     'L0_ffn_W1': 8.0,
     'L0_ffn_W2': 8.0,
     'L0_ffn_W3': 8.0}
    for name, (base, spread) in spreads.items():
        noise = np.random.default_rng([zlib.crc32(name.encode()), seed]).standard_normal(out[name].shape)
        drawn = base * np.exp(spread * noise) if base else spread * noise
        out[name] = jnp.asarray(drawn.astype(out[name].dtype))
    for name, factor in factors.items():
        out[name] = (out[name] * factor).astype(out[name].dtype)
    return out
```

```python
from contextlib import ExitStack

import concourse.bass as bass
from concourse import mybir

P = 128
B = 8
S = 512
SK = 1024
D = 256
H = 16
HD = D // H
KC = D // P
QT = S // P
KT = SK // P
M2 = 2
H8 = H // M2
G = 4
HG = H // G
NPAIR = 6
K_PART = [0, 0, 0, 1, 1, 2]
Q_PART = [0, 1, 2, 0, 1, 0]
K_RUNS = [(0, 0, 3, 1), (1, 3, 2, 1), (2, 5, 1, 1)]
Q_RUNS = [(0, 0, 2, 3), (0, 5, 1, 1), (1, 1, 2, 3), (2, 2, 1, 1)]
N_RUNS = len(K_RUNS) + len(Q_RUNS)
ROW_MASK = NPAIR * HD
ROW_MAX = ROW_MASK + 1
ROWS = ROW_MAX + 3
CAP = 128
DFF = 682
FT = 6
BIG = 2.0 ** 30
SAFE = 60.0
LN_EPS = 1e-5
RMS_EPS = 1e-6

F32 = mybir.dt.float32
BF16 = mybir.dt.bfloat16
U8 = mybir.dt.uint8
I32 = mybir.dt.int32
ALU = mybir.AluOpType
ACT = mybir.ActivationFunctionType
AX = mybir.AxisListType




def program(nc, io, out):
    dram = lambda name, shape, dt: nc.dram_tensor(name, shape, dt, kind="Internal").ap()
    ks_dram = dram("ks_scratch", (B, M2, ROWS, H8, SK), BF16)
    qs_dram = dram("qs_scratch", (B, M2, ROWS, H8, S), BF16)
    v_dram = dram("v_scratch", (B, SK, D), F32)
    mask_dram = dram("mask_scratch", (B, S, SK), BF16)

    with ExitStack() as top:
        sb = lambda name, shape, dt=F32: top.enter_context(nc.sbuf_tensor(name, shape, dt))
        bank = [top.enter_context(nc.psum_tensor(f"bank{i}", [P, 512], F32)) for i in range(4, 8)]
        pair_bank = [top.enter_context(nc.psum_tensor(f"pair_bank{i}", [P, 2, 512], F32)) for i in range(2)]
        banks8 = [pair_bank[0][:, 0], pair_bank[0][:, 1], pair_bank[1][:, 0], pair_bank[1][:, 1]] + [b[:] for b in bank]
        ident = sb("ident", [P, P])
        flags = sb("flags", [1, 2])
        flags_i = sb("flags_i", [1, 1], I32)
        project_phase(nc, top, io, ks_dram, qs_dram, v_dram, banks8, ident, flags, flags_i)
        maximum_phase(nc, top, io, ks_dram, qs_dram, mask_dram, pair_bank, bank, ident, flags_i)
        main_phase(nc, top, io, out, ks_dram, qs_dram, v_dram, mask_dram, pair_bank, bank, ident, flags_i)


def project_phase(nc, top, io, ks_dram, qs_dram, v_dram, banks, ident, flags, flags_i):
    with ExitStack() as ctx:
        sb = lambda name, shape, dt=F32: ctx.enter_context(nc.sbuf_tensor(name, shape, dt))
        sem = lambda name: top.enter_context(nc.semaphore(name))
        wq, wk, wv = (sb(n, [P, KC, D]) for n in ("wq_sb", "wk_sb", "wv_sb"))
        x_sb = [sb(f"x_in{i}", [P, QT, D]) for i in range(2)]
        ctx_sb = [sb(f"ctx_in{i}", [P, KC, SK]) for i in range(2)]
        mask_u8 = [sb(f"mask_in{i}", [P, QT, SK], U8) for i in range(2)]
        mask_bf = sb("mask_bf", [P, QT, SK], BF16)
        masked = sb("masked", [P, QT])
        ones_bf = sb("ones_bf", [P, 1], BF16)
        block_of = sb("block_of", [P, H8])
        stats = sb("stats", [P, QT, 6])
        mv = sb("mv", [P, QT, 2])
        veps = sb("veps", [P, QT])
        neg_half = sb("neg_half", [P, QT])
        rstd = sb("rstd", [P, QT])
        rn = sb("rn", [P, QT])
        has_key = sb("has_key", [P, QT])
        zeros_bf = sb("zeros_bf", [3, H8 * S], BF16)
        xn = sb("xn", [P, QT, D])
        xnT = sb("xnT", [P, KC, S])
        nf_row = sb("nf_row", [1, S], BF16)
        parts_q = [sb(f"parts_q{m}", [P, 3, S], BF16) for m in range(M2)]
        parts_k = [sb(f"parts_k{m}", [P, 3, SK], BF16) for m in range(M2)]
        rest = [sb(f"rest{i}", [P, 512]) for i in range(2)]
        v_sb = sb("v_sb", [P, KT, D])
        absmax = sb("absmax", [P, 6])
        ab = sb("ab", [P, M2])
        bound = sb("bound", [1, H])
        bound1 = sb("bound1", [1, 2])
        c_row = sb("c_row", [1, SK])
        c_tmp = sb("c_tmp", [1, SK])
        k_only = sb("k_only", [1, 2])
        k_row = sb("k_row", [1, SK], BF16)

        w_in, const_ready, const_ready_pe = sem("w_in"), sem("const_ready"), sem("const_ready_pe")
        x_in = [sem(f"x_in_s{i}") for i in range(2)]
        ctx_in = [sem(f"ctx_in_s{i}") for i in range(2)]
        mask_in = [sem(f"mask_in_s{i}") for i in range(2)]
        x_free, ctx_free, mask_free = sem("x_free"), sem("ctx_free"), sem("mask_free")
        var_ready, rstd_ready, masked_ready = sem("var_ready"), sem("rstd_ready"), sem("masked_ready")
        xn_ready, nf_t_ready = sem("xn_ready"), sem("nf_t_ready")
        xT_ready, xT_sb_ready = sem("xT_ready"), sem("xT_sb_ready")
        qk_ready, head_part_ready = sem("qk_ready"), sem("head_part_ready")
        rest_ready, rest_used = sem("rest_ready"), sem("rest_used")
        parts_ready = [sem(f"parts_ready{m}") for m in range(M2)]
        parts_stored = [sem(f"parts_stored{m}") for m in range(M2)]
        v_ready, v_sb_ready, v_stored = sem("v_ready"), sem("v_sb_ready"), sem("v_stored")
        c_ready, c_sb_ready = sem("c_ready"), sem("c_sb_ready")
        rows_ready, rows_stored = sem("rows_ready"), sem("rows_stored")
        ab_ready, bound_ready = sem("ab_ready"), sem("bound_ready")
        maskbf_free = sem("maskbf_free")
        bank_free = [sem(f"bank_free{i}") for i in range(8)]
        zeros_ready, zeros_stored = sem("zeros_ready"), sem("zeros_stored")

        USE = {"xT0": 0, "xT1": 1, "nf": 2, "q0": 3, "q1": 4, "k00": 5, "k01": 6, "k10": 7, "k11": 0,
               "v0": 1, "v1": 2, "v2": 3, "v3": 4, "c0": 5, "c1": 6, "bound": 7}
        qk_tiles = [("q", 0, 0), ("q", 1, 0), ("k", 0, 0), ("k", 0, 1), ("k", 1, 0), ("k", 1, 1)]
        tile_bank = lambda kind, m, half: banks[USE[f"q{m}" if kind == "q" else f"k{m}{half}"]]
        tile_free = lambda kind, m, half: bank_free[USE[f"q{m}" if kind == "q" else f"k{m}{half}"]]

        def part(kind, m, half, j):
            return parts_q[m][:, j, :] if kind == "q" else parts_k[m][:, j, half * 512:(half + 1) * 512]

        block = ctx.enter_context(nc.Block())

        @block.sync
        def _(sp):
            for w, src in ((wq, io["wqT"]), (wk, io["wkT"]), (wv, io["wvT"])):
                sp.dma_start(w[:], src.rearrange("(c p) n -> p c n", p=P)).then_inc(w_in, 16)

            sp.wait_ge(zeros_ready, 1)
            sp.sem_inc(zeros_ready, -1)
            for b in range(B):
                for m in range(M2):
                    sp.dma_start(qs_dram[b, m, ROW_MAX:ROWS].rearrange("r h k -> r (h k)"), zeros_bf[:]
                                 ).then_inc(zeros_stored, 16)

            def load(b, i):
                sp.wait_ge(x_free, 1)
                sp.sem_inc(x_free, -1)
                sp.dma_start(x_sb[i][:], io["x"][b].rearrange("(t p) d -> p t d", p=P)).then_inc(x_in[i], 16)
                sp.wait_ge(mask_free, 1)
                sp.sem_inc(mask_free, -1)
                sp.dma_start(mask_u8[i][:], io["mask"][b].rearrange("(t p) k -> p t k", p=P)).then_inc(mask_in[i], 16)
                sp.wait_ge(ctx_free, 1)
                sp.sem_inc(ctx_free, -1)
                sp.dma_start(ctx_sb[i][:], io["ctxT"][b].rearrange("(c p) k -> p c k", p=P)).then_inc(ctx_in[i], 16)

            def store(b):
                for m in range(M2):
                    sp.wait_ge(parts_ready[m], 3)
                    sp.sem_inc(parts_ready[m], -3)
                    for parts, dst, runs in ((parts_q[m], qs_dram, Q_RUNS), (parts_k[m], ks_dram, K_RUNS)):
                        blocks = dst[b, m, 0:ROW_MASK].rearrange("(r d) h k -> (d h) r k", d=HD)
                        for j, r0, n, step in runs:
                            src = parts[:, j, :].unsqueeze(1)
                            sp.dma_start(blocks[:, r0:r0 + (n - 1) * step + 1:step, :],
                                         src.broadcast_to([P, n, src.shape[2]])).then_inc(parts_stored[m], 16)
                sp.wait_ge(v_sb_ready, 4)
                sp.sem_inc(v_sb_ready, -4)
                sp.dma_start(v_dram[b].rearrange("(t p) n -> p t n", p=P), v_sb[:]).then_inc(v_stored, 16)
                sp.wait_ge(rows_ready, 1)
                sp.sem_inc(rows_ready, -1)
                for m in range(M2):
                    sp.dma_start(ks_dram[b, m, ROW_MASK], k_row[0:1, :].unsqueeze(1).broadcast_to([1, H8, SK])
                                 ).then_inc(rows_stored, 16)
                    sp.dma_start(qs_dram[b, m, ROW_MASK], nf_row[0:1, :].unsqueeze(1).broadcast_to([1, H8, S])
                                 ).then_inc(rows_stored, 16)

            load(0, 0)
            with sp.Fori(0, B - 2, 2) as b:
                for i in range(2):
                    load(b + i + 1, 1 - i)
                    store(b + i)
            load(B - 1, 1)
            store(B - 2)
            store(B - 1)
            sp.wait_ge(zeros_stored, 16 * B * M2)

        @block.gpsimd
        def _(pool):
            nc.gpsimd.memset(zeros_bf[:], 0.0).then_inc(zeros_ready, 1)
            nc.gpsimd.memset(ident[:], 0.0)
            nc.gpsimd.memset(ones_bf[:], 1.0)
            nc.gpsimd.memset(neg_half[:], -0.5)
            nc.gpsimd.memset(block_of[:], 0.0)
            nc.gpsimd.memset(flags[:], 0.0)
            pool.drain()
            nc.gpsimd.affine_select(out=ident[:], in_=ident[:], compare_op=ALU.not_equal, fill=1.0, base=0,
                                    pattern=[[-1, P]], channel_multiplier=1)
            for d in range(HD):
                last = nc.gpsimd.affine_select(out=block_of[:], in_=block_of[:], compare_op=ALU.not_equal, fill=1.0,
                                               base=-H8 * d, pattern=[[-1, H8]], channel_multiplier=1)
                pool.drain()
            pool.drain().then_inc(const_ready, 1)
            pool.drain().then_inc(const_ready_pe, 1)
            with pool.Fori(0, B) as b:
                pool.wait_ge(var_ready, 1)
                pool.sem_inc(var_ready, -1)
                nc.gpsimd.tensor_scalar(veps[:], mv[:, :, 1], LN_EPS, None, ALU.add)
                pool.drain()
                nc.gpsimd.tensor_tensor(rstd[:], veps[:], neg_half[:], ALU.pow).then_inc(rstd_ready, 1)
                for n, (kind, m, half) in enumerate(qk_tiles):
                    pool.wait_ge(rest_ready, 1)
                    pool.sem_inc(rest_ready, -1)
                    nc.gpsimd.tensor_copy(part(kind, m, half, 1), rest[n % 2][:])
                    pool.drain()
                    nc.gpsimd.tensor_tensor(part(kind, m, half, 2), rest[n % 2][:], part(kind, m, half, 1),
                                            ALU.subtract).then_inc(rest_used, 1)
                    pool.drain().then_inc(parts_ready[m], 1)

        @block.scalar
        def _(act):
            with act.Fori(0, B // 2) as bb:
                for i in range(2):
                    b = bb * 2 + i
                    act.wait_ge(mask_in[i], 16)
                    act.sem_inc(mask_in[i], -16)
                    act.wait_ge(maskbf_free, 1)
                    act.sem_inc(maskbf_free, -1)
                    for t in range(QT):
                        nc.scalar.activation(mask_bf[:, t], mask_u8[i][:, t], ACT.Copy,
                                             accum_out=masked[:, t:t + 1])
                    act.drain().then_inc(mask_free, 1)
                    act.drain().then_inc(masked_ready, 1)
                    act.wait_ge(xT_ready, 2)
                    act.sem_inc(xT_ready, -2)
                    for kc in range(KC):
                        nc.scalar.activation(xnT[:, kc], banks[USE[f"xT{kc}"]], ACT.Copy
                                             ).then_inc(bank_free[USE[f"xT{kc}"]], 1)
                    act.drain().then_inc(xT_sb_ready, 1)
                    for n, (kind, m, half) in enumerate(qk_tiles):
                        act.wait_ge(qk_ready, 1)
                        act.sem_inc(qk_ready, -1)
                        if kind == "q":
                            act.wait_ge(parts_stored[m], 16 * N_RUNS)
                            act.sem_inc(parts_stored[m], -16 * N_RUNS)
                        nc.scalar.activation(part(kind, m, half, 0), tile_bank(kind, m, half), ACT.Copy
                                             ).then_inc(head_part_ready, 1)
                    act.wait_ge(v_stored, 16)
                    act.sem_inc(v_stored, -16)
                    for n in range(4):
                        act.wait_ge(v_ready, 1)
                        act.sem_inc(v_ready, -1)
                        nc.scalar.activation(v_sb[:, 2 * n:2 * n + 2, :], banks[USE[f"v{n}"]], ACT.Copy
                                             ).then_inc(bank_free[USE[f"v{n}"]], 1)
                        act.drain().then_inc(v_sb_ready, 1)
                    act.wait_ge(c_ready, 2)
                    act.sem_inc(c_ready, -2)
                    for n in range(2):
                        nc.scalar.activation(c_row[0:1, n * 512:(n + 1) * 512], banks[USE[f"c{n}"]][0:1, :], ACT.Copy
                                             ).then_inc(bank_free[USE[f"c{n}"]], 1)
                    act.drain().then_inc(c_sb_ready, 1)

        @block.vector
        def _(dve):
            for s in bank_free:
                dve.sem_inc(s, 1)
            dve.sem_inc(maskbf_free, 1)
            dve.sem_inc(rest_used, 2)
            dve.sem_inc(v_stored, 16)
            dve.sem_inc(rows_stored, 64)
            for m in range(M2):
                dve.sem_inc(parts_stored[m], 16 * N_RUNS)
            dve.sem_inc(x_free, 2)
            dve.sem_inc(ctx_free, 2)
            dve.sem_inc(mask_free, 2)
            dve.wait_ge(const_ready, 1)
            dve.sem_inc(const_ready, -1)
            with dve.Fori(0, B // 2) as bb:
                for i in range(2):
                    b = bb * 2 + i
                    dve.wait_ge(x_in[i], 16)
                    dve.sem_inc(x_in[i], -16)
                    for t in range(QT):
                        nc.vector.bn_stats(stats[:, t], x_sb[i][:, t])
                    dve.drain()
                    for t in range(QT):
                        nc.vector.bn_aggr(mv[:, t], stats[:, t])
                    dve.drain().then_inc(var_ready, 1)
                    dve.wait_ge(masked_ready, 1)
                    dve.sem_inc(masked_ready, -1)
                    nc.vector.tensor_scalar(has_key[:], masked[:], float(SK), None, ALU.is_lt)
                    dve.wait_ge(rstd_ready, 1)
                    dve.sem_inc(rstd_ready, -1)
                    dve.drain()
                    nc.vector.tensor_tensor(rn[:], rstd[:], has_key[:], ALU.mult)
                    dve.drain()
                    for t in range(QT):
                        nc.vector.tensor_scalar(xn[:, t], x_sb[i][:, t], mv[:, t, 0:1], rn[:, t:t + 1],
                                                ALU.subtract, ALU.mult)
                    dve.drain().then_inc(xn_ready, 1)
                    dve.drain().then_inc(x_free, 1)
                    dve.wait_ge(nf_t_ready, 1)
                    dve.sem_inc(nf_t_ready, -1)
                    dve.wait_ge(rows_stored, 64)
                    dve.sem_inc(rows_stored, -64)
                    nc.vector.tensor_copy(nf_row[0:1, :], banks[USE["nf"]][0:1, :]).then_inc(bank_free[USE["nf"]], 1)
                    for n, (kind, m, half) in enumerate(qk_tiles):
                        dve.wait_ge(head_part_ready, 1)
                        dve.sem_inc(head_part_ready, -1)
                        dve.wait_ge(rest_used, 1)
                        dve.sem_inc(rest_used, -1)
                        nc.vector.tensor_tensor(rest[n % 2][:], tile_bank(kind, m, half), part(kind, m, half, 0),
                                                ALU.subtract).then_inc(rest_ready, 1)
                        nc.vector.tensor_reduce(absmax[:, n:n + 1], tile_bank(kind, m, half), op=ALU.max, axis=AX.X,
                                                apply_absolute_value=True).then_inc(tile_free(kind, m, half), 1)
                    dve.drain()
                    nc.vector.tensor_tensor(absmax[:, 2:6:2], absmax[:, 2:6:2], absmax[:, 3:6:2], ALU.max)
                    dve.drain()
                    nc.vector.tensor_tensor(ab[:], absmax[:, 0:2], absmax[:, 2:6:2], ALU.mult).then_inc(ab_ready, 1)
                    dve.wait_ge(c_sb_ready, 1)
                    dve.sem_inc(c_sb_ready, -1)
                    nc.vector.scalar_tensor_tensor(out=c_tmp[:], in0=c_row[:], scalar=-float(S), in1=c_row[:],
                                                   op0=ALU.add, op1=ALU.mult)
                    dve.drain()
                    nc.vector.tensor_reduce(k_only[0:1, 0:1], c_tmp[:], op=ALU.min, axis=AX.X)
                    dve.drain()
                    nc.vector.tensor_scalar(k_only[0:1, 1:2], k_only[0:1, 0:1], 0.0, None, ALU.is_ge)
                    dve.drain()
                    nc.vector.tensor_scalar(k_row[0:1, :], c_row[:], -BIG / S, k_only[0:1, 1:2], ALU.mult, ALU.mult)
                    nc.vector.tensor_scalar(k_only[0:1, 0:1], k_only[0:1, 1:2], -1.0, 1.0, ALU.mult, ALU.add)
                    dve.wait_ge(bound_ready, 1)
                    dve.sem_inc(bound_ready, -1)
                    nc.vector.tensor_reduce(bound1[0:1, 0:1], banks[USE["bound"]][0:1, 0:H], op=ALU.max, axis=AX.X
                                            ).then_inc(bank_free[USE["bound"]], 1)
                    dve.drain().then_inc(rows_ready, 1)
                    nc.vector.tensor_scalar(bound1[0:1, 1:2], bound1[0:1, 0:1], SAFE * HD ** 0.5, None, ALU.is_le)
                    dve.drain()
                    nc.vector.tensor_scalar(bound1[0:1, 0:1], bound1[0:1, 1:2], -1.0, 1.0, ALU.mult, ALU.add)
                    dve.drain()
                    nc.vector.tensor_tensor(flags[0:1, 0:1], flags[0:1, 0:1], k_only[0:1, 0:1], ALU.max)
                    nc.vector.tensor_tensor(flags[0:1, 1:2], flags[0:1, 1:2], bound1[0:1, 0:1], ALU.max)
                    dve.drain()
            nc.vector.tensor_tensor(flags_i[:], flags[0:1, 0:1], flags[0:1, 1:2], ALU.max)
            dve.wait_ge(rows_stored, 64)
            dve.wait_ge(v_stored, 16)
            for m in range(M2):
                dve.wait_ge(parts_stored[m], 16 * N_RUNS)

        @block.tensor
        def _(pe):
            pe.wait_ge(const_ready_pe, 1)
            pe.sem_inc(const_ready_pe, -1)
            pe.wait_ge(w_in, 48)

            def use_bank(name):
                pe.wait_ge(bank_free[USE[name]], 1)
                pe.sem_inc(bank_free[USE[name]], -1)
                return banks[USE[name]]

            with pe.Fori(0, B // 2) as bb:
                for i in range(2):
                    pe.wait_ge(xn_ready, 1)
                    pe.sem_inc(xn_ready, -1)
                    for kc in range(KC):
                        dst = use_bank(f"xT{kc}")
                        for t in range(QT):
                            last = nc.tensor.transpose(dst[:, t * P:(t + 1) * P], xn[:, t, kc * P:(kc + 1) * P], ident[:])
                        last.then_inc(xT_ready, 1)
                    dst = use_bank("nf")
                    for t in range(QT):
                        last = nc.tensor.transpose(dst[0:1, t * P:(t + 1) * P], has_key[:, t:t + 1], ident[:])
                    last.then_inc(nf_t_ready, 1)
                    pe.wait_ge(xT_sb_ready, 1)
                    pe.sem_inc(xT_sb_ready, -1)
                    pe.wait_ge(ctx_in[i], 16)
                    pe.sem_inc(ctx_in[i], -16)
                    for kind, m, half in qk_tiles:
                        w, src = (wq, xnT) if kind == "q" else (wk, ctx_sb[i])
                        dst = use_bank(f"q{m}" if kind == "q" else f"k{m}{half}")
                        for kc in range(KC):
                            last = nc.tensor.matmul(dst, w[:, kc, m * P:(m + 1) * P],
                                                    src[:, kc, half * 512:(half + 1) * 512],
                                                    start=(kc == 0), stop=(kc == KC - 1))
                        last.then_inc(qk_ready, 1)
                    for n in range(4):
                        dst = use_bank(f"v{n}")
                        for e in range(2):
                            kt = 2 * n + e
                            for kc in range(KC):
                                last = nc.tensor.matmul(dst[:, e * D:(e + 1) * D], ctx_sb[i][:, kc, kt * P:(kt + 1) * P],
                                                        wv[:, kc, :], start=(kc == 0), stop=(kc == KC - 1))
                        last.then_inc(v_ready, 1)
                    for n in range(2):
                        dst = use_bank(f"c{n}")
                        for t in range(QT):
                            last = nc.tensor.matmul(dst[0:1, :], ones_bf[:], mask_bf[:, t, n * 512:(n + 1) * 512],
                                                    start=(t == 0), stop=(t == QT - 1))
                        last.then_inc(c_ready, 1)
                    dst = use_bank("bound")
                    pe.wait_ge(ab_ready, 1)
                    pe.sem_inc(ab_ready, -1)
                    for m in range(M2):
                        last = nc.tensor.matmul(dst[0:1, m * H8:(m + 1) * H8], ab[:, m:m + 1], block_of[:],
                                                start=True, stop=True)
                        if m == 0:
                            last.then_inc(ctx_free, 1)
                    last.then_inc(bound_ready, 1)
                    pe.drain().then_inc(maskbf_free, 1)


def maximum_phase(nc, top, io, ks_dram, qs_dram, mask_dram, pair_bank, bank, ident, flags_i):
    with ExitStack() as ctx:
        sb = lambda name, shape, dt=F32: ctx.enter_context(nc.sbuf_tensor(name, shape, dt))
        sem = lambda name: top.enter_context(nc.semaphore(name))
        ks = sb("max_ks", [P, H8, SK], BF16)
        qs = sb("max_qs", [P, H8, S], BF16)
        mask_u8 = sb("max_mask_in", [P, QT, SK], U8)
        mask_bf = sb("max_mask_bf", [P, QT, SK], BF16)
        mask_fix = sb("max_mask_fix", [P, QT, SK], BF16)
        masked = sb("max_masked", [P, QT])
        has_key = sb("max_has_key", [P, QT])
        lower = sb("max_lower", [P, P], BF16)
        neg_max = sb("neg_max", [P, QT, H8])
        rest = sb("max_rest", [H8, S])
        parts = sb("max_parts", [H8, 3, S], BF16)

        mask_in, mask_done, mask_stored = sem("mmask_in"), sem("mmask_done"), sem("mmask_stored")
        mask_ready, mask_used = sem("mmask_ready"), sem("mmask_used")
        qk_in, qk_used = sem("mqk_in"), sem("mqk_used")
        lower_ready = sem("lower_ready")
        s_ready, s_read = [sem(f"ms_ready{i}") for i in range(2)], [sem(f"ms_read{i}") for i in range(2)]
        neg_ready, negT_ready = sem("neg_ready"), sem("negT_ready")
        parts_ready, parts_stored = sem("mparts_ready"), sem("mparts_stored")
        block = ctx.enter_context(nc.Block())

        @block.sync
        def _(sp):
            general = sp.value_load(flags_i[0:1, 0:1], min_val=0, max_val=1)
            with sp.If(general == 1):
                with sp.Fori(0, B) as b:
                    sp.dma_start(mask_u8[:], io["mask"][b].rearrange("(t p) k -> p t k", p=P)).then_inc(mask_in, 16)
                    sp.wait_ge(mask_done, 1)
                    sp.sem_inc(mask_done, -1)
                    sp.dma_start(mask_dram[b].rearrange("(t p) k -> p t k", p=P), mask_fix[:]).then_inc(mask_stored, 16)
                    for m in range(M2):
                        sp.dma_start(ks[0:ROW_MAX], ks_dram[b, m, 0:ROW_MAX]).then_inc(qk_in, 16)
                        sp.dma_start(qs[0:ROW_MAX], qs_dram[b, m, 0:ROW_MAX]).then_inc(qk_in, 16)
                        sp.wait_ge(parts_ready, 1)
                        sp.sem_inc(parts_ready, -1)
                        sp.dma_start(qs_dram[b, m, ROW_MAX:ROWS].rearrange("r h k -> h r k"), parts[:]
                                     ).then_inc(parts_stored, 16)
                        sp.wait_ge(parts_stored, 16)
                        sp.sem_inc(parts_stored, -16)
                    sp.wait_ge(mask_stored, 16)
                    sp.sem_inc(mask_stored, -16)

        @block.vector
        def _(dve):
            general = dve.value_load(flags_i[0:1, 0:1], min_val=0, max_val=1)
            with dve.If(general == 1):
                nc.vector.tensor_scalar(lower[:], ident[:], -BIG, None, ALU.mult).then_inc(lower_ready, 1)
                dve.sem_inc(s_read[0], 1)
                dve.sem_inc(s_read[1], 1)
                with dve.Fori(0, B) as b:
                    dve.wait_ge(mask_in, 16)
                    dve.sem_inc(mask_in, -16)
                    nc.vector.tensor_copy(mask_bf[:], mask_u8[:])
                    dve.drain()
                    nc.vector.tensor_reduce(masked[:], mask_bf[:], op=ALU.add, axis=AX.X)
                    dve.drain()
                    nc.vector.tensor_scalar(has_key[:], masked[:], float(SK), None, ALU.is_lt)
                    dve.drain()
                    for t in range(QT):
                        nc.vector.tensor_scalar(mask_fix[:, t], mask_bf[:, t], has_key[:, t:t + 1], None, ALU.mult)
                    dve.drain().then_inc(mask_done, 1)
                    dve.sem_inc(mask_ready, 1)
                    for m in range(M2):
                        for h in range(H8):
                            for t in range(QT):
                                i = t % 2
                                dve.wait_ge(s_ready[i], 1)
                                dve.sem_inc(s_ready[i], -1)
                                nc.vector.tensor_reduce(neg_max[:, t, h:h + 1], pair_bank[i][:], op=ALU.max, axis=AX.XY,
                                                        negate=True).then_inc(s_read[i], 1)
                        dve.drain().then_inc(neg_ready, 1)
                        dve.wait_ge(negT_ready, 1)
                        dve.sem_inc(negT_ready, -1)
                        neg_t = bank[0][0:H8, :]
                        nc.vector.tensor_copy(parts[:, 0], neg_t)
                        dve.drain()
                        nc.vector.tensor_tensor(rest[:], neg_t, parts[:, 0], ALU.subtract)
                        dve.drain()
                        nc.vector.tensor_copy(parts[:, 1], rest[:])
                        dve.drain()
                        nc.vector.tensor_tensor(parts[:, 2], rest[:], parts[:, 1], ALU.subtract)
                        dve.drain().then_inc(parts_ready, 1)

        @block.tensor
        def _(pe):
            general = pe.value_load(flags_i[0:1, 0:1], min_val=0, max_val=1)
            with pe.If(general == 1):
                pe.wait_ge(lower_ready, 1)
                pe.sem_inc(lower_ready, -1)
                with pe.Fori(0, B) as b:
                    pe.wait_ge(mask_ready, 1)
                    pe.sem_inc(mask_ready, -1)
                    for m in range(M2):
                        pe.wait_ge(qk_in, 32)
                        pe.sem_inc(qk_in, -32)
                        for h in range(H8):
                            for t in range(QT):
                                i = t % 2
                                pe.wait_ge(s_read[i], 1)
                                pe.sem_inc(s_read[i], -1)
                                for e in range(2):
                                    cols = slice(e * 512, (e + 1) * 512)
                                    nc.tensor.matmul(pair_bank[i][:, e], qs[0:ROW_MAX, h, t * P:(t + 1) * P],
                                                     ks[0:ROW_MAX, h, cols], start=True, stop=False)
                                    last = nc.tensor.matmul(pair_bank[i][:, e], lower[:], mask_fix[:, t, cols],
                                                            start=False, stop=True)
                                last.then_inc(s_ready[i], 1)
                        pe.wait_ge(neg_ready, 1)
                        pe.sem_inc(neg_ready, -1)
                        for t in range(QT):
                            last = nc.tensor.transpose(bank[0][0:H8, t * P:(t + 1) * P], neg_max[:, t], ident[:])
                        last.then_inc(negT_ready, 1)


def main_phase(nc, top, io, out, ks_dram, qs_dram, v_dram, mask_dram, pair_bank, bank, ident, flags_i):
    o_bank, misc = bank[0:2], bank[2:4]
    with ExitStack() as ctx:
        sb = lambda name, shape, dt=F32: ctx.enter_context(nc.sbuf_tensor(name, shape, dt))
        sem = lambda name: top.enter_context(nc.semaphore(name))
        ks = sb("ks", [P, G, HG, SK], BF16)
        qs = sb("qs", [P, G, HG, S], BF16)
        v_in_sb = [sb(f"v_in_sb{i}", [P, KT, HG * HD]) for i in range(2)]
        va = sb("va", [P, KT, G, HG, 32])
        probs = [sb(f"probs{i}", [P, HG, S]) for i in range(2)]
        mask_fix = sb("mask_fix", [P, QT, SK], BF16)
        lower = sb("lower", [P, P], BF16)
        o_sb = sb("o_sb", [P, S])
        den = sb("den", [P, S])
        o_t = sb("o_t", [P, G, S])
        wo = sb("wo", [P, G, D])
        wqkv = sb("wqkv", [P, KC, 3 * D])
        wout = sb("wout", [P, KC, D])
        w1, w2 = (sb(n, [P, KC, FT * P]) for n in ("w1", "w2"))
        w3 = sb("w3", [P, FT, D])
        wr_b, g1_b, g2_b = (sb(n, [P, D]) for n in ("wr_b", "g1_b", "g2_b"))
        iota_r = sb("iota_r", [P, CAP])
        before = sb("before", [P, QT, S], BF16)
        block_of = sb("block_of2", [P, H8])
        causal = sb("causal", [P, CAP])
        neg_half = sb("neg_half2", [P, QT])
        x_sb = sb("x_sb", [P, QT, D])
        x1 = sb("x1", [P, QT, D])
        y = sb("y", [P, QT, D])
        out_sb = sb("out_sb", [P, QT, D])
        stats = sb("stats2", [P, QT, 6])
        mv = sb("mv2", [P, QT, 2])
        veps = sb("veps2", [P, QT])
        rstd = sb("rstd2", [P, QT])
        prod = sb("prod", [P, D])
        score = sb("score", [P, QT])
        ties = sb("ties", [P, S])
        ahead = sb("ahead", [P, S])
        rank = sb("rank", [P, QT])
        sel = sb("sel", [P, QT, CAP])
        sel_t = sb("sel_t", [P, S])
        x_sel = sb("x_sel", [P, D])
        square = sb("square", [P, D])
        ms = sb("ms", [P, 4])
        hid = sb("hid", [P, D])
        hid_t = sb("hid_t", [P, KC, CAP])
        q_t = sb("q_t", [P, KC, CAP])
        v_s = sb("v_s", [P, D])
        k_block = sb("k_block", [P, M2, H8, CAP])
        p_t = k_block[:].rearrange("p m h k -> p (m h) k")
        sc = sb("sc", [P, H, CAP])
        s_max = sb("s_max", [P, H])
        s_den = sb("s_den", [P, H])
        o_s = sb("o_s", [P, D])
        os_t = sb("os_t", [P, KC, CAP])
        att = sb("att", [P, D])
        r1 = sb("r1", [P, D])
        sig = sb("sig", [P, 3 * P])
        gate = sb("gate", [P, FT, P])
        delta = sb("delta", [P, D])

        w_zero, w_in, consts, lower_set = sem("w_zero"), sem("w2_in"), sem("consts"), sem("lower_set")
        rows_set, group_in = sem("rows_set"), [sem(f"group_in{g}") for g in range(G)]
        group_free, v_in, v_in_free = sem("group_free"), [sem(f"v_in{i}") for i in range(2)], sem("v_in_free")
        va_ready, va_free = sem("va_ready"), sem("va_free")
        maskfix_in, maskfix_free = sem("maskfix_in"), sem("maskfix_free")
        s_ready, s_read = [sem(f"s_ready{i}") for i in range(2)], [sem(f"s_read{i}") for i in range(2)]
        o_ready, o_free, ot_ready, ot_free = sem("o_ready"), sem("o_free"), sem("ot_ready"), sem("ot_free")
        misc_free = [sem(f"misc_free{i}") for i in range(2)]
        xres_in, xres_free = sem("xres_in"), sem("xres_free")
        wo_ready, var2_ready, rstd2_ready, y_ready = sem("wo_ready"), sem("var2_ready"), sem("rstd2_ready"), sem("y_ready")
        score_ready, spread_ready, sel_ready = sem("score_ready"), sem("spread_ready"), sem("sel_ready")
        base_ready = sem("base_ready")
        gather_ready, selT_ready, selT_sb = sem("gather_ready"), sem("selT_ready"), sem("selT_sb")
        ms_ready, rms_ready, hid_ready, hidT_ready, hidT_sb = (
            sem("ms_ready"), sem("rms_ready"), sem("hid_ready"), sem("hidT_ready"), sem("hidT_sb"))
        qv_ready, k_ready, qv_sb, kb_ready = sem("qv_ready"), sem("k_ready"), sem("qv_sb"), sem("kb_ready")
        sc_ready, scm_ready, p_ready, den_ready = sem("sc_ready"), sem("scm_ready"), sem("p_ready"), sem("p_sum")
        pT_ready, pT_sb, pv_ready, os_ready = sem("pT_ready"), sem("pT_sb"), sem("pv_ready"), sem("os_ready")
        osT_ready, osT_sb, att_ready = sem("osT_ready"), sem("osT_sb"), sem("att_ready")
        u_ready, w_ready, sig_ready, sig_used, gate_ready = (
            sem("u_ready"), sem("w_ready"), sem("sig_ready"), sem("sig_used"), sem("gate_ready"))
        ff_ready, delta_ready, scat_ready = sem("ff_ready"), sem("delta_ready"), sem("scat_ready")
        out_ready, out_stored = sem("out_ready"), sem("out_stored")

        block = ctx.enter_context(nc.Block())
        N_W = 4 + 1 + 1 + 1 + 1 + 2 + 3

        @block.sync
        def _(sp):
            general = sp.value_load(flags_i[0:1, 0:1], min_val=0, max_val=1)
            sp.wait_ge(w_zero, 1)
            sp.sem_inc(w_zero, -1)
            wo_rows = io["woT"].rearrange("(g j d) n -> j d g n", g=G, j=HG)
            for j in range(HG):
                sp.dma_start(wo[32 * j:32 * j + HD], wo_rows[j]).then_inc(w_in, 16)
            sp.dma_start(wqkv[:], io["wqkvT"].rearrange("(c p) n -> p c n", p=P)).then_inc(w_in, 16)
            sp.dma_start(wout[:], io["woutT"].rearrange("(c p) n -> p c n", p=P)).then_inc(w_in, 16)
            sp.dma_start(w1[:, :, 0:DFF], io["w1T"].rearrange("(c p) n -> p c n", p=P)).then_inc(w_in, 16)
            sp.dma_start(w2[:, :, 0:DFF], io["w2T"].rearrange("(c p) n -> p c n", p=P)).then_inc(w_in, 16)
            full = DFF // P
            sp.dma_start(w3[:, 0:full], io["w3T"][0:full * P].rearrange("(c p) n -> p c n", p=P)).then_inc(w_in, 16)
            sp.dma_start(w3[0:DFF - full * P, full], io["w3T"][full * P:DFF]).then_inc(w_in, 16)
            for dst, name in ((wr_b, "w_router"), (g1_b, "g1"), (g2_b, "g2")):
                sp.dma_start(dst[:], io[name].partition_broadcast(P)).then_inc(w_in, 16)
            sp.wait_ge(rows_set, 1)
            sp.sem_inc(rows_set, -1)

            def load(b):
                for g in range(G):
                    m, h0 = g // (G // M2), (g % (G // M2)) * HG
                    sp.wait_ge(group_free, 1)
                    sp.sem_inc(group_free, -1)
                    sp.dma_start(ks[0:ROW_MAX, g], ks_dram[b, m, 0:ROW_MAX, h0:h0 + HG, :]).then_inc(group_in[g], 16)
                    sp.dma_start(qs[0:ROWS, g], qs_dram[b, m, :, h0:h0 + HG, :]).then_inc(group_in[g], 16)
                    if g == G - 1:
                        with sp.If(general == 1):
                            sp.wait_ge(maskfix_free, 1)
                            sp.sem_inc(maskfix_free, -1)
                            sp.dma_start(mask_fix[:], mask_dram[b].rearrange("(t p) k -> p t k", p=P)).then_inc(maskfix_in, 16)
                    sp.wait_ge(v_in_free, 1)
                    sp.sem_inc(v_in_free, -1)
                    src = v_dram[b].rearrange("(t p) n -> p t n", p=P)[:, :, g * HG * HD:(g + 1) * HG * HD]
                    sp.dma_start(v_in_sb[g % 2][:], src).then_inc(v_in[g % 2], 16)
                sp.wait_ge(xres_free, 1)
                sp.sem_inc(xres_free, -1)
                sp.dma_start(x_sb[:], io["x"][b].rearrange("(t p) d -> p t d", p=P)).then_inc(xres_in, 16)

            def store(b):
                sp.wait_ge(out_ready, 1)
                sp.sem_inc(out_ready, -1)
                sp.dma_start(out[b].rearrange("(t p) d -> p t d", p=P), out_sb[:]).then_inc(out_stored, 16)

            load(0)
            load(1)
            with sp.Fori(2, B) as b:
                load(b)
                store(b - 2)
            store(B - 2)
            store(B - 1)
            sp.wait_ge(out_stored, 16)

        @block.gpsimd
        def _(pool):
            nc.gpsimd.memset(wo[:], 0.0)
            for t in (w1, w2, w3):
                nc.gpsimd.memset(t[:], 0.0)
            pool.drain().then_inc(w_zero, 1)
            nc.gpsimd.memset(ks[ROW_MASK:ROWS], 1.0)
            pool.drain().then_inc(rows_set, 1)
            nc.gpsimd.memset(va[:].rearrange("p t g h c -> p (t g h) c")[:, :, HD:32], 1.0)
            nc.gpsimd.memset(neg_half[:], -0.5)
            nc.gpsimd.memset(before[:], 1.0)
            nc.gpsimd.memset(block_of[:], 1.0)
            nc.gpsimd.memset(causal[:], 0.0)
            nc.gpsimd.iota(iota_r[:], pattern=[[1, CAP]], base=0, channel_multiplier=0,
                           allow_small_or_imprecise_dtypes=True)
            pool.drain()
            for t in range(QT):
                nc.gpsimd.affine_select(out=before[:, t], in_=before[:, t], compare_op=ALU.is_gt, fill=0.0,
                                        base=t * P, pattern=[[-1, S]], channel_multiplier=1)
            nc.gpsimd.affine_select(out=block_of[:], in_=block_of[:], compare_op=ALU.is_ge, fill=0.0,
                                    base=0, pattern=[[-HD, H8]], channel_multiplier=1)
            nc.gpsimd.affine_select(out=causal[:], in_=causal[:], compare_op=ALU.is_ge, fill=-1e30,
                                    base=0, pattern=[[-1, CAP]], channel_multiplier=1)
            pool.drain()
            nc.gpsimd.affine_select(out=block_of[:], in_=block_of[:], compare_op=ALU.is_gt, fill=0.0,
                                    base=HD, pattern=[[HD, H8]], channel_multiplier=-1)
            pool.drain().then_inc(consts, 1)

            def spread_v(g):
                pool.wait_ge(v_in[g % 2], 16)
                pool.sem_inc(v_in[g % 2], -16)
                pool.wait_ge(va_free, 1)
                pool.sem_inc(va_free, -1)
                nc.gpsimd.tensor_copy(va[:, :, g, :, 0:HD], v_in_sb[g % 2][:].rearrange("p t (h d) -> p t h d", h=HG)
                                      ).then_inc(va_ready, 1)
                pool.drain().then_inc(v_in_free, 1)

            def rms(col):
                pool.wait_ge(ms_ready, 1)
                pool.sem_inc(ms_ready, -1)
                nc.gpsimd.tensor_scalar(ms[:, col + 1:col + 2], ms[:, col:col + 1], 1.0 / D, RMS_EPS, ALU.mult, ALU.add)
                pool.drain()
                nc.gpsimd.tensor_tensor(ms[:, col:col + 1], ms[:, col + 1:col + 2], neg_half[:, 0:1], ALU.pow
                                        ).then_inc(rms_ready, 1)

            def norm_and_base():
                pool.wait_ge(var2_ready, 1)
                pool.sem_inc(var2_ready, -1)
                nc.gpsimd.tensor_scalar(veps[:], mv[:, :, 1], LN_EPS, None, ALU.add)
                pool.drain()
                nc.gpsimd.tensor_tensor(rstd[:], veps[:], neg_half[:], ALU.pow).then_inc(rstd2_ready, 1)
                pool.wait_ge(y_ready, 1)
                pool.sem_inc(y_ready, -1)
                nc.gpsimd.tensor_tensor(x1[:], x1[:], y[:], ALU.add).then_inc(base_ready, 1)

            def batch(last):
                norm_and_base()
                spread_v(1)
                rms(0)
                spread_v(2)
                spread_v(3)
                rms(2)
                if not last:
                    spread_v(0)

            for g in range(G):
                spread_v(g)
            spread_v(0)
            with pool.Fori(1, B - 1) as b:
                batch(last=False)
            batch(last=True)
            norm_and_base()
            rms(0)
            rms(2)

        def act_step(act, s):
            for pr in range(2):
                act.wait_ge(s_ready[pr], 1)
                act.sem_inc(s_ready[pr], -1)
                nc.scalar.activation(probs[s % 2][:, 2 * pr:2 * pr + 2, :], pair_bank[pr][:], ACT.Exp,
                                     scale=HD ** -0.5).then_inc(s_read[pr], 1)

        def act_ffn(act, stage):
            if stage == "selT":
                act.wait_ge(selT_ready, 1)
                act.sem_inc(selT_ready, -1)
                nc.scalar.activation(sel_t[:], misc[0][:], ACT.Copy).then_inc(misc_free[0], 1)
                act.drain().then_inc(selT_sb, 1)
            elif stage == "hidT":
                act.wait_ge(hidT_ready, 1)
                act.sem_inc(hidT_ready, -1)
                nc.scalar.activation(hid_t[:], misc[1][:, 0:KC * CAP].rearrange("p (c k) -> p c k", c=KC), ACT.Copy
                                     ).then_inc(misc_free[1], 1)
                act.drain().then_inc(hidT_sb, 1)
            elif stage == "qv":
                act.wait_ge(qv_ready, 1)
                act.sem_inc(qv_ready, -1)
                nc.scalar.activation(q_t[:], misc[0][:, 0:KC * CAP].rearrange("p (c k) -> p c k", c=KC), ACT.Copy)
                nc.scalar.activation(v_s[:], misc[0][:, D:2 * D], ACT.Copy).then_inc(misc_free[0], 1)
                act.drain().then_inc(qv_sb, 1)
            elif stage == "exp":
                act.wait_ge(scm_ready, 1)
                act.sem_inc(scm_ready, -1)
                nc.scalar.activation(sc[:], sc[:], ACT.Exp, scale=HD ** -0.5).then_inc(p_ready, 1)
                act.drain().then_inc(den_ready, 1)
            elif stage.startswith("pT"):
                n = int(stage[2])
                act.wait_ge(pT_ready, 1)
                act.sem_inc(pT_ready, -1)
                nc.scalar.activation(p_t[:, 4 * n:4 * n + 4, :], misc[n % 2][:].rearrange("p (h k) -> p h k", h=4), ACT.Copy
                                     ).then_inc(misc_free[n % 2], 1)
                if n == 3:
                    act.drain().then_inc(pT_sb, 1)
            elif stage == "osT":
                act.wait_ge(osT_ready, 1)
                act.sem_inc(osT_ready, -1)
                nc.scalar.activation(os_t[:], misc[1][:, 0:KC * CAP].rearrange("p (c k) -> p c k", c=KC), ACT.Copy
                                     ).then_inc(misc_free[1], 1)
                act.drain().then_inc(osT_sb, 1)
            elif stage == "sig":
                act.wait_ge(u_ready, 1)
                act.sem_inc(u_ready, -1)
                act.wait_ge(sig_used, 1)
                act.sem_inc(sig_used, -1)
                nc.scalar.activation(sig[:], misc[0][:, 0:3 * P], ACT.Exp, scale=-1.0).then_inc(sig_ready, 1)

        @block.scalar
        def _(act):
            for s in range(G * KT):
                act_step(act, s)
            with act.Fori(1, B) as b:
                for s in range(G * KT):
                    act_step(act, s)
                    for stage, at in ACT_SLOT:
                        if at == s:
                            act_ffn(act, stage)
            for stage, at in ACT_SLOT:
                act_ffn(act, stage)

        def group_end(dve, g):
            dve.drain()
            dve.wait_ge(o_ready, 1)
            dve.sem_inc(o_ready, -1)
            dve.sem_inc(group_free, 1)
            dve.sem_inc(va_free, 1)
            nc.vector.tensor_copy(o_sb[:], o_bank[g % 2][:]).then_inc(o_free, 1)
            dve.drain()
            nc.vector.stream_shuffle(den[:], o_sb[:], mask=[HD] * 32)
            dve.drain()
            nc.vector.reciprocal(den[:], den[:])
            dve.drain()
            if g == 0:
                dve.wait_ge(ot_free, 1)
                dve.sem_inc(ot_free, -1)
            nc.vector.tensor_tensor(o_t[:, g], o_sb[:], den[:], ALU.mult).then_inc(ot_ready, 1)

        def square_sum(dve, src, col):
            nc.vector.scalar_tensor_tensor(out=square[:], in0=src, scalar=1.0, in1=src, op0=ALU.mult, op1=ALU.mult,
                                           accum_out=ms[:, col:col + 1])
            dve.drain().then_inc(ms_ready, 1)

        def dve_ffn(dve, stage):
            dve.drain()
            if stage == "x1":
                dve.wait_ge(xres_in, 16)
                dve.sem_inc(xres_in, -16)
                for pr in range(2):
                    dve.wait_ge(wo_ready, 1)
                    dve.sem_inc(wo_ready, -1)
                    nc.vector.tensor_tensor(x1[:, 2 * pr:2 * pr + 2], x_sb[:, 2 * pr:2 * pr + 2],
                                            misc[pr][:].rearrange("p (t d) -> p t d", t=2), ALU.add
                                            ).then_inc(misc_free[pr], 1)
                dve.drain().then_inc(xres_free, 1)
                dve.sem_inc(ot_free, 1)
                for t in range(QT):
                    nc.vector.bn_stats(stats[:, t], x1[:, t])
                dve.drain()
                for t in range(QT):
                    nc.vector.bn_aggr(mv[:, t], stats[:, t])
                dve.drain().then_inc(var2_ready, 1)
            elif stage == "y":
                dve.wait_ge(rstd2_ready, 1)
                dve.sem_inc(rstd2_ready, -1)
                for t in range(QT):
                    nc.vector.tensor_scalar(y[:, t], x1[:, t], mv[:, t, 0:1], rstd[:, t:t + 1], ALU.subtract, ALU.mult)
                dve.drain().then_inc(y_ready, 1)
                for t in range(QT):
                    nc.vector.scalar_tensor_tensor(out=prod[:], in0=y[:, t], scalar=1.0, in1=wr_b[:], op0=ALU.mult,
                                                   op1=ALU.mult, accum_out=score[:, t:t + 1])
                    dve.drain()
                dve.drain().then_inc(score_ready, 1)
            elif stage == "rank":
                dve.wait_ge(spread_ready, 1)
                dve.sem_inc(spread_ready, -1)
                for t in range(QT):
                    nc.vector.scalar_tensor_tensor(out=ties[:], in0=misc[0][:], scalar=score[:, t:t + 1],
                                                   in1=before[:, t], op0=ALU.is_equal, op1=ALU.mult)
                    dve.drain()
                    last = nc.vector.scalar_tensor_tensor(out=ahead[:], in0=misc[0][:], scalar=score[:, t:t + 1],
                                                          in1=ties[:], op0=ALU.is_gt, op1=ALU.add,
                                                          accum_out=rank[:, t:t + 1])
                    dve.drain()
                    nc.vector.tensor_scalar(sel[:, t], iota_r[:], rank[:, t:t + 1], None, ALU.is_equal)
                dve.drain().then_inc(misc_free[0], 1)
                dve.drain().then_inc(sel_ready, 1)
            elif stage == "hid":
                dve.wait_ge(gather_ready, 1)
                dve.sem_inc(gather_ready, -1)
                nc.vector.tensor_copy(x_sel[:], misc[1][:, 0:D]).then_inc(misc_free[1], 1)
                dve.drain()
                square_sum(dve, x_sel[:], 0)
                dve.wait_ge(rms_ready, 1)
                dve.sem_inc(rms_ready, -1)
                nc.vector.scalar_tensor_tensor(out=hid[:], in0=x_sel[:], scalar=ms[:, 0:1], in1=g1_b[:],
                                               op0=ALU.mult, op1=ALU.mult).then_inc(hid_ready, 1)
            elif stage == "k_block":
                dve.wait_ge(k_ready, 1)
                dve.sem_inc(k_ready, -1)
                for m in range(M2):
                    src = misc[1][:, m * CAP:(m + 1) * CAP]
                    last = nc.vector.tensor_tensor(k_block[:, m], src.unsqueeze(1).broadcast_to([P, H8, CAP]),
                                                   block_of[:].unsqueeze(2).broadcast_to([P, H8, CAP]), ALU.mult)
                last.then_inc(misc_free[1], 1)
                dve.drain().then_inc(kb_ready, 1)
            elif stage == "softmax":
                for n in range(4):
                    dve.wait_ge(sc_ready, 1)
                    dve.sem_inc(sc_ready, -1)
                    nc.vector.tensor_tensor(sc[:, 4 * n:4 * n + 4], misc[n % 2][:].rearrange("p (h k) -> p h k", h=4),
                                            causal[:].unsqueeze(1).broadcast_to([P, 4, CAP]), ALU.add
                                            ).then_inc(misc_free[n % 2], 1)
                dve.drain()
                nc.vector.tensor_reduce(s_max[:], sc[:], op=ALU.max, axis=AX.X)
                dve.drain()
                nc.vector.tensor_tensor(sc[:], sc[:], s_max[:].unsqueeze(2).broadcast_to([P, H, CAP]), ALU.subtract
                                        ).then_inc(scm_ready, 1)
            elif stage == "sum":
                dve.wait_ge(den_ready, 1)
                dve.sem_inc(den_ready, -1)
                nc.vector.tensor_reduce(s_max[:], sc[:], op=ALU.add, axis=AX.X)
                dve.drain()
                nc.vector.reciprocal(s_den[:], s_max[:])
                dve.drain()
            elif stage == "os":
                dve.wait_ge(pv_ready, 1)
                dve.sem_inc(pv_ready, -1)
                nc.vector.tensor_tensor(o_s[:].rearrange("p (h d) -> p h d", h=H),
                                        misc[0][:, 0:D].rearrange("p (h d) -> p h d", h=H),
                                        s_den[:].unsqueeze(2).broadcast_to([P, H, HD]), ALU.mult
                                        ).then_inc(misc_free[0], 1)
                dve.drain().then_inc(os_ready, 1)
            elif stage == "hid2":
                dve.wait_ge(att_ready, 1)
                dve.sem_inc(att_ready, -1)
                nc.vector.tensor_copy(att[:], misc[0][:, 0:D]).then_inc(misc_free[0], 1)
                dve.drain()
                nc.vector.tensor_tensor(r1[:], x_sel[:], att[:], ALU.add)
                dve.drain()
                square_sum(dve, r1[:], 2)
                dve.wait_ge(rms_ready, 1)
                dve.sem_inc(rms_ready, -1)
                nc.vector.scalar_tensor_tensor(out=hid[:], in0=r1[:], scalar=ms[:, 2:3], in1=g2_b[:],
                                               op0=ALU.mult, op1=ALU.mult).then_inc(hid_ready, 1)
            elif stage == "gate":
                dve.wait_ge(sig_ready, 1)
                dve.sem_inc(sig_ready, -1)
                nc.vector.tensor_scalar(sig[:], sig[:], 1.0, None, ALU.add)
                dve.drain()
                nc.vector.reciprocal(sig[:], sig[:])
                dve.drain()
                nc.vector.tensor_tensor(sig[:], sig[:], misc[0][:, 0:3 * P], ALU.mult).then_inc(misc_free[0], 1)
                dve.wait_ge(w_ready, 1)
                dve.sem_inc(w_ready, -1)
                dve.drain()
                yield_half = gate_half[0]
                nc.vector.tensor_tensor(gate[:, 3 * yield_half:3 * yield_half + 3],
                                        sig[:].rearrange("p (f k) -> p f k", f=3),
                                        misc[1][:, 0:3 * P].rearrange("p (f k) -> p f k", f=3), ALU.mult
                                        ).then_inc(misc_free[1], 1)
                dve.drain().then_inc(sig_used, 1)
                gate_half[0] = 1 - yield_half
                if yield_half == 1:
                    dve.drain().then_inc(gate_ready, 1)
            elif stage == "delta":
                dve.wait_ge(ff_ready, 1)
                dve.sem_inc(ff_ready, -1)
                nc.vector.tensor_tensor(delta[:], att[:], misc[0][:, 0:D], ALU.add).then_inc(misc_free[0], 1)
                dve.drain().then_inc(delta_ready, 1)
            elif stage == "out":
                dve.wait_ge(base_ready, 1)
                dve.sem_inc(base_ready, -1)
                dve.wait_ge(out_stored, 16)
                dve.sem_inc(out_stored, -16)
                for pr in range(2):
                    dve.wait_ge(scat_ready, 1)
                    dve.sem_inc(scat_ready, -1)
                    nc.vector.tensor_tensor(out_sb[:, 2 * pr:2 * pr + 2], x1[:, 2 * pr:2 * pr + 2],
                                            misc[pr][:].rearrange("p (t d) -> p t d", t=2), ALU.add
                                            ).then_inc(misc_free[pr], 1)
                dve.drain().then_inc(out_ready, 1)

        gate_half = [0]

        @block.vector
        def _(dve):
            nc.vector.tensor_scalar(lower[:], ident[:], -BIG, None, ALU.mult)
            dve.sem_inc(maskfix_free, 1)
            dve.sem_inc(group_free, G)
            dve.sem_inc(va_free, G)
            dve.sem_inc(v_in_free, 2)
            dve.sem_inc(o_free, 2)
            dve.sem_inc(ot_free, 1)
            dve.sem_inc(misc_free[0], 1)
            dve.sem_inc(misc_free[1], 1)
            dve.sem_inc(xres_free, 1)
            dve.sem_inc(sig_used, 1)
            dve.sem_inc(out_stored, 16)
            dve.wait_ge(consts, 1)
            dve.sem_inc(consts, -1)
            dve.drain().then_inc(lower_set, 1)
            for g in range(G):
                group_end(dve, g)
            with dve.Fori(1, B) as b:
                for stage in DVE_ORDER:
                    if isinstance(stage, int):
                        group_end(dve, stage)
                    else:
                        dve_ffn(dve, stage)
            for stage in DVE_ORDER:
                if not isinstance(stage, int):
                    dve_ffn(dve, stage)

        def scores(pe, s, general):
            g, t = s // KT, s % KT
            if t == 0:
                pe.wait_ge(group_in[g], 32)
                pe.sem_inc(group_in[g], -32)
            for pr in range(2):
                if s > 0:
                    pe.wait_ge(s_read[pr], 1)
                    pe.sem_inc(s_read[pr], -1)
                for e in range(2):
                    j = 2 * pr + e
                    last = nc.tensor.matmul(pair_bank[pr][:, e], ks[0:ROWS, g, j, t * P:(t + 1) * P],
                                            qs[0:ROWS, g, j, :], start=True, stop=not general)
                    if general:
                        for n in range(QT):
                            last = nc.tensor.matmul(pair_bank[pr][:, e, n * P:(n + 1) * P],
                                                    mask_fix[:, n, t * P:(t + 1) * P], lower[:],
                                                    start=False, stop=(n == QT - 1))
                last.then_inc(s_ready[pr], 1)

        def values(pe, s):
            g, t = s // KT, s % KT
            if t == 0:
                pe.wait_ge(va_ready, 1)
                pe.sem_inc(va_ready, -1)
                pe.wait_ge(o_free, 1)
                pe.sem_inc(o_free, -1)
            for j in range(HG):
                last = nc.tensor.matmul(o_bank[g % 2][32 * j:32 * j + 32], va[:, t, g, j], probs[s % 2][:, j],
                                        start=(t == 0), stop=(t == KT - 1))
            if t == KT - 1:
                last.then_inc(o_ready, 1)

        def pe_attention(pe, with_ffn, general):
            if general:
                pe.wait_ge(maskfix_in, 16)
                pe.sem_inc(maskfix_in, -16)
            for s in range(G * KT):
                scores(pe, s, general)
                if s > 0:
                    values(pe, s - 1)
                if with_ffn:
                    for stage, at in PE_SLOT:
                        if at == s:
                            pe_ffn(pe, stage)
            pe.wait_ge(s_read[0], 1)
            pe.sem_inc(s_read[0], -1)
            pe.wait_ge(s_read[1], 1)
            pe.sem_inc(s_read[1], -1)
            if general:
                pe.sem_inc(maskfix_free, 1)
            values(pe, G * KT - 1)

        def transposes(dst, srcs):
            for n, src in enumerate(srcs):
                last = nc.tensor.transpose(dst[:, n * P:(n + 1) * P], src, ident[:])
            return last

        def product(dst, pairs):
            for n, (a, c) in enumerate(pairs):
                last = nc.tensor.matmul(dst, a, c, start=(n == 0), stop=(n == len(pairs) - 1))
            return last

        def pe_ffn(pe, stage):
            if stage == "wo":
                pe.wait_ge(ot_ready, G)
                pe.sem_inc(ot_ready, -G)
                for pr in range(2):
                    pe.wait_ge(misc_free[pr], 1)
                    pe.sem_inc(misc_free[pr], -1)
                    for e in range(2):
                        t = 2 * pr + e
                        last = product(misc[pr][:, e * D:(e + 1) * D],
                                       [(o_t[:, g, t * P:(t + 1) * P], wo[:, g]) for g in range(G)])
                    last.then_inc(wo_ready, 1)
            elif stage == "spread":
                pe.wait_ge(score_ready, 1)
                pe.sem_inc(score_ready, -1)
                pe.wait_ge(misc_free[0], 1)
                pe.sem_inc(misc_free[0], -1)
                transposes(misc[0], [score[:, t:t + 1].broadcast_to([P, P]) for t in range(QT)]).then_inc(spread_ready, 1)
            elif stage == "gather":
                pe.wait_ge(sel_ready, 1)
                pe.sem_inc(sel_ready, -1)
                pe.wait_ge(misc_free[1], 1)
                pe.sem_inc(misc_free[1], -1)
                product(misc[1][:, 0:D], [(sel[:, t], y[:, t]) for t in range(QT)]).then_inc(gather_ready, 1)
                pe.wait_ge(misc_free[0], 1)
                pe.sem_inc(misc_free[0], -1)
                transposes(misc[0], [sel[:, t] for t in range(QT)]).then_inc(selT_ready, 1)
            elif stage == "hidT":
                pe.wait_ge(hid_ready, 1)
                pe.sem_inc(hid_ready, -1)
                pe.wait_ge(misc_free[1], 1)
                pe.sem_inc(misc_free[1], -1)
                transposes(misc[1], [hid[:, c * P:(c + 1) * P] for c in range(KC)]).then_inc(hidT_ready, 1)
            elif stage == "qkv":
                pe.wait_ge(hidT_sb, 1)
                pe.sem_inc(hidT_sb, -1)
                pe.wait_ge(misc_free[0], 1)
                pe.sem_inc(misc_free[0], -1)
                for n in range(2):
                    product(misc[0][:, n * CAP:(n + 1) * CAP],
                            [(wqkv[:, c, n * P:(n + 1) * P], hid_t[:, c]) for c in range(KC)])
                product(misc[0][:, D:2 * D], [(hid_t[:, c], wqkv[:, c, 2 * D:3 * D]) for c in range(KC)]
                        ).then_inc(qv_ready, 1)
                pe.wait_ge(misc_free[1], 1)
                pe.sem_inc(misc_free[1], -1)
                for n in range(2):
                    last = product(misc[1][:, n * CAP:(n + 1) * CAP],
                                   [(wqkv[:, c, D + n * P:D + (n + 1) * P], hid_t[:, c]) for c in range(KC)])
                last.then_inc(k_ready, 1)
            elif stage in ("sc0", "sc1"):
                m = int(stage[2])
                if m == 0:
                    pe.wait_ge(kb_ready, 1)
                    pe.sem_inc(kb_ready, -1)
                    pe.wait_ge(qv_sb, 1)
                    pe.sem_inc(qv_sb, -1)
                for e in range(2):
                    pe.wait_ge(misc_free[e], 1)
                    pe.sem_inc(misc_free[e], -1)
                    nc.tensor.matmul(misc[e][:], q_t[:, m], k_block[:, m, 4 * e:4 * e + 4, :], start=True, stop=True
                                     ).then_inc(sc_ready, 1)
            elif stage in ("pT0", "pT1"):
                m = int(stage[2])
                if m == 0:
                    pe.wait_ge(p_ready, 1)
                    pe.sem_inc(p_ready, -1)
                for e in range(2):
                    pe.wait_ge(misc_free[e], 1)
                    pe.sem_inc(misc_free[e], -1)
                    h0 = 8 * m + 4 * e
                    transposes(misc[e], [sc[:, h] for h in range(h0, h0 + 4)]).then_inc(pT_ready, 1)
            elif stage == "pv":
                pe.wait_ge(pT_sb, 1)
                pe.sem_inc(pT_sb, -1)
                pe.wait_ge(misc_free[0], 1)
                pe.sem_inc(misc_free[0], -1)
                for h in range(H):
                    last = nc.tensor.matmul(misc[0][:, h * HD:(h + 1) * HD], p_t[:, h], v_s[:, h * HD:(h + 1) * HD],
                                            start=True, stop=True)
                last.then_inc(pv_ready, 1)
            elif stage == "osT":
                pe.wait_ge(os_ready, 1)
                pe.sem_inc(os_ready, -1)
                pe.wait_ge(misc_free[1], 1)
                pe.sem_inc(misc_free[1], -1)
                transposes(misc[1], [o_s[:, c * P:(c + 1) * P] for c in range(KC)]).then_inc(osT_ready, 1)
            elif stage == "wout":
                pe.wait_ge(osT_sb, 1)
                pe.sem_inc(osT_sb, -1)
                pe.wait_ge(misc_free[0], 1)
                pe.sem_inc(misc_free[0], -1)
                product(misc[0][:, 0:D], [(os_t[:, c], wout[:, c]) for c in range(KC)]).then_inc(att_ready, 1)
            elif stage in ("up0", "up1"):
                r = int(stage[2])
                if r == 0:
                    pe.wait_ge(hidT_sb, 1)
                    pe.sem_inc(hidT_sb, -1)
                for w, dst, free, ready in ((w1, misc[0], misc_free[0], u_ready), (w2, misc[1], misc_free[1], w_ready)):
                    pe.wait_ge(free, 1)
                    pe.sem_inc(free, -1)
                    for f in range(3):
                        last = product(dst[:, f * P:(f + 1) * P],
                                       [(w[:, c, (3 * r + f) * P:(3 * r + f + 1) * P], hid_t[:, c]) for c in range(KC)])
                    last.then_inc(ready, 1)
            elif stage == "down":
                pe.wait_ge(gate_ready, 1)
                pe.sem_inc(gate_ready, -1)
                pe.wait_ge(misc_free[0], 1)
                pe.sem_inc(misc_free[0], -1)
                product(misc[0][:, 0:D], [(gate[:, f], w3[:, f]) for f in range(FT)]).then_inc(ff_ready, 1)
            elif stage == "scatter":
                pe.wait_ge(delta_ready, 1)
                pe.sem_inc(delta_ready, -1)
                pe.wait_ge(selT_sb, 1)
                pe.sem_inc(selT_sb, -1)
                for pr in range(2):
                    pe.wait_ge(misc_free[pr], 1)
                    pe.sem_inc(misc_free[pr], -1)
                    for e in range(2):
                        t = 2 * pr + e
                        last = nc.tensor.matmul(misc[pr][:, e * D:(e + 1) * D], sel_t[:, t * P:(t + 1) * P], delta[:],
                                                start=True, stop=True)
                    last.then_inc(scat_ready, 1)

        @block.tensor
        def _(pe):
            in_general = pe.value_load(flags_i[0:1, 0:1], min_val=0, max_val=1)
            pe.wait_ge(w_in, 16 * N_W)
            pe.wait_ge(lower_set, 1)
            pe.sem_inc(lower_set, -1)

            def batches(general):
                pe_attention(pe, False, general)
                with pe.Fori(1, B) as b:
                    pe_attention(pe, True, general)

            with pe.If(in_general == 1):
                batches(True)
            with pe.Else():
                batches(False)
            for stage, at in PE_SLOT:
                pe_ffn(pe, stage)


PE_SLOT = [("wo", 0), ("spread", 4), ("gather", 8), ("hidT", 10), ("qkv", 12), ("sc0", 14), ("sc1", 15),
           ("pT0", 20), ("pT1", 21), ("pv", 22), ("osT", 23), ("wout", 24), ("hidT", 26), ("up0", 27), ("up1", 29),
           ("down", 30), ("scatter", 31)]
ACT_SLOT = [("selT", 9), ("hidT", 11), ("qv", 13), ("exp", 19), ("pT0", 20), ("pT1", 20), ("pT2", 21), ("pT3", 21),
            ("osT", 23), ("hidT", 26), ("sig", 27), ("sig", 29)]
DVE_ORDER = ["x1", "y", "rank", 0, "hid", "k_block", "softmax", 1, "sum", "os", "hid2", 2,
             "gate", "gate", "delta", "out", 3]


def kernel(**inputs):
    import numpy as np
    import concourse.bacc as bacc
    from concourse import mybir
    from concourse.bass_utils import run_bass_kernel_spmd

    c = np.ascontiguousarray
    a = {k: np.asarray(v) for k, v in inputs.items()}

    def head_minor(w):
        return c(w.reshape(M2, H8, HD, D).transpose(0, 2, 1, 3).reshape(D, D).T)

    arrays = {
        "x": c(a["x"]),
        "ctxT": c(a["ctx_1024"].transpose(0, 2, 1)),
        "mask": c(a["mask_BxSxS2_bk0"]),
        "wqT": head_minor(a["L0_xattn_w_q"]),
        "wkT": head_minor(a["L0_xattn_w_k"]),
        "wvT": c(a["L0_xattn_w_v"].T),
        "woT": c(a["L0_xattn_w_o"].T),
        "w_router": c(a["L0_ffn_w_router"]),
        "wqkvT": c(a["L0_ffn_W_qkv"].T),
        "woutT": c(a["L0_ffn_W_out"].T),
        "g1": c(a["L0_ffn_g1"]),
        "g2": c(a["L0_ffn_g2"]),
        "w1T": c(a["L0_ffn_W1"].T),
        "w2T": c(a["L0_ffn_W2"].T),
        "w3T": c(a["L0_ffn_W3"].T),
    }
    nc = bacc.Bacc("TRN2", target_bir_lowering=False, num_devices=1)
    io = {n: nc.dram_tensor(f"in_{n}", v.shape, mybir.dt.from_np(v.dtype), kind="ExternalInput").ap()
          for n, v in arrays.items()}
    out = nc.dram_tensor("out_dram", (B, S, D), mybir.dt.float32, kind="ExternalOutput").ap()
    program(nc, io, out)
    r = run_bass_kernel_spmd(nc, [{f"in_{n}": v for n, v in arrays.items()}], core_ids=[0])
    return r.results[0]["out_dram"]
```

```python
from contextlib import ExitStack

import concourse.bass as bass
from concourse import mybir

P = 128
B = 8
S = 512
SK = 1024
D = 256
H = 16
HD = D // H
KC = D // P
QT = S // P
KT = SK // P
M2 = 2
H8 = H // M2
G = 4
HG = H // G
NPAIR = 6
K_PART = [0, 0, 0, 1, 1, 2]
Q_PART = [0, 1, 2, 0, 1, 0]
K_RUNS = [(0, 0, 3, 1), (1, 3, 2, 1), (2, 5, 1, 1)]
Q_RUNS = [(0, 0, 2, 3), (0, 5, 1, 1), (1, 1, 2, 3), (2, 2, 1, 1)]
N_RUNS = len(K_RUNS) + len(Q_RUNS)
ROW_MASK = NPAIR * HD
ROW_MAX = ROW_MASK + 1
ROWS = ROW_MAX + 3
CAP = 128
DFF = 682
FT = 6
BIG = 2.0 ** 30
SAFE = 60.0
LN_EPS = 1e-5
RMS_EPS = 1e-6

F32 = mybir.dt.float32
BF16 = mybir.dt.bfloat16
U8 = mybir.dt.uint8
I32 = mybir.dt.int32
ALU = mybir.AluOpType
ACT = mybir.ActivationFunctionType
AX = mybir.AxisListType




def program(nc, io, out):
    dram = lambda name, shape, dt: nc.dram_tensor(name, shape, dt, kind="Internal").ap()
    ks_dram = dram("ks_scratch", (B, M2, ROWS, H8, SK), BF16)
    qs_dram = dram("qs_scratch", (B, M2, ROWS, H8, S), BF16)
    v_dram = dram("v_scratch", (B, SK, D), F32)
    mask_dram = dram("mask_scratch", (B, S, SK), BF16)

    with ExitStack() as top:
        sb = lambda name, shape, dt=F32: top.enter_context(nc.sbuf_tensor(name, shape, dt))
        bank = [top.enter_context(nc.psum_tensor(f"bank{i}", [P, 512], F32)) for i in range(4, 8)]
        pair_bank = [top.enter_context(nc.psum_tensor(f"pair_bank{i}", [P, 2, 512], F32)) for i in range(2)]
        banks8 = [pair_bank[0][:, 0], pair_bank[0][:, 1], pair_bank[1][:, 0], pair_bank[1][:, 1]] + [b[:] for b in bank]
        ident = sb("ident", [P, P])
        flags = sb("flags", [1, 2])
        flags_i = sb("flags_i", [1, 1], I32)
        ones3 = sb("ones3", [ROWS - ROW_MAX, SK // 2], BF16)
        project_phase(nc, top, io, ks_dram, qs_dram, v_dram, banks8, ident, flags, flags_i, ones3)
        maximum_phase(nc, top, io, ks_dram, qs_dram, mask_dram, pair_bank, bank, ident, flags_i)
        main_phase(nc, top, io, out, ks_dram, qs_dram, v_dram, mask_dram, pair_bank, bank, ident, flags_i, ones3)


def project_phase(nc, top, io, ks_dram, qs_dram, v_dram, banks, ident, flags, flags_i, ones3):
    with ExitStack() as ctx:
        sb = lambda name, shape, dt=F32: ctx.enter_context(nc.sbuf_tensor(name, shape, dt))
        sem = lambda name: top.enter_context(nc.semaphore(name))
        wq, wk, wv = (sb(n, [P, KC, D]) for n in ("wq_sb", "wk_sb", "wv_sb"))
        x_sb = [sb(f"x_in{i}", [P, QT, D]) for i in range(2)]
        ctx_sb = [sb(f"ctx_in{i}", [P, KC, SK]) for i in range(2)]
        mask_u8 = [sb(f"mask_in{i}", [P, QT, SK], U8) for i in range(2)]
        mask_bf = sb("mask_bf", [P, QT, SK], BF16)
        masked = sb("masked", [P, QT])
        ones_bf = sb("ones_bf", [P, 1], BF16)
        block_of = sb("block_of", [P, H8])
        stats = sb("stats", [P, QT, 6])
        mv = sb("mv", [P, QT, 2])
        veps = sb("veps", [P, QT])
        neg_half = sb("neg_half", [P, QT])
        rstd = sb("rstd", [P, QT])
        rn = sb("rn", [P, QT])
        has_key = sb("has_key", [P, QT])
        zeros_bf = sb("zeros_bf", [3, H8 * S], BF16)
        xn = sb("xn", [P, QT, D])
        xnT = sb("xnT", [P, KC, S])
        nf_row = sb("nf_row", [1, S], BF16)
        parts_q = [[sb(f"parts_q{m}_{i}", [P, 3, S], BF16) for m in range(M2)] for i in range(2)]
        parts_k = [[sb(f"parts_k{m}_{i}", [P, 3, SK], BF16) for m in range(M2)] for i in range(2)]
        rest = [sb(f"rest{i}", [P, 512]) for i in range(3)]
        v_sb = sb("v_sb", [P, KT, D])
        absmax = sb("absmax", [P, 6])
        ab = sb("ab", [P, B, M2])
        bound = sb("bound", [B * M2, 1])
        bound1 = sb("bound1", [1, 2])
        c_row = sb("c_row", [1, SK])
        c_tmp = sb("c_tmp", [1, SK])
        k_only = sb("k_only", [1, 2])
        k_row = sb("k_row", [1, SK], BF16)

        wk_in, wv_in, wq_in, const_ready = sem("wk_in"), sem("wv_in"), sem("wq_in"), sem("const_ready")
        x_in = [sem(f"x_in_s{i}") for i in range(2)]
        ctx_in = [sem(f"ctx_in_s{i}") for i in range(2)]
        mask_in = [sem(f"mask_in_s{i}") for i in range(2)]
        x_free, ctx_free, mask_free = sem("x_free"), sem("ctx_free"), sem("mask_free")
        var_ready, rstd_ready, masked_ready = sem("var_ready"), sem("rstd_ready"), sem("masked_ready")
        xn_ready, nf_t_ready = sem("xn_ready"), sem("nf_t_ready")
        xT_ready, xT_sb_ready = sem("xT_ready"), sem("xT_sb_ready")
        qk_ready, head_part_ready = sem("qk_ready"), sem("head_part_ready")
        rest_ready, mid_ready, rest_used = sem("rest_ready"), sem("mid_ready"), sem("rest_used")
        k_parts_ready, q_parts_ready = sem("k_parts_ready"), sem("q_parts_ready")
        parts_stored = [sem(f"parts_stored{i}") for i in range(2)]
        v_ready, v_sb_ready, v_stored = sem("v_ready"), sem("v_sb_ready"), sem("v_stored")
        c_ready, c_sb_ready = sem("c_ready"), sem("c_sb_ready")
        rows_ready, rows_stored = sem("rows_ready"), sem("rows_stored")
        ab_ready, bound_ready, bound_sb, bound_t_ready = (
            sem("ab_ready"), sem("bound_ready"), sem("bound_sb"), sem("bound_t_ready"))
        maskbf_free = sem("maskbf_free")
        bank_free = [sem(f"bank_free{i}") for i in range(8)]
        zeros_ready, zeros_stored = sem("zeros_ready"), sem("zeros_stored")

        USE = {"k00": 0, "k01": 1, "k10": 2, "k11": 3, "v0": 4, "v1": 5, "v2": 6, "v3": 7,
               "xT0": 0, "xT1": 1, "nf": 2, "c0": 3, "c1": 4, "q0": 5, "q1": 6}
        qk_tiles = [("k", 0, 0), ("k", 0, 1), ("k", 1, 0), ("k", 1, 1), ("q", 0, 0), ("q", 1, 0)]
        tile_bank = lambda kind, m, half: banks[USE[f"q{m}" if kind == "q" else f"k{m}{half}"]]
        tile_free = lambda kind, m, half: bank_free[USE[f"q{m}" if kind == "q" else f"k{m}{half}"]]

        def part(i, kind, m, half, j):
            return parts_q[i][m][:, j, :] if kind == "q" else parts_k[i][m][:, j, half * 512:(half + 1) * 512]

        block = ctx.enter_context(nc.Block())

        @block.sync
        def _(sp):
            def weights(w, src, s):
                sp.dma_start(w[:], src.rearrange("(c p) n -> p c n", p=P)).then_inc(s, 16)

            def load(b, i):
                sp.wait_ge(ctx_free, 1)
                sp.sem_inc(ctx_free, -1)
                sp.dma_start(ctx_sb[i][:], io["ctxT"][b].rearrange("(c p) k -> p c k", p=P)).then_inc(ctx_in[i], 16)
                sp.wait_ge(x_free, 1)
                sp.sem_inc(x_free, -1)
                sp.dma_start(x_sb[i][:], io["x"][b].rearrange("(t p) d -> p t d", p=P)).then_inc(x_in[i], 16)
                sp.wait_ge(mask_free, 1)
                sp.sem_inc(mask_free, -1)
                sp.dma_start(mask_u8[i][:], io["mask"][b].rearrange("(t p) k -> p t k", p=P)).then_inc(mask_in[i], 16)

            def store_parts(b, i, m, parts, dst, runs):
                blocks = dst[b, m, 0:ROW_MASK].rearrange("(r d) h k -> (d h) r k", d=HD)
                for j, r0, n, step in runs:
                    src = parts[:, j, :].unsqueeze(1)
                    sp.dma_start(blocks[:, r0:r0 + (n - 1) * step + 1:step, :],
                                 src.broadcast_to([P, n, src.shape[2]])).then_inc(parts_stored[i], 16)

            def store(b, i):
                for m in range(M2):
                    sp.wait_ge(k_parts_ready, 2)
                    sp.sem_inc(k_parts_ready, -2)
                    store_parts(b, i, m, parts_k[i][m], ks_dram, K_RUNS)
                sp.wait_ge(v_sb_ready, 1)
                sp.sem_inc(v_sb_ready, -1)
                sp.dma_start(v_dram[b].rearrange("(t p) n -> p t n", p=P), v_sb[:]).then_inc(v_stored, 16)
                sp.wait_ge(rows_ready, 1)
                sp.sem_inc(rows_ready, -1)
                for m in range(M2):
                    sp.dma_start(ks_dram[b, m, ROW_MASK], k_row[0:1, :].unsqueeze(1).broadcast_to([1, H8, SK])
                                 ).then_inc(rows_stored, 16)
                    sp.dma_start(qs_dram[b, m, ROW_MASK], nf_row[0:1, :].unsqueeze(1).broadcast_to([1, H8, S])
                                 ).then_inc(rows_stored, 16)
                for m in range(M2):
                    sp.wait_ge(q_parts_ready, 1)
                    sp.sem_inc(q_parts_ready, -1)
                    store_parts(b, i, m, parts_q[i][m], qs_dram, Q_RUNS)

            weights(wk, io["wkT"], wk_in)
            load(0, 0)
            weights(wv, io["wvT"], wv_in)
            weights(wq, io["wqT"], wq_in)
            sp.wait_ge(zeros_ready, 1)
            sp.sem_inc(zeros_ready, -1)
            sp.dma_start(qs_dram[:, :, ROW_MAX:ROWS].rearrange("b m r h k -> r (b m) (h k)"),
                         zeros_bf[:].unsqueeze(1).broadcast_to([ROWS - ROW_MAX, B * M2, H8 * S])).then_inc(zeros_stored, 16)
            with sp.Fori(0, B - 2, 2) as b:
                for i in range(2):
                    load(b + i + 1, 1 - i)
                    store(b + i, i)
            load(B - 1, 1)
            store(B - 2, 0)
            store(B - 1, 1)
            sp.wait_ge(zeros_stored, 16)

        @block.gpsimd
        def _(pool):
            nc.gpsimd.memset(ident[:], 0.0)
            nc.gpsimd.memset(ones_bf[:], 1.0)
            nc.gpsimd.memset(neg_half[:], -0.5)
            nc.gpsimd.memset(block_of[:], 0.0)
            nc.gpsimd.memset(flags[:], 0.0)
            pool.drain()
            nc.gpsimd.affine_select(out=ident[:], in_=ident[:], compare_op=ALU.not_equal, fill=1.0, base=0,
                                    pattern=[[-1, P]], channel_multiplier=1)
            for d in range(HD):
                last = nc.gpsimd.affine_select(out=block_of[:], in_=block_of[:], compare_op=ALU.not_equal, fill=1.0,
                                               base=-H8 * d, pattern=[[-1, H8]], channel_multiplier=1)
                pool.drain()
            pool.drain().then_inc(const_ready, 1)
            nc.gpsimd.memset(zeros_bf[:], 0.0).then_inc(zeros_ready, 1)
            nc.gpsimd.memset(ones3[:], 1.0)
            with pool.Fori(0, B // 2) as bb:
                for i in range(2):
                    pool.wait_ge(var_ready, 1)
                    pool.sem_inc(var_ready, -1)
                    nc.gpsimd.tensor_scalar(veps[:], mv[:, :, 1], LN_EPS, None, ALU.add)
                    pool.drain()
                    nc.gpsimd.tensor_tensor(rstd[:], veps[:], neg_half[:], ALU.pow).then_inc(rstd_ready, 1)
                    for n, (kind, m, half) in enumerate(qk_tiles):
                        pool.wait_ge(mid_ready, 1)
                        pool.sem_inc(mid_ready, -1)
                        nc.gpsimd.tensor_tensor(part(i, kind, m, half, 2), rest[n % 3][:], part(i, kind, m, half, 1),
                                                ALU.subtract).then_inc(rest_used, 1)
                        pool.drain().then_inc(k_parts_ready if kind == "k" else q_parts_ready, 1)

        @block.scalar
        def _(act):
            with act.Fori(0, B // 2) as bb:
                for i in range(2):
                    def head_part(n):
                        kind, m, half = qk_tiles[n]
                        act.wait_ge(qk_ready, 1)
                        act.sem_inc(qk_ready, -1)
                        nc.scalar.activation(part(i, kind, m, half, 0), tile_bank(kind, m, half), ACT.Copy
                                             ).then_inc(head_part_ready, 1)

                    def middle_part(n):
                        kind, m, half = qk_tiles[n]
                        act.wait_ge(rest_ready, 1)
                        act.sem_inc(rest_ready, -1)
                        nc.scalar.activation(part(i, kind, m, half, 1), rest[n % 3][:], ACT.Copy).then_inc(mid_ready, 1)

                    def mask_sum(t):
                        nc.scalar.activation(mask_bf[:, t], mask_u8[i][:, t], ACT.Copy, accum_out=masked[:, t:t + 1])

                    act.wait_ge(parts_stored[i], 2 * 16 * N_RUNS)
                    act.sem_inc(parts_stored[i], -2 * 16 * N_RUNS)
                    head_part(0)
                    act.wait_ge(mask_in[i], 16)
                    act.sem_inc(mask_in[i], -16)
                    act.wait_ge(maskbf_free, 1)
                    act.sem_inc(maskbf_free, -1)
                    mask_sum(0)
                    for n in range(1, 4):
                        head_part(n)
                        middle_part(n - 1)
                        mask_sum(n)
                    act.drain().then_inc(mask_free, 1)
                    act.drain().then_inc(masked_ready, 1)
                    middle_part(3)
                    act.wait_ge(v_stored, 16)
                    act.sem_inc(v_stored, -16)
                    for n in range(4):
                        act.wait_ge(v_ready, 1)
                        act.sem_inc(v_ready, -1)
                        nc.scalar.activation(v_sb[:, 2 * n:2 * n + 2, :], banks[USE[f"v{n}"]], ACT.Copy
                                             ).then_inc(bank_free[USE[f"v{n}"]], 1)
                    act.drain().then_inc(v_sb_ready, 1)
                    act.wait_ge(xT_ready, 2)
                    act.sem_inc(xT_ready, -2)
                    for kc in range(KC):
                        nc.scalar.activation(xnT[:, kc], banks[USE[f"xT{kc}"]], ACT.Copy
                                             ).then_inc(bank_free[USE[f"xT{kc}"]], 1)
                    act.drain().then_inc(xT_sb_ready, 1)
                    act.wait_ge(c_ready, 2)
                    act.sem_inc(c_ready, -2)
                    for n in range(2):
                        nc.scalar.activation(c_row[0:1, n * 512:(n + 1) * 512], banks[USE[f"c{n}"]][0:1, :], ACT.Copy
                                             ).then_inc(bank_free[USE[f"c{n}"]], 1)
                    act.drain().then_inc(c_sb_ready, 1)
                    head_part(4)
                    head_part(5)
                    middle_part(4)
                    middle_part(5)

        @block.vector
        def _(dve):
            for s in bank_free:
                dve.sem_inc(s, 1)
            dve.sem_inc(maskbf_free, 1)
            dve.sem_inc(rest_used, 3)
            dve.sem_inc(v_stored, 16)
            dve.sem_inc(rows_stored, 64)
            for i in range(2):
                dve.sem_inc(parts_stored[i], 2 * 16 * N_RUNS)
            dve.sem_inc(x_free, 2)
            dve.sem_inc(ctx_free, 2)
            dve.sem_inc(mask_free, 2)
            with dve.Fori(0, B // 2) as bb:
                for i in range(2):
                    b = bb * 2 + i
                    dve.wait_ge(x_in[i], 16)
                    dve.sem_inc(x_in[i], -16)
                    for t in range(QT):
                        nc.vector.bn_stats(stats[:, t], x_sb[i][:, t])
                    dve.drain()
                    for t in range(QT):
                        nc.vector.bn_aggr(mv[:, t], stats[:, t])
                    dve.drain().then_inc(var_ready, 1)
                    def rest_and_max(n):
                        kind, m, half = qk_tiles[n]
                        dve.wait_ge(head_part_ready, 1)
                        dve.sem_inc(head_part_ready, -1)
                        dve.wait_ge(rest_used, 1)
                        dve.sem_inc(rest_used, -1)
                        nc.vector.tensor_tensor(rest[n % 3][:], tile_bank(kind, m, half), part(i, kind, m, half, 0),
                                                ALU.subtract).then_inc(rest_ready, 1)
                        nc.vector.tensor_reduce(absmax[:, n:n + 1], tile_bank(kind, m, half), op=ALU.max, axis=AX.X,
                                                apply_absolute_value=True).then_inc(tile_free(kind, m, half), 1)

                    for n in range(4):
                        rest_and_max(n)
                    dve.wait_ge(masked_ready, 1)
                    dve.sem_inc(masked_ready, -1)
                    nc.vector.tensor_scalar(has_key[:], masked[:], float(SK), None, ALU.is_lt)
                    dve.wait_ge(rstd_ready, 1)
                    dve.sem_inc(rstd_ready, -1)
                    dve.drain()
                    nc.vector.tensor_tensor(rn[:], rstd[:], has_key[:], ALU.mult)
                    dve.drain()
                    for t in range(QT):
                        nc.vector.tensor_scalar(xn[:, t], x_sb[i][:, t], mv[:, t, 0:1], rn[:, t:t + 1],
                                                ALU.subtract, ALU.mult)
                    dve.drain().then_inc(xn_ready, 1)
                    dve.drain().then_inc(x_free, 1)
                    dve.wait_ge(nf_t_ready, 1)
                    dve.sem_inc(nf_t_ready, -1)
                    dve.wait_ge(rows_stored, 64)
                    dve.sem_inc(rows_stored, -64)
                    nc.vector.tensor_copy(nf_row[0:1, :], banks[USE["nf"]][0:1, :]).then_inc(bank_free[USE["nf"]], 1)
                    dve.wait_ge(c_sb_ready, 1)
                    dve.sem_inc(c_sb_ready, -1)
                    nc.vector.scalar_tensor_tensor(out=c_tmp[:], in0=c_row[:], scalar=-float(S), in1=c_row[:],
                                                   op0=ALU.add, op1=ALU.mult)
                    dve.drain()
                    nc.vector.tensor_reduce(k_only[0:1, 0:1], c_tmp[:], op=ALU.min, axis=AX.X)
                    dve.drain()
                    nc.vector.tensor_scalar(k_only[0:1, 1:2], k_only[0:1, 0:1], 0.0, None, ALU.is_ge)
                    dve.drain()
                    nc.vector.tensor_scalar(k_row[0:1, :], c_row[:], -BIG / S, k_only[0:1, 1:2], ALU.mult, ALU.mult)
                    nc.vector.tensor_scalar(k_only[0:1, 0:1], k_only[0:1, 1:2], -1.0, 1.0, ALU.mult, ALU.add)
                    dve.drain().then_inc(rows_ready, 1)
                    dve.wait_ge(const_ready, 1)
                    nc.vector.tensor_tensor(flags[0:1, 0:1], flags[0:1, 0:1], k_only[0:1, 0:1], ALU.max)
                    for n in range(4, 6):
                        rest_and_max(n)
                    dve.drain()
                    nc.vector.tensor_tensor(absmax[:, 0:4:2], absmax[:, 0:4:2], absmax[:, 1:4:2], ALU.max)
                    dve.drain()
                    nc.vector.tensor_tensor(ab[:, b, :], absmax[:, 4:6], absmax[:, 0:4:2], ALU.mult)
            dve.drain().then_inc(ab_ready, 1)
            dve.wait_ge(bound_ready, 1)
            dve.sem_inc(bound_ready, -1)
            nc.vector.tensor_reduce(bound[:], banks[7][0:B * M2, 0:H8], op=ALU.max, axis=AX.X).then_inc(bound_sb, 1)
            dve.wait_ge(bound_t_ready, 1)
            dve.sem_inc(bound_t_ready, -1)
            nc.vector.tensor_reduce(bound1[0:1, 0:1], banks[7][0:1, 0:B * M2], op=ALU.max, axis=AX.X)
            dve.drain()
            nc.vector.tensor_scalar(bound1[0:1, 1:2], bound1[0:1, 0:1], SAFE * HD ** 0.5, None, ALU.is_le)
            dve.drain()
            nc.vector.tensor_scalar(flags[0:1, 1:2], bound1[0:1, 1:2], -1.0, 1.0, ALU.mult, ALU.add)
            dve.drain()
            nc.vector.tensor_tensor(flags_i[:], flags[0:1, 0:1], flags[0:1, 1:2], ALU.max)
            dve.wait_ge(rows_stored, 64)
            dve.wait_ge(v_stored, 16)
            for i in range(2):
                dve.wait_ge(parts_stored[i], 2 * 16 * N_RUNS)

        @block.tensor
        def _(pe):
            pe.wait_ge(wk_in, 16)

            def use_bank(name):
                pe.wait_ge(bank_free[USE[name]], 1)
                pe.sem_inc(bank_free[USE[name]], -1)
                return banks[USE[name]]

            with pe.Fori(0, B // 2) as bb:
                for i in range(2):
                    def project(kind, m, half):
                        w, src = (wq, xnT) if kind == "q" else (wk, ctx_sb[i])
                        dst = use_bank(f"q{m}" if kind == "q" else f"k{m}{half}")
                        for kc in range(KC):
                            last = nc.tensor.matmul(dst, w[:, kc, m * P:(m + 1) * P],
                                                    src[:, kc, half * 512:(half + 1) * 512],
                                                    start=(kc == 0), stop=(kc == KC - 1))
                        last.then_inc(qk_ready, 1)

                    pe.wait_ge(ctx_in[i], 16)
                    pe.sem_inc(ctx_in[i], -16)
                    for tile in qk_tiles[:4]:
                        project(*tile)
                    pe.wait_ge(wv_in, 16)
                    for n in range(4):
                        dst = use_bank(f"v{n}")
                        for e in range(2):
                            kt = 2 * n + e
                            for kc in range(KC):
                                last = nc.tensor.matmul(dst[:, e * D:(e + 1) * D], ctx_sb[i][:, kc, kt * P:(kt + 1) * P],
                                                        wv[:, kc, :], start=(kc == 0), stop=(kc == KC - 1))
                        last.then_inc(v_ready, 1)
                    pe.wait_ge(xn_ready, 1)
                    pe.sem_inc(xn_ready, -1)
                    pe.wait_ge(const_ready, 1)
                    for kc in range(KC):
                        dst = use_bank(f"xT{kc}")
                        for t in range(QT):
                            last = nc.tensor.transpose(dst[:, t * P:(t + 1) * P], xn[:, t, kc * P:(kc + 1) * P], ident[:])
                        last.then_inc(xT_ready, 1)
                    dst = use_bank("nf")
                    for t in range(QT):
                        last = nc.tensor.transpose(dst[0:1, t * P:(t + 1) * P], has_key[:, t:t + 1], ident[:])
                    last.then_inc(nf_t_ready, 1)
                    for n in range(2):
                        dst = use_bank(f"c{n}")
                        for t in range(QT):
                            last = nc.tensor.matmul(dst[0:1, :], ones_bf[:], mask_bf[:, t, n * 512:(n + 1) * 512],
                                                    start=(t == 0), stop=(t == QT - 1))
                        last.then_inc(c_ready, 1)
                    pe.drain().then_inc(maskbf_free, 1)
                    pe.wait_ge(xT_sb_ready, 1)
                    pe.sem_inc(xT_sb_ready, -1)
                    pe.wait_ge(wq_in, 16)
                    for tile in qk_tiles[4:]:
                        project(*tile)
                    pe.drain().then_inc(ctx_free, 1)
            pe.wait_ge(ab_ready, 1)
            pe.sem_inc(ab_ready, -1)
            pe.wait_ge(bank_free[7], 1)
            pe.sem_inc(bank_free[7], -1)
            nc.tensor.matmul(banks[7][0:B * M2, 0:H8], ab[:].rearrange("p b m -> p (b m)"), block_of[:],
                             start=True, stop=True).then_inc(bound_ready, 1)
            pe.wait_ge(bound_sb, 1)
            pe.sem_inc(bound_sb, -1)
            nc.tensor.transpose(banks[7][0:1, 0:B * M2], bound[:], ident[0:B * M2, 0:B * M2]).then_inc(bound_t_ready, 1)


def maximum_phase(nc, top, io, ks_dram, qs_dram, mask_dram, pair_bank, bank, ident, flags_i):
    with ExitStack() as ctx:
        sb = lambda name, shape, dt=F32: ctx.enter_context(nc.sbuf_tensor(name, shape, dt))
        sem = lambda name: top.enter_context(nc.semaphore(name))
        ks = sb("max_ks", [P, H8, SK], BF16)
        qs = sb("max_qs", [P, H8, S], BF16)
        mask_u8 = sb("max_mask_in", [P, QT, SK], U8)
        mask_bf = sb("max_mask_bf", [P, QT, SK], BF16)
        mask_fix = sb("max_mask_fix", [P, QT, SK], BF16)
        masked = sb("max_masked", [P, QT])
        has_key = sb("max_has_key", [P, QT])
        lower = sb("max_lower", [P, P], BF16)
        neg_max = sb("neg_max", [P, QT, H8])
        rest = sb("max_rest", [H8, S])
        parts = sb("max_parts", [H8, 3, S], BF16)

        mask_in, mask_done, mask_stored = sem("mmask_in"), sem("mmask_done"), sem("mmask_stored")
        mask_ready, mask_used = sem("mmask_ready"), sem("mmask_used")
        qk_in, qk_used = sem("mqk_in"), sem("mqk_used")
        lower_ready = sem("lower_ready")
        s_ready, s_read = [sem(f"ms_ready{i}") for i in range(2)], [sem(f"ms_read{i}") for i in range(2)]
        neg_ready, negT_ready = sem("neg_ready"), sem("negT_ready")
        parts_ready, parts_stored = sem("mparts_ready"), sem("mparts_stored")
        block = ctx.enter_context(nc.Block())

        @block.sync
        def _(sp):
            general = sp.value_load(flags_i[0:1, 0:1], min_val=0, max_val=1)
            with sp.If(general == 1):
                with sp.Fori(0, B) as b:
                    sp.dma_start(mask_u8[:], io["mask"][b].rearrange("(t p) k -> p t k", p=P)).then_inc(mask_in, 16)
                    sp.wait_ge(mask_done, 1)
                    sp.sem_inc(mask_done, -1)
                    sp.dma_start(mask_dram[b].rearrange("(t p) k -> p t k", p=P), mask_fix[:]).then_inc(mask_stored, 16)
                    for m in range(M2):
                        sp.dma_start(ks[0:ROW_MAX], ks_dram[b, m, 0:ROW_MAX]).then_inc(qk_in, 16)
                        sp.dma_start(qs[0:ROW_MAX], qs_dram[b, m, 0:ROW_MAX]).then_inc(qk_in, 16)
                        sp.wait_ge(parts_ready, 1)
                        sp.sem_inc(parts_ready, -1)
                        sp.dma_start(qs_dram[b, m, ROW_MAX:ROWS].rearrange("r h k -> h r k"), parts[:]
                                     ).then_inc(parts_stored, 16)
                        sp.wait_ge(parts_stored, 16)
                        sp.sem_inc(parts_stored, -16)
                    sp.wait_ge(mask_stored, 16)
                    sp.sem_inc(mask_stored, -16)

        @block.vector
        def _(dve):
            general = dve.value_load(flags_i[0:1, 0:1], min_val=0, max_val=1)
            with dve.If(general == 1):
                nc.vector.tensor_scalar(lower[:], ident[:], -BIG, None, ALU.mult).then_inc(lower_ready, 1)
                dve.sem_inc(s_read[0], 1)
                dve.sem_inc(s_read[1], 1)
                with dve.Fori(0, B) as b:
                    dve.wait_ge(mask_in, 16)
                    dve.sem_inc(mask_in, -16)
                    nc.vector.tensor_copy(mask_bf[:], mask_u8[:])
                    dve.drain()
                    nc.vector.tensor_reduce(masked[:], mask_bf[:], op=ALU.add, axis=AX.X)
                    dve.drain()
                    nc.vector.tensor_scalar(has_key[:], masked[:], float(SK), None, ALU.is_lt)
                    dve.drain()
                    for t in range(QT):
                        nc.vector.tensor_scalar(mask_fix[:, t], mask_bf[:, t], has_key[:, t:t + 1], None, ALU.mult)
                    dve.drain().then_inc(mask_done, 1)
                    dve.sem_inc(mask_ready, 1)
                    for m in range(M2):
                        for h in range(H8):
                            for t in range(QT):
                                i = t % 2
                                dve.wait_ge(s_ready[i], 1)
                                dve.sem_inc(s_ready[i], -1)
                                nc.vector.tensor_reduce(neg_max[:, t, h:h + 1], pair_bank[i][:], op=ALU.max, axis=AX.XY,
                                                        negate=True).then_inc(s_read[i], 1)
                        dve.drain().then_inc(neg_ready, 1)
                        dve.wait_ge(negT_ready, 1)
                        dve.sem_inc(negT_ready, -1)
                        neg_t = bank[0][0:H8, :]
                        nc.vector.tensor_copy(parts[:, 0], neg_t)
                        dve.drain()
                        nc.vector.tensor_tensor(rest[:], neg_t, parts[:, 0], ALU.subtract)
                        dve.drain()
                        nc.vector.tensor_copy(parts[:, 1], rest[:])
                        dve.drain()
                        nc.vector.tensor_tensor(parts[:, 2], rest[:], parts[:, 1], ALU.subtract)
                        dve.drain().then_inc(parts_ready, 1)

        @block.tensor
        def _(pe):
            general = pe.value_load(flags_i[0:1, 0:1], min_val=0, max_val=1)
            with pe.If(general == 1):
                pe.wait_ge(lower_ready, 1)
                pe.sem_inc(lower_ready, -1)
                with pe.Fori(0, B) as b:
                    pe.wait_ge(mask_ready, 1)
                    pe.sem_inc(mask_ready, -1)
                    for m in range(M2):
                        pe.wait_ge(qk_in, 32)
                        pe.sem_inc(qk_in, -32)
                        for h in range(H8):
                            for t in range(QT):
                                i = t % 2
                                pe.wait_ge(s_read[i], 1)
                                pe.sem_inc(s_read[i], -1)
                                for e in range(2):
                                    cols = slice(e * 512, (e + 1) * 512)
                                    nc.tensor.matmul(pair_bank[i][:, e], qs[0:ROW_MAX, h, t * P:(t + 1) * P],
                                                     ks[0:ROW_MAX, h, cols], start=True, stop=False)
                                    last = nc.tensor.matmul(pair_bank[i][:, e], lower[:], mask_fix[:, t, cols],
                                                            start=False, stop=True)
                                last.then_inc(s_ready[i], 1)
                        pe.wait_ge(neg_ready, 1)
                        pe.sem_inc(neg_ready, -1)
                        for t in range(QT):
                            last = nc.tensor.transpose(bank[0][0:H8, t * P:(t + 1) * P], neg_max[:, t], ident[:])
                        last.then_inc(negT_ready, 1)


def main_phase(nc, top, io, out, ks_dram, qs_dram, v_dram, mask_dram, pair_bank, bank, ident, flags_i, ones3):
    o_bank, misc = bank[0:2], bank[2:4]
    with ExitStack() as ctx:
        sb = lambda name, shape, dt=F32: ctx.enter_context(nc.sbuf_tensor(name, shape, dt))
        sem = lambda name: top.enter_context(nc.semaphore(name))
        ks = sb("ks", [P, G, HG, SK], BF16)
        qs = sb("qs", [P, G, HG, S], BF16)
        v_in_sb = [sb(f"v_in_sb{i}", [P, KT, HG * HD]) for i in range(2)]
        va = sb("va", [P, KT, G, HG, 32])
        probs = [sb(f"probs{i}", [P, HG, S]) for i in range(2)]
        mask_fix = sb("mask_fix", [P, QT, SK], BF16)
        lower = sb("lower", [P, P], BF16)
        o_sb = sb("o_sb", [P, S])
        den, den2, inv = sb("den", [P, S]), sb("den2", [P, S]), sb("inv", [P, S // 32])
        o_t = sb("o_t", [P, G, S])
        wo = sb("wo", [P, G, D])
        wqkv = sb("wqkv", [P, KC, 3 * D])
        wout = sb("wout", [P, KC, D])
        w1, w2 = (sb(n, [P, KC, FT * P]) for n in ("w1", "w2"))
        w3 = sb("w3", [P, FT, D])
        wr_b, g1_b, g2_b = (sb(n, [P, D]) for n in ("wr_b", "g1_b", "g2_b"))
        iota_r = sb("iota_r", [P, CAP])
        before = sb("before", [P, QT, S], BF16)
        block_of = sb("block_of2", [P, H8])
        causal = sb("causal", [P, CAP])
        neg_half = sb("neg_half2", [P, QT])
        x1 = sb("x1", [P, QT, D])
        y = sb("y", [P, QT, D])
        base = sb("base", [P, QT, D])
        out_sb = sb("out_sb", [P, QT, D])
        stats = sb("stats2", [P, QT, 6])
        mv = sb("mv2", [P, QT, 2])
        veps = sb("veps2", [P, QT])
        rstd = sb("rstd2", [P, QT])
        prod = sb("prod", [P, D])
        score = sb("score", [P, QT])
        all_scores = sb("all_scores", [P, S])
        ties = sb("ties", [P, S])
        rank = sb("rank", [P, QT])
        sel = sb("sel", [P, QT, CAP])
        sel_t = sb("sel_t", [P, S])
        x_sel = sb("x_sel", [P, D])
        x_keep = sb("x_keep", [P, D])
        ms = sb("ms", [P, 4])
        hid = sb("hid", [P, D])
        hid2 = sb("hid2", [P, D])
        hid_t = sb("hid_t", [P, KC, CAP])
        q_t = sb("q_t", [P, KC, CAP])
        v_s = sb("v_s", [P, D])
        k_block = sb("k_block", [P, M2, H8, CAP])
        p_t = k_block[:].rearrange("p m h k -> p (m h) k")
        sc = sb("sc", [P, H, CAP])
        s_max = sb("s_max", [P, H])
        s_den = sb("s_den", [P, H])
        o_s = sb("o_s", [P, D])
        os_t = sb("os_t", [P, KC, CAP])
        att = sb("att", [P, D])
        sig = [sb(f"sig{r}", [P, 3 * P]) for r in range(2)]
        up = [sb(f"up{r}", [P, 3 * P]) for r in range(2)]
        gate = sb("gate", [P, FT, P])
        delta = sb("delta", [P, D])

        w_zero, w_in, consts, lower_set = sem("w_zero"), sem("w2_in"), sem("consts"), sem("lower_set")
        rows_set, group_in = sem("rows_set"), [sem(f"group_in{g}") for g in range(G)]
        group_free, v_in, v_in_free = sem("group_free"), [sem(f"v_in{i}") for i in range(2)], sem("v_in_free")
        va_ready, va_free = sem("va_ready"), sem("va_free")
        maskfix_in, maskfix_free = sem("maskfix_in"), sem("maskfix_free")
        s_ready, s_read = [sem(f"s_ready{i}") for i in range(2)], [sem(f"s_read{i}") for i in range(2)]
        o_ready, o_free, ot_ready, ot_free = sem("o_ready"), sem("o_free"), sem("ot_ready"), sem("ot_free")
        misc_free = [sem(f"misc_free{i}") for i in range(2)]
        xres_in, xres_free = sem("xres_in"), sem("xres_free")
        wo_ready, var2_ready, rstd2_ready, y_ready = sem("wo_ready"), sem("var2_ready"), sem("rstd2_ready"), sem("y_ready")
        score_ready, spread_ready, sel_ready = sem("score_ready"), sem("spread_ready"), sem("sel_ready")
        base_ready, base_free, all_ready = sem("base_ready"), sem("base_free"), sem("all_ready")
        gather_ready, selT_ready, selT_sb = sem("gather_ready"), sem("selT_ready"), sem("selT_sb")
        ms_ready, rms_ready, hid_ready, hidT_ready, hidT_sb = (
            sem("ms_ready"), sem("rms_ready"), sem("hid_ready"), sem("hidT_ready"), sem("hidT_sb"))
        qv_ready, k_ready, qv_sb, kb_ready = sem("qv_ready"), sem("k_ready"), sem("qv_sb"), sem("kb_ready")
        sc_ready, scm_ready, p_ready, den_ready = sem("sc_ready"), sem("scm_ready"), sem("p_ready"), sem("p_sum")
        pT_ready, pT_sb, pv_ready, os_ready = sem("pT_ready"), sem("pT_sb"), sem("pv_ready"), sem("os_ready")
        osT_ready, osT_sb, att_ready = sem("osT_ready"), sem("osT_sb"), sem("att_ready")
        hid2_ready, hid2T_ready, hid2T_sb = sem("hid2_ready"), sem("hid2T_ready"), sem("hid2T_sb")
        u_ready, w_ready, sig_ready, sig_used, gate_ready = (
            sem("u_ready"), sem("w_ready"), sem("sig_ready"), sem("sig_used"), sem("gate_ready"))
        ff_ready, delta_ready, scat_ready = sem("ff_ready"), sem("delta_ready"), sem("scat_ready")
        out_ready, out_stored = sem("out_ready"), sem("out_stored")

        block = ctx.enter_context(nc.Block())
        N_W = 4 + 1 + 1 + 1 + 1 + 2 + 3

        @block.sync
        def _(sp):
            general = sp.value_load(flags_i[0:1, 0:1], min_val=0, max_val=1)
            def load_group(b, g):
                m, h0 = g // (G // M2), (g % (G // M2)) * HG
                sp.wait_ge(group_free, 1)
                sp.sem_inc(group_free, -1)
                sp.dma_start(ks[0:ROW_MAX, g], ks_dram[b, m, 0:ROW_MAX, h0:h0 + HG, :]).then_inc(group_in[g], 16)
                sp.dma_start(qs[0:ROWS, g], qs_dram[b, m, :, h0:h0 + HG, :]).then_inc(group_in[g], 16)
                if g == G - 1:
                    with sp.If(general == 1):
                        sp.wait_ge(maskfix_free, 1)
                        sp.sem_inc(maskfix_free, -1)
                        sp.dma_start(mask_fix[:], mask_dram[b].rearrange("(t p) k -> p t k", p=P)).then_inc(maskfix_in, 16)
                sp.wait_ge(v_in_free, 1)
                sp.sem_inc(v_in_free, -1)
                src = v_dram[b].rearrange("(t p) n -> p t n", p=P)[:, :, g * HG * HD:(g + 1) * HG * HD]
                sp.dma_start(v_in_sb[g % 2][:], src).then_inc(v_in[g % 2], 16)

            def load_x(b):
                sp.wait_ge(xres_free, 1)
                sp.sem_inc(xres_free, -1)
                sp.dma_start(x1[:], io["x"][b].rearrange("(t p) d -> p t d", p=P)).then_inc(xres_in, 16)

            def store(b):
                sp.wait_ge(out_ready, 1)
                sp.sem_inc(out_ready, -1)
                sp.dma_start(out[b].rearrange("(t p) d -> p t d", p=P), out_sb[:]).then_inc(out_stored, 16)

            sp.dma_start(ks[ROW_MAX:ROWS].rearrange("p g j (e k) -> p (g j e) k", e=2),
                         ones3[:].unsqueeze(1).broadcast_to([ROWS - ROW_MAX, G * HG * 2, SK // 2])).then_inc(rows_set, 16)
            load_group(0, 0)
            load_group(0, 1)
            sp.wait_ge(w_zero, 1)
            sp.sem_inc(w_zero, -1)
            wo_rows = io["woT"].rearrange("(g j d) n -> j d g n", g=G, j=HG)
            for j in range(HG):
                sp.dma_start(wo[32 * j:32 * j + HD], wo_rows[j]).then_inc(w_in, 16)
            sp.dma_start(wqkv[:], io["wqkvT"].rearrange("(c p) n -> p c n", p=P)).then_inc(w_in, 16)
            sp.dma_start(wout[:], io["woutT"].rearrange("(c p) n -> p c n", p=P)).then_inc(w_in, 16)
            sp.dma_start(w1[:, :, 0:DFF], io["w1T"].rearrange("(c p) n -> p c n", p=P)).then_inc(w_in, 16)
            sp.dma_start(w2[:, :, 0:DFF], io["w2T"].rearrange("(c p) n -> p c n", p=P)).then_inc(w_in, 16)
            full = DFF // P
            sp.dma_start(w3[:, 0:full], io["w3T"][0:full * P].rearrange("(c p) n -> p c n", p=P)).then_inc(w_in, 16)
            sp.dma_start(w3[0:DFF - full * P, full], io["w3T"][full * P:DFF]).then_inc(w_in, 16)
            for dst, name in ((wr_b, "w_router"), (g1_b, "g1"), (g2_b, "g2")):
                sp.dma_start(dst[:], io[name].partition_broadcast(P)).then_inc(w_in, 16)
            for g in range(2, G):
                load_group(0, g)
            for b in range(2):
                for g in range(G - 1):
                    load_group(b + 1, g)
                load_x(b)
                load_group(b + 1, G - 1)
            with sp.Fori(2, B - 1) as b:
                for g in range(G - 1):
                    load_group(b + 1, g)
                store(b - 2)
                load_x(b)
                load_group(b + 1, G - 1)
            store(B - 3)
            load_x(B - 1)
            store(B - 2)
            store(B - 1)
            sp.wait_ge(out_stored, 16)

        @block.gpsimd
        def _(pool):
            def spread_v(g):
                pool.wait_ge(v_in[g % 2], 16)
                pool.sem_inc(v_in[g % 2], -16)
                pool.wait_ge(va_free, 1)
                pool.sem_inc(va_free, -1)
                nc.gpsimd.tensor_copy(va[:, :, g, :, 0:HD], v_in_sb[g % 2][:].rearrange("p t (h d) -> p t h d", h=HG)
                                      ).then_inc(va_ready, 1)
                pool.drain().then_inc(v_in_free, 1)

            nc.gpsimd.memset(va[:].rearrange("p t g h c -> p (t g h) c")[:, :, HD:32], 1.0)
            nc.gpsimd.memset(wo[:], 0.0)
            nc.gpsimd.memset(w1[:, :, DFF:], 0.0)
            nc.gpsimd.memset(w2[:, :, DFF:], 0.0)
            nc.gpsimd.memset(w3[:, DFF // P], 0.0)
            pool.drain().then_inc(w_zero, 1)
            spread_v(0)
            spread_v(1)
            nc.gpsimd.memset(neg_half[:], -0.5)
            nc.gpsimd.memset(before[:], 1.0)
            nc.gpsimd.memset(block_of[:], 1.0)
            nc.gpsimd.memset(causal[:], 0.0)
            nc.gpsimd.iota(iota_r[:], pattern=[[1, CAP]], base=0, channel_multiplier=0,
                           allow_small_or_imprecise_dtypes=True)
            pool.drain()
            for t in range(QT):
                nc.gpsimd.affine_select(out=before[:, t], in_=before[:, t], compare_op=ALU.is_gt, fill=0.0,
                                        base=t * P, pattern=[[-1, S]], channel_multiplier=1)
            nc.gpsimd.affine_select(out=block_of[:], in_=block_of[:], compare_op=ALU.is_ge, fill=0.0,
                                    base=0, pattern=[[-HD, H8]], channel_multiplier=1)
            nc.gpsimd.affine_select(out=causal[:], in_=causal[:], compare_op=ALU.is_ge, fill=-1e30,
                                    base=0, pattern=[[-1, CAP]], channel_multiplier=1)
            pool.drain()
            nc.gpsimd.affine_select(out=block_of[:], in_=block_of[:], compare_op=ALU.is_gt, fill=0.0,
                                    base=HD, pattern=[[HD, H8]], channel_multiplier=-1)
            pool.drain().then_inc(consts, 1)

            def rms(col):
                pool.wait_ge(ms_ready, 1)
                pool.sem_inc(ms_ready, -1)
                nc.gpsimd.tensor_scalar(ms[:, col + 1:col + 2], ms[:, col:col + 1], 1.0 / D, RMS_EPS, ALU.mult, ALU.add)
                pool.drain()
                nc.gpsimd.tensor_tensor(ms[:, col:col + 1], ms[:, col + 1:col + 2], neg_half[:, 0:1], ALU.pow
                                        ).then_inc(rms_ready, 1)

            def norm():
                pool.wait_ge(var2_ready, 1)
                pool.sem_inc(var2_ready, -1)
                nc.gpsimd.tensor_scalar(veps[:], mv[:, :, 1], LN_EPS, None, ALU.add)
                pool.drain()
                nc.gpsimd.tensor_tensor(rstd[:], veps[:], neg_half[:], ALU.pow).then_inc(rstd2_ready, 1)

            def make_base():
                pool.wait_ge(y_ready, 1)
                pool.sem_inc(y_ready, -1)
                pool.wait_ge(base_free, 1)
                pool.sem_inc(base_free, -1)
                nc.gpsimd.tensor_tensor(base[:], x1[:], y[:], ALU.add).then_inc(base_ready, 1)
                pool.drain().then_inc(xres_free, 1)

            def batch(first, last):
                norm()
                spread_v(3)
                rms(0)
                if not first:
                    rms(2)
                if not last:
                    spread_v(0)
                    spread_v(1)
                make_base()
                if not last:
                    spread_v(2)

            for g in (2, 3, 0, 1, 2):
                spread_v(g)
            batch(first=True, last=False)
            with pool.Fori(2, B - 1) as b:
                batch(first=False, last=False)
            batch(first=False, last=True)
            norm()
            rms(0)
            rms(2)
            make_base()
            rms(2)

        def act_step(act, s):
            for pr in range(2):
                act.wait_ge(s_ready[pr], 1)
                act.sem_inc(s_ready[pr], -1)
                nc.scalar.activation(probs[s % 2][:, 2 * pr:2 * pr + 2, :], pair_bank[pr][:], ACT.Exp,
                                     scale=HD ** -0.5).then_inc(s_read[pr], 1)

        def act_ffn(act, stage):
            if stage == "selT":
                act.wait_ge(selT_ready, 1)
                act.sem_inc(selT_ready, -1)
                nc.scalar.activation(sel_t[:], misc[1][:], ACT.Copy).then_inc(misc_free[1], 1)
                act.drain().then_inc(selT_sb, 1)
            elif stage == "spread":
                act.wait_ge(spread_ready, 1)
                act.sem_inc(spread_ready, -1)
                nc.scalar.activation(all_scores[:], misc[1][:], ACT.Copy).then_inc(misc_free[1], 1)
                act.drain().then_inc(all_ready, 1)
            elif stage == "hid2T":
                act.wait_ge(hid2T_ready, 1)
                act.sem_inc(hid2T_ready, -1)
                nc.scalar.activation(hid_t[:], misc[1][:, 0:KC * CAP].rearrange("p (c k) -> p c k", c=KC), ACT.Copy
                                     ).then_inc(misc_free[1], 1)
                act.drain().then_inc(hid2T_sb, 1)
            elif stage == "hidT":
                act.wait_ge(hidT_ready, 1)
                act.sem_inc(hidT_ready, -1)
                nc.scalar.activation(hid_t[:], misc[1][:, 0:KC * CAP].rearrange("p (c k) -> p c k", c=KC), ACT.Copy
                                     ).then_inc(misc_free[1], 1)
                act.drain().then_inc(hidT_sb, 1)
            elif stage == "qv":
                act.wait_ge(qv_ready, 1)
                act.sem_inc(qv_ready, -1)
                nc.scalar.activation(q_t[:], misc[1][:, 0:KC * CAP].rearrange("p (c k) -> p c k", c=KC), ACT.Copy)
                nc.scalar.activation(v_s[:], misc[1][:, D:2 * D], ACT.Copy).then_inc(misc_free[1], 1)
                act.drain().then_inc(qv_sb, 1)
            elif stage == "exp":
                act.wait_ge(scm_ready, 1)
                act.sem_inc(scm_ready, -1)
                nc.scalar.activation(sc[:], sc[:], ACT.Exp, scale=HD ** -0.5).then_inc(p_ready, 1)
                act.drain().then_inc(den_ready, 1)
            elif stage.startswith("pT"):
                n = int(stage[2])
                act.wait_ge(pT_ready, 1)
                act.sem_inc(pT_ready, -1)
                nc.scalar.activation(p_t[:, 4 * n:4 * n + 4, :], misc[n % 2][:].rearrange("p (h k) -> p h k", h=4), ACT.Copy
                                     ).then_inc(misc_free[n % 2], 1)
                if n == 3:
                    act.drain().then_inc(pT_sb, 1)
            elif stage == "osT":
                act.wait_ge(osT_ready, 1)
                act.sem_inc(osT_ready, -1)
                nc.scalar.activation(os_t[:], misc[0][:, 0:KC * CAP].rearrange("p (c k) -> p c k", c=KC), ACT.Copy
                                     ).then_inc(misc_free[0], 1)
                act.drain().then_inc(osT_sb, 1)
            elif stage in ("u0", "u1"):
                r = int(stage[1])
                act.wait_ge(u_ready, 1)
                act.sem_inc(u_ready, -1)
                act.wait_ge(sig_used, 1)
                act.sem_inc(sig_used, -1)
                nc.scalar.activation(sig[r][:], misc[0][:, 0:3 * P], ACT.Exp, scale=-1.0)
                nc.scalar.activation(up[r][:], misc[0][:, 0:3 * P], ACT.Copy).then_inc(misc_free[0], 1)
            elif stage in ("w0", "w1"):
                r = int(stage[1])
                act.wait_ge(w_ready, 1)
                act.sem_inc(w_ready, -1)
                nc.scalar.activation(gate[:, 3 * r:3 * r + 3], misc[1][:, 0:3 * P].rearrange("p (f k) -> p f k", f=3),
                                     ACT.Copy).then_inc(misc_free[1], 1)
                act.drain().then_inc(sig_ready, 1)

        @block.scalar
        def _(act):
            def batch(parts):
                for s in range(G * KT):
                    act_step(act, s)
                    for part, stage, at in ACT_SLOT:
                        if at == s and part in parts:
                            act_ffn(act, stage)

            batch("")
            batch("A")
            with act.Fori(2, B) as b:
                batch("AB")
            for part, stage, at in ACT_SLOT:
                act_ffn(act, stage)
            for part, stage, at in ACT_SLOT:
                if part == "B":
                    act_ffn(act, stage)

        def group_end(dve, g):
            dve.drain()
            dve.wait_ge(o_ready, 1)
            dve.sem_inc(o_ready, -1)
            dve.sem_inc(group_free, 1)
            dve.sem_inc(va_free, 1)
            nc.vector.tensor_copy(o_sb[:], o_bank[g % 2][:]).then_inc(o_free, 1)
            dve.drain()
            nc.vector.transpose(den[:], o_sb[:])
            dve.drain()
            nc.vector.reciprocal(inv[:], den[:].rearrange("p (c r) -> p c r", r=32)[:, :, HD])
            dve.drain()
            nc.vector.tensor_copy(den[:].rearrange("p (c r) -> p c r", r=32), inv[:].unsqueeze(2).broadcast_to([P, S // 32, 32]))
            dve.drain()
            nc.vector.transpose(den2[:], den[:])
            dve.drain()
            if g == 0:
                dve.wait_ge(ot_free, 1)
                dve.sem_inc(ot_free, -1)
            nc.vector.tensor_tensor(o_t[:, g], o_sb[:], den2[:], ALU.mult).then_inc(ot_ready, 1)

        def square_sum(dve, src, col):
            nc.vector.scalar_tensor_tensor(out=prod[:], in0=src, scalar=1.0, in1=src, op0=ALU.mult, op1=ALU.mult,
                                           accum_out=ms[:, col:col + 1])
            dve.drain().then_inc(ms_ready, 1)

        def dve_ffn(dve, stage):
            dve.drain()
            if stage == "x1":
                dve.wait_ge(xres_in, 16)
                dve.sem_inc(xres_in, -16)
                for pr in range(2):
                    dve.wait_ge(wo_ready, 1)
                    dve.sem_inc(wo_ready, -1)
                    nc.vector.tensor_tensor(x1[:, 2 * pr:2 * pr + 2], x1[:, 2 * pr:2 * pr + 2],
                                            misc[pr][:].rearrange("p (t d) -> p t d", t=2), ALU.add
                                            ).then_inc(misc_free[pr], 1)
                dve.sem_inc(ot_free, 1)
                dve.drain()
                for t in range(QT):
                    nc.vector.bn_stats(stats[:, t], x1[:, t])
                dve.drain()
                for t in range(QT):
                    nc.vector.bn_aggr(mv[:, t], stats[:, t])
                dve.drain().then_inc(var2_ready, 1)
            elif stage == "y":
                dve.wait_ge(rstd2_ready, 1)
                dve.sem_inc(rstd2_ready, -1)
                for t in range(QT):
                    nc.vector.tensor_scalar(y[:, t], x1[:, t], mv[:, t, 0:1], rstd[:, t:t + 1], ALU.subtract, ALU.mult)
                dve.drain().then_inc(y_ready, 1)
                for t in range(QT):
                    nc.vector.scalar_tensor_tensor(out=prod[:], in0=y[:, t], scalar=1.0, in1=wr_b[:], op0=ALU.mult,
                                                   op1=ALU.mult, accum_out=score[:, t:t + 1])
                    dve.drain()
                dve.drain().then_inc(score_ready, 1)
            elif stage == "rank":
                dve.wait_ge(all_ready, 1)
                dve.sem_inc(all_ready, -1)
                for t in range(QT):
                    nc.vector.scalar_tensor_tensor(out=ties[:], in0=all_scores[:], scalar=score[:, t:t + 1],
                                                   in1=before[:, t], op0=ALU.is_equal, op1=ALU.mult)
                    dve.drain()
                    last = nc.vector.scalar_tensor_tensor(out=ties[:], in0=all_scores[:], scalar=score[:, t:t + 1],
                                                          in1=ties[:], op0=ALU.is_gt, op1=ALU.add,
                                                          accum_out=rank[:, t:t + 1])
                    dve.drain()
                    nc.vector.tensor_scalar(sel[:, t], iota_r[:], rank[:, t:t + 1], None, ALU.is_equal)
                dve.drain().then_inc(sel_ready, 1)
            elif stage == "hid":
                dve.wait_ge(gather_ready, 1)
                dve.sem_inc(gather_ready, -1)
                nc.vector.tensor_copy(x_sel[:], misc[1][:, 0:D]).then_inc(misc_free[1], 1)
                dve.drain()
                square_sum(dve, x_sel[:], 0)
                dve.wait_ge(rms_ready, 1)
                dve.sem_inc(rms_ready, -1)
                nc.vector.scalar_tensor_tensor(out=hid[:], in0=x_sel[:], scalar=ms[:, 0:1], in1=g1_b[:],
                                               op0=ALU.mult, op1=ALU.mult).then_inc(hid_ready, 1)
            elif stage == "k_block":
                dve.wait_ge(k_ready, 1)
                dve.sem_inc(k_ready, -1)
                for m in range(M2):
                    src = misc[0][:, m * CAP:(m + 1) * CAP]
                    last = nc.vector.tensor_tensor(k_block[:, m], src.unsqueeze(1).broadcast_to([P, H8, CAP]),
                                                   block_of[:].unsqueeze(2).broadcast_to([P, H8, CAP]), ALU.mult)
                last.then_inc(misc_free[0], 1)
                dve.drain().then_inc(kb_ready, 1)
            elif stage == "softmax":
                for n in range(4):
                    dve.wait_ge(sc_ready, 1)
                    dve.sem_inc(sc_ready, -1)
                    nc.vector.tensor_tensor(sc[:, 4 * n:4 * n + 4], misc[n % 2][:].rearrange("p (h k) -> p h k", h=4),
                                            causal[:].unsqueeze(1).broadcast_to([P, 4, CAP]), ALU.add
                                            ).then_inc(misc_free[n % 2], 1)
                dve.drain()
                nc.vector.tensor_reduce(s_max[:], sc[:], op=ALU.max, axis=AX.X)
                dve.drain()
                nc.vector.tensor_tensor(sc[:], sc[:], s_max[:].unsqueeze(2).broadcast_to([P, H, CAP]), ALU.subtract
                                        ).then_inc(scm_ready, 1)
            elif stage == "sum":
                dve.wait_ge(den_ready, 1)
                dve.sem_inc(den_ready, -1)
                nc.vector.tensor_reduce(s_max[:], sc[:], op=ALU.add, axis=AX.X)
                dve.drain()
                nc.vector.reciprocal(s_den[:], s_max[:])
                nc.vector.tensor_copy(x_keep[:], x_sel[:])
            elif stage == "os":
                dve.wait_ge(pv_ready, 1)
                dve.sem_inc(pv_ready, -1)
                nc.vector.tensor_tensor(o_s[:].rearrange("p (h d) -> p h d", h=H),
                                        misc[0][:, 0:D].rearrange("p (h d) -> p h d", h=H),
                                        s_den[:].unsqueeze(2).broadcast_to([P, H, HD]), ALU.mult
                                        ).then_inc(misc_free[0], 1)
                dve.drain().then_inc(os_ready, 1)
            elif stage == "hid2":
                dve.wait_ge(att_ready, 1)
                dve.sem_inc(att_ready, -1)
                nc.vector.tensor_copy(att[:], misc[0][:, 0:D]).then_inc(misc_free[0], 1)
                dve.drain()
                nc.vector.tensor_tensor(hid2[:], x_keep[:], att[:], ALU.add)
                dve.drain()
                square_sum(dve, hid2[:], 2)
                dve.wait_ge(rms_ready, 1)
                dve.sem_inc(rms_ready, -1)
                nc.vector.scalar_tensor_tensor(out=hid2[:], in0=hid2[:], scalar=ms[:, 2:3], in1=g2_b[:],
                                               op0=ALU.mult, op1=ALU.mult).then_inc(hid2_ready, 1)
            elif stage in ("gate0", "gate1"):
                r = int(stage[4])
                dve.wait_ge(sig_ready, 1)
                dve.sem_inc(sig_ready, -1)
                nc.vector.tensor_scalar(sig[r][:], sig[r][:], 1.0, None, ALU.add)
                half = gate[:, 3 * r:3 * r + 3]
                nc.vector.tensor_tensor(half, half, up[r][:].rearrange("p (f k) -> p f k", f=3), ALU.mult)
                dve.drain()
                nc.vector.reciprocal(sig[r][:], sig[r][:])
                dve.drain()
                nc.vector.tensor_tensor(half, half, sig[r][:].rearrange("p (f k) -> p f k", f=3), ALU.mult
                                        ).then_inc(gate_ready, 1)
                dve.drain().then_inc(sig_used, 1)
            elif stage == "delta":
                dve.wait_ge(ff_ready, 1)
                dve.sem_inc(ff_ready, -1)
                nc.vector.tensor_tensor(delta[:], att[:], misc[0][:, 0:D], ALU.add).then_inc(misc_free[0], 1)
                dve.drain().then_inc(delta_ready, 1)
            elif stage == "base":
                dve.wait_ge(base_ready, 1)
                dve.sem_inc(base_ready, -1)
            elif stage == "out":
                dve.wait_ge(out_stored, 16)
                dve.sem_inc(out_stored, -16)
                for pr in (1, 0):
                    dve.wait_ge(scat_ready, 1)
                    dve.sem_inc(scat_ready, -1)
                    nc.vector.tensor_tensor(out_sb[:, 2 * pr:2 * pr + 2], base[:, 2 * pr:2 * pr + 2],
                                            misc[pr][:].rearrange("p (t d) -> p t d", t=2), ALU.add
                                            ).then_inc(misc_free[pr], 1)
                dve.drain().then_inc(out_ready, 1)
                dve.sem_inc(base_free, 1)

        @block.vector
        def _(dve):
            nc.vector.tensor_scalar(lower[:], ident[:], -BIG, None, ALU.mult)
            dve.sem_inc(maskfix_free, 1)
            dve.sem_inc(group_free, G)
            dve.sem_inc(va_free, G)
            dve.sem_inc(v_in_free, 2)
            dve.sem_inc(o_free, 2)
            dve.sem_inc(ot_free, 1)
            dve.sem_inc(misc_free[0], 1)
            dve.sem_inc(misc_free[1], 1)
            dve.sem_inc(xres_free, 1)
            dve.sem_inc(sig_used, 2)
            dve.sem_inc(base_free, 1)
            dve.sem_inc(out_stored, 16)
            dve.drain().then_inc(lower_set, 1)
            def batch(parts, attention=True):
                for part, stage in DVE_ORDER:
                    if part == "group":
                        if attention:
                            group_end(dve, stage)
                    elif part in parts:
                        dve_ffn(dve, stage)

            batch("")
            dve.wait_ge(consts, 1)
            dve.sem_inc(consts, -1)
            batch("A")
            with dve.Fori(2, B) as b:
                batch("AB")
            batch("AB", attention=False)
            batch("B", attention=False)

        def scores(pe, s, general):
            g, t = s // KT, s % KT
            if t == 0:
                pe.wait_ge(group_in[g], 32)
                pe.sem_inc(group_in[g], -32)
            for pr in range(2):
                if s > 0:
                    pe.wait_ge(s_read[pr], 1)
                    pe.sem_inc(s_read[pr], -1)
                for e in range(2):
                    j = 2 * pr + e
                    last = nc.tensor.matmul(pair_bank[pr][:, e], ks[0:ROWS, g, j, t * P:(t + 1) * P],
                                            qs[0:ROWS, g, j, :], start=True, stop=not general)
                    if general:
                        for n in range(QT):
                            last = nc.tensor.matmul(pair_bank[pr][:, e, n * P:(n + 1) * P],
                                                    mask_fix[:, n, t * P:(t + 1) * P], lower[:],
                                                    start=False, stop=(n == QT - 1))
                last.then_inc(s_ready[pr], 1)

        def values(pe, s):
            g, t = s // KT, s % KT
            if t == 0:
                pe.wait_ge(va_ready, 1)
                pe.sem_inc(va_ready, -1)
                pe.wait_ge(o_free, 1)
                pe.sem_inc(o_free, -1)
            for j in range(HG):
                last = nc.tensor.matmul(o_bank[g % 2][32 * j:32 * j + 32], va[:, t, g, j], probs[s % 2][:, j],
                                        start=(t == 0), stop=(t == KT - 1))
            if t == KT - 1:
                last.then_inc(o_ready, 1)

        def pe_attention(pe, parts, general):
            if general:
                pe.wait_ge(maskfix_in, 16)
                pe.sem_inc(maskfix_in, -16)
            for s in range(G * KT):
                scores(pe, s, general)
                if s > 0:
                    values(pe, s - 1)
                for part, stage, at in PE_SLOT:
                    if at == s and part in parts:
                        pe_ffn(pe, stage)
            pe.wait_ge(s_read[0], 1)
            pe.sem_inc(s_read[0], -1)
            pe.wait_ge(s_read[1], 1)
            pe.sem_inc(s_read[1], -1)
            if general:
                pe.sem_inc(maskfix_free, 1)
            values(pe, G * KT - 1)

        def transposes(dst, srcs):
            for n, src in enumerate(srcs):
                last = nc.tensor.transpose(dst[:, n * P:(n + 1) * P], src, ident[:])
            return last

        def product(dst, pairs):
            for n, (a, c) in enumerate(pairs):
                last = nc.tensor.matmul(dst, a, c, start=(n == 0), stop=(n == len(pairs) - 1))
            return last

        def pe_ffn(pe, stage):
            if stage.startswith("wo") and stage != "wout":
                t = int(stage[2])
                pr, e = t // 2, t % 2
                if t == 0:
                    pe.wait_ge(ot_ready, G)
                    pe.sem_inc(ot_ready, -G)
                if e == 0:
                    pe.wait_ge(misc_free[pr], 1)
                    pe.sem_inc(misc_free[pr], -1)
                last = product(misc[pr][:, e * D:(e + 1) * D], [(o_t[:, g, t * P:(t + 1) * P], wo[:, g]) for g in range(G)])
                if e == 1:
                    last.then_inc(wo_ready, 1)
            elif stage == "spread":
                pe.wait_ge(score_ready, 1)
                pe.sem_inc(score_ready, -1)
                pe.wait_ge(misc_free[1], 1)
                pe.sem_inc(misc_free[1], -1)
                transposes(misc[1], [score[:, t:t + 1].broadcast_to([P, P]) for t in range(QT)]).then_inc(spread_ready, 1)
            elif stage == "gather":
                pe.wait_ge(sel_ready, 1)
                pe.sem_inc(sel_ready, -1)
                pe.wait_ge(misc_free[1], 1)
                pe.sem_inc(misc_free[1], -1)
                product(misc[1][:, 0:D], [(sel[:, t], y[:, t]) for t in range(QT)]).then_inc(gather_ready, 1)
            elif stage == "selT":
                pe.wait_ge(misc_free[1], 1)
                pe.sem_inc(misc_free[1], -1)
                transposes(misc[1], [sel[:, t] for t in range(QT)]).then_inc(selT_ready, 1)
            elif stage == "hid2T":
                pe.wait_ge(hid2_ready, 1)
                pe.sem_inc(hid2_ready, -1)
                pe.wait_ge(misc_free[1], 1)
                pe.sem_inc(misc_free[1], -1)
                transposes(misc[1], [hid2[:, c * P:(c + 1) * P] for c in range(KC)]).then_inc(hid2T_ready, 1)
            elif stage == "hidT":
                pe.wait_ge(hid_ready, 1)
                pe.sem_inc(hid_ready, -1)
                pe.wait_ge(misc_free[1], 1)
                pe.sem_inc(misc_free[1], -1)
                transposes(misc[1], [hid[:, c * P:(c + 1) * P] for c in range(KC)]).then_inc(hidT_ready, 1)
            elif stage == "qv":
                pe.wait_ge(hidT_sb, 1)
                pe.sem_inc(hidT_sb, -1)
                pe.wait_ge(misc_free[1], 1)
                pe.sem_inc(misc_free[1], -1)
                for n in range(2):
                    product(misc[1][:, n * CAP:(n + 1) * CAP],
                            [(wqkv[:, c, n * P:(n + 1) * P], hid_t[:, c]) for c in range(KC)])
                product(misc[1][:, D:2 * D], [(hid_t[:, c], wqkv[:, c, 2 * D:3 * D]) for c in range(KC)]
                        ).then_inc(qv_ready, 1)
            elif stage == "k":
                pe.wait_ge(misc_free[0], 1)
                pe.sem_inc(misc_free[0], -1)
                for n in range(2):
                    last = product(misc[0][:, n * CAP:(n + 1) * CAP],
                                   [(wqkv[:, c, D + n * P:D + (n + 1) * P], hid_t[:, c]) for c in range(KC)])
                last.then_inc(k_ready, 1)
            elif stage in ("sc0", "sc1"):
                m = int(stage[2])
                if m == 0:
                    pe.wait_ge(kb_ready, 1)
                    pe.sem_inc(kb_ready, -1)
                    pe.wait_ge(qv_sb, 1)
                    pe.sem_inc(qv_sb, -1)
                for e in range(2):
                    pe.wait_ge(misc_free[e], 1)
                    pe.sem_inc(misc_free[e], -1)
                    nc.tensor.matmul(misc[e][:], q_t[:, m], k_block[:, m, 4 * e:4 * e + 4, :], start=True, stop=True
                                     ).then_inc(sc_ready, 1)
            elif stage in ("pT0", "pT1"):
                m = int(stage[2])
                if m == 0:
                    pe.wait_ge(p_ready, 1)
                    pe.sem_inc(p_ready, -1)
                for e in range(2):
                    pe.wait_ge(misc_free[e], 1)
                    pe.sem_inc(misc_free[e], -1)
                    h0 = 8 * m + 4 * e
                    transposes(misc[e], [sc[:, h] for h in range(h0, h0 + 4)]).then_inc(pT_ready, 1)
            elif stage in ("pv0", "pv1"):
                m = int(stage[2])
                if m == 0:
                    pe.wait_ge(pT_sb, 1)
                    pe.sem_inc(pT_sb, -1)
                    pe.wait_ge(misc_free[0], 1)
                    pe.sem_inc(misc_free[0], -1)
                for h in range(H8 * m, H8 * m + H8):
                    last = nc.tensor.matmul(misc[0][:, h * HD:(h + 1) * HD], p_t[:, h], v_s[:, h * HD:(h + 1) * HD],
                                            start=True, stop=True)
                if m == 1:
                    last.then_inc(pv_ready, 1)
            elif stage == "osT":
                pe.wait_ge(os_ready, 1)
                pe.sem_inc(os_ready, -1)
                pe.wait_ge(misc_free[0], 1)
                pe.sem_inc(misc_free[0], -1)
                transposes(misc[0], [o_s[:, c * P:(c + 1) * P] for c in range(KC)]).then_inc(osT_ready, 1)
            elif stage == "wout":
                pe.wait_ge(osT_sb, 1)
                pe.sem_inc(osT_sb, -1)
                pe.wait_ge(misc_free[0], 1)
                pe.sem_inc(misc_free[0], -1)
                product(misc[0][:, 0:D], [(os_t[:, c], wout[:, c]) for c in range(KC)]).then_inc(att_ready, 1)
            elif stage in ("u0", "u1", "w0", "w1"):
                r = int(stage[1])
                if stage == "u0":
                    pe.wait_ge(hid2T_sb, 1)
                    pe.sem_inc(hid2T_sb, -1)
                w, i, ready = (w1, 0, u_ready) if stage[0] == "u" else (w2, 1, w_ready)
                pe.wait_ge(misc_free[i], 1)
                pe.sem_inc(misc_free[i], -1)
                for f in range(3):
                    last = product(misc[i][:, f * P:(f + 1) * P],
                                   [(w[:, c, (3 * r + f) * P:(3 * r + f + 1) * P], hid_t[:, c]) for c in range(KC)])
                last.then_inc(ready, 1)
            elif stage in ("down0", "down1"):
                r = int(stage[4])
                pe.wait_ge(gate_ready, 1)
                pe.sem_inc(gate_ready, -1)
                if r == 0:
                    pe.wait_ge(misc_free[0], 1)
                    pe.sem_inc(misc_free[0], -1)
                for f in range(3 * r, 3 * r + 3):
                    last = nc.tensor.matmul(misc[0][:, 0:D], gate[:, f], w3[:, f], start=(f == 0), stop=(f == FT - 1))
                if r == 1:
                    last.then_inc(ff_ready, 1)
            elif stage in ("scat1", "scat0"):
                pr = int(stage[4])
                if pr == 1:
                    pe.wait_ge(delta_ready, 1)
                    pe.sem_inc(delta_ready, -1)
                    pe.wait_ge(selT_sb, 1)
                    pe.sem_inc(selT_sb, -1)
                pe.wait_ge(misc_free[pr], 1)
                pe.sem_inc(misc_free[pr], -1)
                for e in range(2):
                    t = 2 * pr + e
                    last = nc.tensor.matmul(misc[pr][:, e * D:(e + 1) * D], sel_t[:, t * P:(t + 1) * P], delta[:],
                                            start=True, stop=True)
                last.then_inc(scat_ready, 1)

        @block.tensor
        def _(pe):
            in_general = pe.value_load(flags_i[0:1, 0:1], min_val=0, max_val=1)
            pe.wait_ge(rows_set, 16)
            pe.wait_ge(lower_set, 1)
            pe.sem_inc(lower_set, -1)

            def batches(general):
                pe_attention(pe, "", general)
                pe.wait_ge(w_in, 16 * N_W)
                pe_attention(pe, "A", general)
                with pe.Fori(2, B) as b:
                    pe_attention(pe, "AB", general)

            with pe.If(in_general == 1):
                batches(True)
            with pe.Else():
                batches(False)
            for part, stage, at in PE_SLOT:
                pe_ffn(pe, stage)
            for part, stage, at in PE_SLOT:
                if part == "B":
                    pe_ffn(pe, stage)


PE_SLOT = [("A", "wo0", 2), ("A", "wo1", 3), ("A", "wo2", 4), ("A", "wo3", 5), ("B", "pv0", 6), ("B", "pv1", 7),
           ("B", "selT", 8), ("A", "spread", 9), ("B", "osT", 9), ("A", "gather", 13), ("B", "wout", 14),
           ("A", "hidT", 15), ("A", "qv", 16), ("A", "k", 17), ("B", "hid2T", 18), ("B", "u0", 19), ("B", "w0", 20),
           ("B", "u1", 21), ("B", "w1", 22), ("A", "sc0", 23), ("A", "sc1", 24), ("B", "down0", 25), ("B", "down1", 26),
           ("B", "scat1", 28), ("B", "scat0", 29), ("A", "pT0", 30), ("A", "pT1", 31)]
ACT_SLOT = [("B", "selT", 8), ("A", "spread", 9), ("B", "osT", 9), ("A", "hidT", 15), ("A", "qv", 17),
            ("B", "hid2T", 18), ("B", "u0", 19), ("B", "w0", 20), ("B", "u1", 21), ("B", "w1", 22), ("A", "exp", 27),
            ("A", "pT0", 30), ("A", "pT1", 30), ("A", "pT2", 31), ("A", "pT3", 31)]
DVE_ORDER = [("B", "base"), ("A", "x1"), ("A", "y"), ("B", "os"), ("A", "rank"), ("A", "hid"), ("group", 0),
             ("B", "hid2"), ("A", "k_block"), ("group", 1), ("B", "gate0"), ("B", "gate1"), ("A", "softmax"),
             ("B", "delta"), ("group", 2), ("B", "out"), ("A", "sum"), ("group", 3)]


def kernel(**inputs):
    import numpy as np
    import concourse.bacc as bacc
    from concourse import mybir
    from concourse.bass_utils import run_bass_kernel_spmd

    c = np.ascontiguousarray
    a = {k: np.asarray(v) for k, v in inputs.items()}

    def head_minor(w):
        return c(w.reshape(M2, H8, HD, D).transpose(0, 2, 1, 3).reshape(D, D).T)

    arrays = {
        "x": c(a["x"]),
        "ctxT": c(a["ctx_1024"].transpose(0, 2, 1)),
        "mask": c(a["mask_BxSxS2_bk0"]),
        "wqT": head_minor(a["L0_xattn_w_q"]),
        "wkT": head_minor(a["L0_xattn_w_k"]),
        "wvT": c(a["L0_xattn_w_v"].T),
        "woT": c(a["L0_xattn_w_o"].T),
        "w_router": c(a["L0_ffn_w_router"]),
        "wqkvT": c(a["L0_ffn_W_qkv"].T),
        "woutT": c(a["L0_ffn_W_out"].T),
        "g1": c(a["L0_ffn_g1"]),
        "g2": c(a["L0_ffn_g2"]),
        "w1T": c(a["L0_ffn_W1"].T),
        "w2T": c(a["L0_ffn_W2"].T),
        "w3T": c(a["L0_ffn_W3"].T),
    }
    nc = bacc.Bacc("TRN2", target_bir_lowering=False, num_devices=1)
    io = {n: nc.dram_tensor(f"in_{n}", v.shape, mybir.dt.from_np(v.dtype), kind="ExternalInput").ap()
          for n, v in arrays.items()}
    out = nc.dram_tensor("out_dram", (B, S, D), mybir.dt.float32, kind="ExternalOutput").ap()
    program(nc, io, out)
    r = run_bass_kernel_spmd(nc, [{f"in_{n}": v for n, v in arrays.items()}], core_ids=[0])
    return r.results[0]["out_dram"]
```

```python
from contextlib import ExitStack

import concourse.bass as bass
from concourse import mybir

P = 128
B = 8
S = 512
SK = 1024
D = 256
H = 16
HD = D // H
KC = D // P
QT = S // P
KT = SK // P
M2 = 2
H8 = H // M2
G = 4
HG = H // G
NPAIR = 6
K_PART = [0, 0, 0, 1, 1, 2]
Q_PART = [0, 1, 2, 0, 1, 0]
K_RUNS = [(0, 0, 3, 1), (1, 3, 2, 1), (2, 5, 1, 1)]
Q_RUNS = [(0, 0, 2, 3), (0, 5, 1, 1), (1, 1, 2, 3), (2, 2, 1, 1)]
N_RUNS = len(K_RUNS) + len(Q_RUNS)
ROW_MASK = NPAIR * HD
ROW_MAX = ROW_MASK + 1
ROWS = ROW_MAX + 3
CAP = 128
DFF = 682
FT = 6
BIG = 2.0 ** 30
SAFE = 60.0
LN_EPS = 1e-5
RMS_EPS = 1e-6

F32 = mybir.dt.float32
BF16 = mybir.dt.bfloat16
U8 = mybir.dt.uint8
I32 = mybir.dt.int32
ALU = mybir.AluOpType
ACT = mybir.ActivationFunctionType
AX = mybir.AxisListType




def program(nc, io, out):
    dram = lambda name, shape, dt: nc.dram_tensor(name, shape, dt, kind="Internal").ap()
    ks_dram = dram("ks_scratch", (B, M2, ROWS, H8, SK), BF16)
    qs_dram = dram("qs_scratch", (B, M2, ROWS, H8, S), BF16)
    v_dram = dram("v_scratch", (B, SK, D), F32)
    mask_dram = dram("mask_scratch", (B, S, SK), BF16)

    with ExitStack() as top:
        sb = lambda name, shape, dt=F32: top.enter_context(nc.sbuf_tensor(name, shape, dt))
        bank = [top.enter_context(nc.psum_tensor(f"bank{i}", [P, 512], F32)) for i in range(4, 8)]
        pair_bank = [top.enter_context(nc.psum_tensor(f"pair_bank{i}", [P, 2, 512], F32)) for i in range(2)]
        banks8 = [pair_bank[0][:, 0], pair_bank[0][:, 1], pair_bank[1][:, 0], pair_bank[1][:, 1]] + [b[:] for b in bank]
        ident = sb("ident", [P, P])
        flags = sb("flags", [1, 2])
        flags_i = sb("flags_i", [1, 1], I32)
        ones3 = sb("ones3", [ROWS - ROW_MAX, SK // 2], BF16)
        project_phase(nc, top, io, ks_dram, qs_dram, v_dram, banks8, ident, flags, flags_i, ones3)
        maximum_phase(nc, top, io, ks_dram, qs_dram, mask_dram, pair_bank, bank, ident, flags_i)
        main_phase(nc, top, io, out, ks_dram, qs_dram, v_dram, mask_dram, pair_bank, bank, ident, flags_i, ones3)


def project_phase(nc, top, io, ks_dram, qs_dram, v_dram, banks, ident, flags, flags_i, ones3):
    with ExitStack() as ctx:
        sb = lambda name, shape, dt=F32: ctx.enter_context(nc.sbuf_tensor(name, shape, dt))
        sem = lambda name: top.enter_context(nc.semaphore(name))
        wq, wk, wv = (sb(n, [P, KC, D]) for n in ("wq_sb", "wk_sb", "wv_sb"))
        x_sb = [sb(f"x_in{i}", [P, QT, D]) for i in range(2)]
        ctx_sb = [sb(f"ctx_in{i}", [P, KC, SK]) for i in range(2)]
        mask_u8 = [sb(f"mask_in{i}", [P, QT, SK], U8) for i in range(2)]
        mask_bf = sb("mask_bf", [P, QT, SK], BF16)
        masked = sb("masked", [P, QT])
        ones_bf = sb("ones_bf", [P, 1], BF16)
        block_of = sb("block_of", [P, H8])
        stats = sb("stats", [P, QT, 6])
        mv = sb("mv", [P, QT, 2])
        veps = sb("veps", [P, QT])
        neg_half = sb("neg_half", [P, QT])
        rstd = sb("rstd", [P, QT])
        rn = sb("rn", [P, QT])
        has_key = sb("has_key", [P, QT])
        zeros_bf = sb("zeros_bf", [3, H8 * S], BF16)
        xn = sb("xn", [P, QT, D])
        xnT = sb("xnT", [P, KC, S])
        nf_row = sb("nf_row", [1, S], BF16)
        parts_q = [[sb(f"parts_q{m}_{i}", [P, 3, S], BF16) for m in range(M2)] for i in range(2)]
        parts_k = [[sb(f"parts_k{m}_{i}", [P, 3, SK], BF16) for m in range(M2)] for i in range(2)]
        rest = [sb(f"rest{i}", [P, 512]) for i in range(3)]
        v_sb = sb("v_sb", [P, KT, D])
        absmax = sb("absmax", [P, 6])
        ab = sb("ab", [P, B, M2])
        bound = sb("bound", [B * M2, 1])
        bound1 = sb("bound1", [1, 2])
        c_row = sb("c_row", [1, SK])
        c_tmp = sb("c_tmp", [1, SK])
        k_only = sb("k_only", [1, 2])
        k_row = sb("k_row", [1, SK], BF16)

        wk_in, wv_in, wq_in, const_ready = sem("wk_in"), sem("wv_in"), sem("wq_in"), sem("const_ready")
        x_in = [sem(f"x_in_s{i}") for i in range(2)]
        ctx_in = [sem(f"ctx_in_s{i}") for i in range(2)]
        mask_in = [sem(f"mask_in_s{i}") for i in range(2)]
        x_free, ctx_free, mask_free = sem("x_free"), sem("ctx_free"), sem("mask_free")
        var_ready, rstd_ready, masked_ready = sem("var_ready"), sem("rstd_ready"), sem("masked_ready")
        xn_ready, nf_t_ready = sem("xn_ready"), sem("nf_t_ready")
        xT_ready, xT_sb_ready = sem("xT_ready"), sem("xT_sb_ready")
        qk_ready, head_part_ready = sem("qk_ready"), sem("head_part_ready")
        rest_ready, mid_ready, rest_used = sem("rest_ready"), sem("mid_ready"), sem("rest_used")
        k_parts_ready, q_parts_ready = sem("k_parts_ready"), sem("q_parts_ready")
        parts_stored = [sem(f"parts_stored{i}") for i in range(2)]
        v_ready, v_sb_ready, v_stored = sem("v_ready"), sem("v_sb_ready"), sem("v_stored")
        c_ready, c_sb_ready = sem("c_ready"), sem("c_sb_ready")
        rows_ready, rows_stored = sem("rows_ready"), sem("rows_stored")
        ab_ready, bound_ready, bound_sb, bound_t_ready = (
            sem("ab_ready"), sem("bound_ready"), sem("bound_sb"), sem("bound_t_ready"))
        maskbf_free = sem("maskbf_free")
        bank_free = [sem(f"bank_free{i}") for i in range(8)]
        zeros_ready, zeros_stored = sem("zeros_ready"), sem("zeros_stored")

        USE = {"k00": 0, "k01": 1, "k10": 2, "k11": 3, "v0": 4, "v1": 5, "v2": 6, "v3": 7,
               "xT0": 0, "xT1": 1, "nf": 2, "c0": 3, "c1": 4, "q0": 5, "q1": 6}
        qk_tiles = [("k", 0, 0), ("k", 0, 1), ("k", 1, 0), ("k", 1, 1), ("q", 0, 0), ("q", 1, 0)]
        tile_bank = lambda kind, m, half: banks[USE[f"q{m}" if kind == "q" else f"k{m}{half}"]]
        tile_free = lambda kind, m, half: bank_free[USE[f"q{m}" if kind == "q" else f"k{m}{half}"]]

        def part(i, kind, m, half, j):
            return parts_q[i][m][:, j, :] if kind == "q" else parts_k[i][m][:, j, half * 512:(half + 1) * 512]

        block = ctx.enter_context(nc.Block())

        @block.sync
        def _(sp):
            def weights(w, src, s):
                sp.dma_start(w[:], src.rearrange("(c p) n -> p c n", p=P)).then_inc(s, 16)

            def load(b, i):
                sp.wait_ge(ctx_free, 1)
                sp.sem_inc(ctx_free, -1)
                sp.dma_start(ctx_sb[i][:], io["ctxT"][b].rearrange("(c p) k -> p c k", p=P)).then_inc(ctx_in[i], 16)
                sp.wait_ge(x_free, 1)
                sp.sem_inc(x_free, -1)
                sp.dma_start(x_sb[i][:], io["x"][b].rearrange("(t p) d -> p t d", p=P)).then_inc(x_in[i], 16)
                sp.wait_ge(mask_free, 1)
                sp.sem_inc(mask_free, -1)
                sp.dma_start(mask_u8[i][:], io["mask"][b].rearrange("(t p) k -> p t k", p=P)).then_inc(mask_in[i], 16)

            def store_parts(b, i, m, parts, dst, runs):
                blocks = dst[b, m, 0:ROW_MASK].rearrange("(r d) h k -> (d h) r k", d=HD)
                for j, r0, n, step in runs:
                    src = parts[:, j, :].unsqueeze(1)
                    sp.dma_start(blocks[:, r0:r0 + (n - 1) * step + 1:step, :],
                                 src.broadcast_to([P, n, src.shape[2]])).then_inc(parts_stored[i], 16)

            def store(b, i):
                for m in range(M2):
                    sp.wait_ge(k_parts_ready, 2)
                    sp.sem_inc(k_parts_ready, -2)
                    store_parts(b, i, m, parts_k[i][m], ks_dram, K_RUNS)
                sp.wait_ge(v_sb_ready, 1)
                sp.sem_inc(v_sb_ready, -1)
                sp.dma_start(v_dram[b].rearrange("(t p) n -> p t n", p=P), v_sb[:]).then_inc(v_stored, 16)
                for m in range(M2):
                    sp.wait_ge(q_parts_ready, 1)
                    sp.sem_inc(q_parts_ready, -1)
                    store_parts(b, i, m, parts_q[i][m], qs_dram, Q_RUNS)
                sp.wait_ge(rows_ready, 1)
                sp.sem_inc(rows_ready, -1)
                for m in range(M2):
                    sp.dma_start(ks_dram[b, m, ROW_MASK], k_row[0:1, :].unsqueeze(1).broadcast_to([1, H8, SK])
                                 ).then_inc(rows_stored, 16)
                    sp.dma_start(qs_dram[b, m, ROW_MASK], nf_row[0:1, :].unsqueeze(1).broadcast_to([1, H8, S])
                                 ).then_inc(rows_stored, 16)

            weights(wk, io["wkT"], wk_in)
            load(0, 0)
            weights(wv, io["wvT"], wv_in)
            weights(wq, io["wqT"], wq_in)
            sp.wait_ge(zeros_ready, 1)
            sp.sem_inc(zeros_ready, -1)
            sp.dma_start(qs_dram[:, :, ROW_MAX:ROWS].rearrange("b m r h k -> r (b m) (h k)"),
                         zeros_bf[:].unsqueeze(1).broadcast_to([ROWS - ROW_MAX, B * M2, H8 * S])).then_inc(zeros_stored, 16)
            with sp.Fori(0, B - 2, 2) as b:
                for i in range(2):
                    load(b + i + 1, 1 - i)
                    store(b + i, i)
            load(B - 1, 1)
            store(B - 2, 0)
            store(B - 1, 1)
            sp.wait_ge(zeros_stored, 16)

        @block.gpsimd
        def _(pool):
            nc.gpsimd.memset(ident[:], 0.0)
            nc.gpsimd.memset(ones_bf[:], 1.0)
            nc.gpsimd.memset(neg_half[:], -0.5)
            nc.gpsimd.memset(block_of[:], 0.0)
            nc.gpsimd.memset(flags[:], 0.0)
            pool.drain()
            nc.gpsimd.affine_select(out=ident[:], in_=ident[:], compare_op=ALU.not_equal, fill=1.0, base=0,
                                    pattern=[[-1, P]], channel_multiplier=1)
            for d in range(HD):
                last = nc.gpsimd.affine_select(out=block_of[:], in_=block_of[:], compare_op=ALU.not_equal, fill=1.0,
                                               base=-H8 * d, pattern=[[-1, H8]], channel_multiplier=1)
                pool.drain()
            pool.drain().then_inc(const_ready, 1)
            nc.gpsimd.memset(zeros_bf[:], 0.0).then_inc(zeros_ready, 1)
            nc.gpsimd.memset(ones3[:], 1.0)
            with pool.Fori(0, B // 2) as bb:
                for i in range(2):
                    pool.wait_ge(var_ready, 1)
                    pool.sem_inc(var_ready, -1)
                    nc.gpsimd.tensor_scalar(veps[:], mv[:, :, 1], LN_EPS, None, ALU.add)
                    pool.drain()
                    nc.gpsimd.tensor_tensor(rstd[:], veps[:], neg_half[:], ALU.pow).then_inc(rstd_ready, 1)
                    for n, (kind, m, half) in enumerate(qk_tiles):
                        pool.wait_ge(mid_ready, 1)
                        pool.sem_inc(mid_ready, -1)
                        nc.gpsimd.tensor_tensor(part(i, kind, m, half, 2), rest[n % 3][:], part(i, kind, m, half, 1),
                                                ALU.subtract).then_inc(rest_used, 1)
                        pool.drain().then_inc(k_parts_ready if kind == "k" else q_parts_ready, 1)

        @block.scalar
        def _(act):
            with act.Fori(0, B // 2) as bb:
                for i in range(2):
                    def head_part(n):
                        kind, m, half = qk_tiles[n]
                        act.wait_ge(qk_ready, 1)
                        act.sem_inc(qk_ready, -1)
                        nc.scalar.activation(part(i, kind, m, half, 0), tile_bank(kind, m, half), ACT.Copy
                                             ).then_inc(head_part_ready, 1)

                    def middle_part(n):
                        kind, m, half = qk_tiles[n]
                        act.wait_ge(rest_ready, 1)
                        act.sem_inc(rest_ready, -1)
                        nc.scalar.activation(part(i, kind, m, half, 1), rest[n % 3][:], ACT.Copy).then_inc(mid_ready, 1)

                    def mask_sum(t):
                        nc.scalar.activation(mask_bf[:, t], mask_u8[i][:, t], ACT.Copy, accum_out=masked[:, t:t + 1])

                    act.wait_ge(mask_in[i], 16)
                    act.sem_inc(mask_in[i], -16)
                    act.wait_ge(maskbf_free, 1)
                    act.sem_inc(maskbf_free, -1)
                    for t in range(QT):
                        mask_sum(t)
                    act.drain().then_inc(mask_free, 1)
                    act.drain().then_inc(masked_ready, 1)
                    act.wait_ge(parts_stored[i], 2 * 16 * N_RUNS)
                    act.sem_inc(parts_stored[i], -2 * 16 * N_RUNS)
                    head_part(0)
                    head_part(1)
                    middle_part(0)
                    head_part(2)
                    head_part(3)
                    act.wait_ge(v_stored, 16)
                    act.sem_inc(v_stored, -16)

                    def v_tiles(n):
                        act.wait_ge(v_ready, 1)
                        act.sem_inc(v_ready, -1)
                        nc.scalar.activation(v_sb[:, 2 * n:2 * n + 2, :], banks[USE[f"v{n}"]], ACT.Copy
                                             ).then_inc(bank_free[USE[f"v{n}"]], 1)

                    for n in range(3):
                        middle_part(n + 1)
                        v_tiles(n)
                    v_tiles(3)
                    act.drain().then_inc(v_sb_ready, 1)
                    act.wait_ge(xT_ready, 2)
                    act.sem_inc(xT_ready, -2)
                    for kc in range(KC):
                        nc.scalar.activation(xnT[:, kc], banks[USE[f"xT{kc}"]], ACT.Copy
                                             ).then_inc(bank_free[USE[f"xT{kc}"]], 1)
                    act.drain().then_inc(xT_sb_ready, 1)
                    act.wait_ge(c_ready, 2)
                    act.sem_inc(c_ready, -2)
                    for n in range(2):
                        nc.scalar.activation(c_row[0:1, n * 512:(n + 1) * 512], banks[USE[f"c{n}"]][0:1, :], ACT.Copy
                                             ).then_inc(bank_free[USE[f"c{n}"]], 1)
                    act.drain().then_inc(c_sb_ready, 1)
                    head_part(4)
                    head_part(5)
                    middle_part(4)
                    middle_part(5)

        @block.vector
        def _(dve):
            for s in bank_free:
                dve.sem_inc(s, 1)
            dve.sem_inc(maskbf_free, 1)
            dve.sem_inc(rest_used, 3)
            dve.sem_inc(v_stored, 16)
            dve.sem_inc(rows_stored, 64)
            for i in range(2):
                dve.sem_inc(parts_stored[i], 2 * 16 * N_RUNS)
            dve.sem_inc(x_free, 2)
            dve.sem_inc(ctx_free, 2)
            dve.sem_inc(mask_free, 2)
            with dve.Fori(0, B // 2) as bb:
                for i in range(2):
                    b = bb * 2 + i
                    dve.wait_ge(x_in[i], 16)
                    dve.sem_inc(x_in[i], -16)
                    for t in range(QT):
                        nc.vector.bn_stats(stats[:, t], x_sb[i][:, t])
                    dve.drain()
                    for t in range(QT):
                        nc.vector.bn_aggr(mv[:, t], stats[:, t])
                    dve.drain().then_inc(var_ready, 1)
                    def rest_and_max(n):
                        kind, m, half = qk_tiles[n]
                        dve.wait_ge(head_part_ready, 1)
                        dve.sem_inc(head_part_ready, -1)
                        dve.wait_ge(rest_used, 1)
                        dve.sem_inc(rest_used, -1)
                        nc.vector.tensor_tensor(rest[n % 3][:], tile_bank(kind, m, half), part(i, kind, m, half, 0),
                                                ALU.subtract).then_inc(rest_ready, 1)
                        nc.vector.tensor_reduce(absmax[:, n:n + 1], tile_bank(kind, m, half), op=ALU.max, axis=AX.X,
                                                apply_absolute_value=True).then_inc(tile_free(kind, m, half), 1)

                    rest_and_max(0)
                    dve.wait_ge(masked_ready, 1)
                    dve.sem_inc(masked_ready, -1)
                    nc.vector.tensor_scalar(has_key[:], masked[:], float(SK), None, ALU.is_lt)
                    dve.wait_ge(rstd_ready, 1)
                    dve.sem_inc(rstd_ready, -1)
                    dve.drain()
                    nc.vector.tensor_tensor(rn[:], rstd[:], has_key[:], ALU.mult)
                    dve.drain()
                    for t in range(QT):
                        nc.vector.tensor_scalar(xn[:, t], x_sb[i][:, t], mv[:, t, 0:1], rn[:, t:t + 1],
                                                ALU.subtract, ALU.mult)
                    dve.drain().then_inc(xn_ready, 1)
                    dve.drain().then_inc(x_free, 1)
                    for n in range(1, 4):
                        rest_and_max(n)
                    dve.wait_ge(nf_t_ready, 1)
                    dve.sem_inc(nf_t_ready, -1)
                    dve.wait_ge(rows_stored, 64)
                    dve.sem_inc(rows_stored, -64)
                    nc.vector.tensor_copy(nf_row[0:1, :], banks[USE["nf"]][0:1, :]).then_inc(bank_free[USE["nf"]], 1)
                    dve.wait_ge(c_sb_ready, 1)
                    dve.sem_inc(c_sb_ready, -1)
                    nc.vector.scalar_tensor_tensor(out=c_tmp[:], in0=c_row[:], scalar=-float(S), in1=c_row[:],
                                                   op0=ALU.add, op1=ALU.mult)
                    dve.drain()
                    nc.vector.tensor_reduce(k_only[0:1, 0:1], c_tmp[:], op=ALU.min, axis=AX.X)
                    for n in range(4, 6):
                        rest_and_max(n)
                    dve.drain()
                    nc.vector.tensor_scalar(k_only[0:1, 1:2], k_only[0:1, 0:1], 0.0, None, ALU.is_ge)
                    dve.drain()
                    nc.vector.tensor_scalar(k_row[0:1, :], c_row[:], -BIG / S, k_only[0:1, 1:2], ALU.mult, ALU.mult)
                    nc.vector.tensor_scalar(k_only[0:1, 0:1], k_only[0:1, 1:2], -1.0, 1.0, ALU.mult, ALU.add)
                    dve.drain().then_inc(rows_ready, 1)
                    dve.wait_ge(const_ready, 1)
                    nc.vector.tensor_tensor(flags[0:1, 0:1], flags[0:1, 0:1], k_only[0:1, 0:1], ALU.max)
                    dve.drain()
                    nc.vector.tensor_tensor(absmax[:, 0:4:2], absmax[:, 0:4:2], absmax[:, 1:4:2], ALU.max)
                    dve.drain()
                    nc.vector.tensor_tensor(ab[:, b, :], absmax[:, 4:6], absmax[:, 0:4:2], ALU.mult)
            dve.drain().then_inc(ab_ready, 1)
            dve.wait_ge(bound_ready, 1)
            dve.sem_inc(bound_ready, -1)
            nc.vector.tensor_reduce(bound[:], banks[7][0:B * M2, 0:H8], op=ALU.max, axis=AX.X).then_inc(bound_sb, 1)
            dve.wait_ge(bound_t_ready, 1)
            dve.sem_inc(bound_t_ready, -1)
            nc.vector.tensor_reduce(bound1[0:1, 0:1], banks[7][0:1, 0:B * M2], op=ALU.max, axis=AX.X)
            dve.drain()
            nc.vector.tensor_scalar(bound1[0:1, 1:2], bound1[0:1, 0:1], SAFE * HD ** 0.5, None, ALU.is_le)
            dve.drain()
            nc.vector.tensor_scalar(flags[0:1, 1:2], bound1[0:1, 1:2], -1.0, 1.0, ALU.mult, ALU.add)
            dve.drain()
            nc.vector.tensor_tensor(flags_i[:], flags[0:1, 0:1], flags[0:1, 1:2], ALU.max)
            dve.wait_ge(rows_stored, 64)
            dve.wait_ge(v_stored, 16)
            for i in range(2):
                dve.wait_ge(parts_stored[i], 2 * 16 * N_RUNS)

        @block.tensor
        def _(pe):
            pe.wait_ge(wk_in, 16)

            def use_bank(name):
                pe.wait_ge(bank_free[USE[name]], 1)
                pe.sem_inc(bank_free[USE[name]], -1)
                return banks[USE[name]]

            with pe.Fori(0, B // 2) as bb:
                for i in range(2):
                    def project(kind, m, half):
                        w, src = (wq, xnT) if kind == "q" else (wk, ctx_sb[i])
                        dst = use_bank(f"q{m}" if kind == "q" else f"k{m}{half}")
                        for kc in range(KC):
                            last = nc.tensor.matmul(dst, w[:, kc, m * P:(m + 1) * P],
                                                    src[:, kc, half * 512:(half + 1) * 512],
                                                    start=(kc == 0), stop=(kc == KC - 1))
                            if kind == "q" and m == 0 and kc == 0:
                                last.then_inc(maskbf_free, 1)
                        last.then_inc(qk_ready, 1)

                    pe.wait_ge(ctx_in[i], 16)
                    pe.sem_inc(ctx_in[i], -16)
                    for tile in qk_tiles[:4]:
                        project(*tile)
                    pe.wait_ge(wv_in, 16)
                    for n in range(4):
                        dst = use_bank(f"v{n}")
                        for e in range(2):
                            kt = 2 * n + e
                            for kc in range(KC):
                                last = nc.tensor.matmul(dst[:, e * D:(e + 1) * D], ctx_sb[i][:, kc, kt * P:(kt + 1) * P],
                                                        wv[:, kc, :], start=(kc == 0), stop=(kc == KC - 1))
                        last.then_inc(v_ready, 1)
                    pe.wait_ge(xn_ready, 1)
                    pe.sem_inc(xn_ready, -1)
                    pe.wait_ge(const_ready, 1)
                    for kc in range(KC):
                        dst = use_bank(f"xT{kc}")
                        for t in range(QT):
                            last = nc.tensor.transpose(dst[:, t * P:(t + 1) * P], xn[:, t, kc * P:(kc + 1) * P], ident[:])
                            if kc == 0 and t == 0:
                                last.then_inc(ctx_free, 1)
                        last.then_inc(xT_ready, 1)
                    dst = use_bank("nf")
                    for t in range(QT):
                        last = nc.tensor.transpose(dst[0:1, t * P:(t + 1) * P], has_key[:, t:t + 1], ident[:])
                    last.then_inc(nf_t_ready, 1)
                    for n in range(2):
                        dst = use_bank(f"c{n}")
                        for t in range(QT):
                            last = nc.tensor.matmul(dst[0:1, :], ones_bf[:], mask_bf[:, t, n * 512:(n + 1) * 512],
                                                    start=(t == 0), stop=(t == QT - 1))
                        last.then_inc(c_ready, 1)
                    pe.wait_ge(xT_sb_ready, 1)
                    pe.sem_inc(xT_sb_ready, -1)
                    pe.wait_ge(wq_in, 16)
                    for tile in qk_tiles[4:]:
                        project(*tile)
            pe.wait_ge(ab_ready, 1)
            pe.sem_inc(ab_ready, -1)
            pe.wait_ge(bank_free[7], 1)
            pe.sem_inc(bank_free[7], -1)
            nc.tensor.matmul(banks[7][0:B * M2, 0:H8], ab[:].rearrange("p b m -> p (b m)"), block_of[:],
                             start=True, stop=True).then_inc(bound_ready, 1)
            pe.wait_ge(bound_sb, 1)
            pe.sem_inc(bound_sb, -1)
            nc.tensor.transpose(banks[7][0:1, 0:B * M2], bound[:], ident[0:B * M2, 0:B * M2]).then_inc(bound_t_ready, 1)


def maximum_phase(nc, top, io, ks_dram, qs_dram, mask_dram, pair_bank, bank, ident, flags_i):
    with ExitStack() as ctx:
        sb = lambda name, shape, dt=F32: ctx.enter_context(nc.sbuf_tensor(name, shape, dt))
        sem = lambda name: top.enter_context(nc.semaphore(name))
        ks = sb("max_ks", [P, H8, SK], BF16)
        qs = sb("max_qs", [P, H8, S], BF16)
        mask_u8 = sb("max_mask_in", [P, QT, SK], U8)
        mask_bf = sb("max_mask_bf", [P, QT, SK], BF16)
        mask_fix = sb("max_mask_fix", [P, QT, SK], BF16)
        masked = sb("max_masked", [P, QT])
        has_key = sb("max_has_key", [P, QT])
        lower = sb("max_lower", [P, P], BF16)
        neg_max = sb("neg_max", [P, QT, H8])
        rest = sb("max_rest", [H8, S])
        parts = sb("max_parts", [H8, 3, S], BF16)

        mask_in, mask_done, mask_stored = sem("mmask_in"), sem("mmask_done"), sem("mmask_stored")
        mask_ready, mask_used = sem("mmask_ready"), sem("mmask_used")
        qk_in, qk_used = sem("mqk_in"), sem("mqk_used")
        lower_ready = sem("lower_ready")
        s_ready, s_read = [sem(f"ms_ready{i}") for i in range(2)], [sem(f"ms_read{i}") for i in range(2)]
        neg_ready, negT_ready = sem("neg_ready"), sem("negT_ready")
        parts_ready, parts_stored = sem("mparts_ready"), sem("mparts_stored")
        block = ctx.enter_context(nc.Block())

        @block.sync
        def _(sp):
            general = sp.value_load(flags_i[0:1, 0:1], min_val=0, max_val=1)
            with sp.If(general == 1):
                with sp.Fori(0, B) as b:
                    sp.dma_start(mask_u8[:], io["mask"][b].rearrange("(t p) k -> p t k", p=P)).then_inc(mask_in, 16)
                    sp.wait_ge(mask_done, 1)
                    sp.sem_inc(mask_done, -1)
                    sp.dma_start(mask_dram[b].rearrange("(t p) k -> p t k", p=P), mask_fix[:]).then_inc(mask_stored, 16)
                    for m in range(M2):
                        sp.dma_start(ks[0:ROW_MAX], ks_dram[b, m, 0:ROW_MAX]).then_inc(qk_in, 16)
                        sp.dma_start(qs[0:ROW_MAX], qs_dram[b, m, 0:ROW_MAX]).then_inc(qk_in, 16)
                        sp.wait_ge(parts_ready, 1)
                        sp.sem_inc(parts_ready, -1)
                        sp.dma_start(qs_dram[b, m, ROW_MAX:ROWS].rearrange("r h k -> h r k"), parts[:]
                                     ).then_inc(parts_stored, 16)
                        sp.wait_ge(parts_stored, 16)
                        sp.sem_inc(parts_stored, -16)
                    sp.wait_ge(mask_stored, 16)
                    sp.sem_inc(mask_stored, -16)

        @block.vector
        def _(dve):
            general = dve.value_load(flags_i[0:1, 0:1], min_val=0, max_val=1)
            with dve.If(general == 1):
                nc.vector.tensor_scalar(lower[:], ident[:], -BIG, None, ALU.mult).then_inc(lower_ready, 1)
                dve.sem_inc(s_read[0], 1)
                dve.sem_inc(s_read[1], 1)
                with dve.Fori(0, B) as b:
                    dve.wait_ge(mask_in, 16)
                    dve.sem_inc(mask_in, -16)
                    nc.vector.tensor_copy(mask_bf[:], mask_u8[:])
                    dve.drain()
                    nc.vector.tensor_reduce(masked[:], mask_bf[:], op=ALU.add, axis=AX.X)
                    dve.drain()
                    nc.vector.tensor_scalar(has_key[:], masked[:], float(SK), None, ALU.is_lt)
                    dve.drain()
                    for t in range(QT):
                        nc.vector.tensor_scalar(mask_fix[:, t], mask_bf[:, t], has_key[:, t:t + 1], None, ALU.mult)
                    dve.drain().then_inc(mask_done, 1)
                    dve.sem_inc(mask_ready, 1)
                    for m in range(M2):
                        for h in range(H8):
                            for t in range(QT):
                                i = t % 2
                                dve.wait_ge(s_ready[i], 1)
                                dve.sem_inc(s_ready[i], -1)
                                nc.vector.tensor_reduce(neg_max[:, t, h:h + 1], pair_bank[i][:], op=ALU.max, axis=AX.XY,
                                                        negate=True).then_inc(s_read[i], 1)
                        dve.drain().then_inc(neg_ready, 1)
                        dve.wait_ge(negT_ready, 1)
                        dve.sem_inc(negT_ready, -1)
                        neg_t = bank[0][0:H8, :]
                        nc.vector.tensor_copy(parts[:, 0], neg_t)
                        dve.drain()
                        nc.vector.tensor_tensor(rest[:], neg_t, parts[:, 0], ALU.subtract)
                        dve.drain()
                        nc.vector.tensor_copy(parts[:, 1], rest[:])
                        dve.drain()
                        nc.vector.tensor_tensor(parts[:, 2], rest[:], parts[:, 1], ALU.subtract)
                        dve.drain().then_inc(parts_ready, 1)

        @block.tensor
        def _(pe):
            general = pe.value_load(flags_i[0:1, 0:1], min_val=0, max_val=1)
            with pe.If(general == 1):
                pe.wait_ge(lower_ready, 1)
                pe.sem_inc(lower_ready, -1)
                with pe.Fori(0, B) as b:
                    pe.wait_ge(mask_ready, 1)
                    pe.sem_inc(mask_ready, -1)
                    for m in range(M2):
                        pe.wait_ge(qk_in, 32)
                        pe.sem_inc(qk_in, -32)
                        for h in range(H8):
                            for t in range(QT):
                                i = t % 2
                                pe.wait_ge(s_read[i], 1)
                                pe.sem_inc(s_read[i], -1)
                                for e in range(2):
                                    cols = slice(e * 512, (e + 1) * 512)
                                    nc.tensor.matmul(pair_bank[i][:, e], qs[0:ROW_MAX, h, t * P:(t + 1) * P],
                                                     ks[0:ROW_MAX, h, cols], start=True, stop=False)
                                    last = nc.tensor.matmul(pair_bank[i][:, e], lower[:], mask_fix[:, t, cols],
                                                            start=False, stop=True)
                                last.then_inc(s_ready[i], 1)
                        pe.wait_ge(neg_ready, 1)
                        pe.sem_inc(neg_ready, -1)
                        for t in range(QT):
                            last = nc.tensor.transpose(bank[0][0:H8, t * P:(t + 1) * P], neg_max[:, t], ident[:])
                        last.then_inc(negT_ready, 1)


def main_phase(nc, top, io, out, ks_dram, qs_dram, v_dram, mask_dram, pair_bank, bank, ident, flags_i, ones3):
    o_bank, misc = bank[0:2], bank[2:4]
    with ExitStack() as ctx:
        sb = lambda name, shape, dt=F32: ctx.enter_context(nc.sbuf_tensor(name, shape, dt))
        sem = lambda name: top.enter_context(nc.semaphore(name))
        ks = sb("ks", [P, G, HG, SK], BF16)
        qs = sb("qs", [P, G, HG, S], BF16)
        v_in_sb = [sb(f"v_in_sb{i}", [P, KT, HG * HD]) for i in range(2)]
        va = sb("va", [P, KT, G, HG, 32])
        probs = [sb(f"probs{i}", [P, HG, S]) for i in range(2)]
        mask_fix = sb("mask_fix", [P, QT, SK], BF16)
        lower = sb("lower", [P, P], BF16)
        o_sb = sb("o_sb", [P, S])
        den, den_rows, inv = sb("den", [P, S]), sb("den_rows", [P, S]), sb("inv", [P, S // 32])
        o_pad = sb("o_pad", [P, G, S])
        o_t = sb("o_t", [P, KC, S])
        wo = sb("wo", [P, KC, D])
        wqkv = sb("wqkv", [P, KC, 3 * D])
        wout = sb("wout", [P, G, D])
        w1, w2 = (sb(n, [P, KC, FT * P]) for n in ("w1", "w2"))
        w3 = sb("w3", [P, FT, D])
        wr_b, g1_b, g2_b = (sb(n, [P, D]) for n in ("wr_b", "g1_b", "g2_b"))
        iota_r = sb("iota_r", [P, CAP])
        before = sb("before", [P, QT, S], BF16)
        block_of = sb("block_of2", [P, H8])
        causal = sb("causal", [P, CAP])
        neg_half = sb("neg_half2", [P, QT])
        x1 = sb("x1", [P, QT, D])
        y = sb("y", [P, QT, D])
        base = sb("base", [P, QT, D])
        out_sb = sb("out_sb", [P, QT, D])
        stats = sb("stats2", [P, QT, 6])
        mv = sb("mv2", [P, QT, 2])
        veps = sb("veps2", [P, QT])
        rstd = sb("rstd2", [P, QT])
        score = sb("score", [P, QT])
        all_scores = sb("all_scores", [P, S])
        ties = [den, den_rows]
        prod = den_rows[:, 0:D]
        rank = sb("rank", [P, QT])
        sel = sb("sel", [P, QT, CAP])
        sel_t = sb("sel_t", [P, S])
        x_sel = sb("x_sel", [P, D])
        x_keep = sb("x_keep", [P, D])
        ms = sb("ms", [P, 4])
        hid = sb("hid", [P, D])
        hid_t = sb("hid_t", [P, KC, CAP])
        q_t = sb("q_t", [P, KC, CAP])
        v_s = sb("v_s", [P, H, 32])
        k_block = sb("k_block", [P, M2, H8, CAP])
        p_t = k_block[:].rearrange("p m h k -> p (m h) k")
        sc = sb("sc", [P, H, CAP])
        s_max = sb("s_max", [P, H])
        os_t = sb("os_t", [P, G, CAP])
        att = sb("att", [P, D])
        sig = [sb(f"sig{r}", [P, 3 * P]) for r in range(2)]
        up = [sb(f"up{r}", [P, 3 * P]) for r in range(2)]
        gate = sb("gate", [P, FT, P])

        w_zero, w_in, consts, lower_set = sem("w_zero"), sem("w2_in"), sem("consts"), sem("lower_set")
        rows_set, group_in = sem("rows_set"), [sem(f"group_in{g}") for g in range(G)]
        group_free, v_in, v_in_free = sem("group_free"), [sem(f"v_in{i}") for i in range(2)], sem("v_in_free")
        va_ready, va_free = sem("va_ready"), sem("va_free")
        maskfix_in, maskfix_free = sem("maskfix_in"), sem("maskfix_free")
        s_ready, s_read = [sem(f"s_ready{i}") for i in range(2)], [sem(f"s_read{i}") for i in range(2)]
        o_ready, o_free, ot_ready, ot_free = sem("o_ready"), sem("o_free"), sem("ot_ready"), sem("ot_free")
        misc_free = [sem(f"misc_free{i}") for i in range(2)]
        xres_in, xres_free = sem("xres_in"), sem("xres_free")
        wo_ready, var2_ready, rstd2_ready, y_ready = sem("wo_ready"), sem("var2_ready"), sem("rstd2_ready"), sem("y_ready")
        score_ready, spread_ready, sel_ready = sem("score_ready"), sem("spread_ready"), sem("sel_ready")
        base_ready, base_free, all_ready = sem("base_ready"), sem("base_free"), sem("all_ready")
        gather_ready, selT_ready, selT_sb = sem("gather_ready"), sem("selT_ready"), sem("selT_sb")
        ms_ready, rms_ready, hid_ready, hidT_ready, hidT_sb = (
            sem("ms_ready"), sem("rms_ready"), sem("hid_ready"), sem("hidT_ready"), sem("hidT_sb"))
        qv_ready, k_ready, qv_sb, kb_ready = sem("qv_ready"), sem("k_ready"), sem("qv_sb"), sem("kb_ready")
        sc_ready, scm_ready, p_ready, opad_ready = sem("sc_ready"), sem("scm_ready"), sem("p_ready"), sem("opad_ready")
        pT_ready, pT_sb, pv_ready, os_ready = sem("pT_ready"), sem("pT_sb"), sem("pv_ready"), sem("os_ready")
        att_ready = sem("att_ready")
        hid2_ready, hid2T_ready, hid2T_sb = sem("hid2_ready"), sem("hid2T_ready"), sem("hid2T_sb")
        u_ready, w_ready, sig_ready, sig_used, gate_ready = (
            sem("u_ready"), sem("w_ready"), sem("sig_ready"), sem("sig_used"), sem("gate_ready"))
        ff_ready, delta_ready, scat_ready = sem("ff_ready"), sem("delta_ready"), sem("scat_ready")
        out_ready, out_stored = sem("out_ready"), sem("out_stored")

        block = ctx.enter_context(nc.Block())
        N_W = 1 + 1 + 4 + 1 + 1 + 2 + 3

        @block.sync
        def _(sp):
            general = sp.value_load(flags_i[0:1, 0:1], min_val=0, max_val=1)
            def load_group(b, g):
                m, h0 = g // (G // M2), (g % (G // M2)) * HG
                sp.wait_ge(group_free, 1)
                sp.sem_inc(group_free, -1)
                sp.dma_start(ks[0:ROW_MAX, g], ks_dram[b, m, 0:ROW_MAX, h0:h0 + HG, :]).then_inc(group_in[g], 16)
                sp.dma_start(qs[0:ROWS, g], qs_dram[b, m, :, h0:h0 + HG, :]).then_inc(group_in[g], 16)
                sp.wait_ge(v_in_free, 1)
                sp.sem_inc(v_in_free, -1)
                src = v_dram[b].rearrange("(t p) n -> p t n", p=P)[:, :, g * HG * HD:(g + 1) * HG * HD]
                sp.dma_start(v_in_sb[g % 2][:], src).then_inc(v_in[g % 2], 16)

            def compact(g):
                if g == 0:
                    sp.wait_ge(ot_free, 1)
                    sp.sem_inc(ot_free, -1)
                sp.wait_ge(opad_ready, 1)
                sp.sem_inc(opad_ready, -1)
                r0 = (g % 2) * HG * HD
                for j in range(HG):
                    sp.dma_start(o_t[r0 + HD * j:r0 + HD * (j + 1), g // 2], o_pad[32 * j:32 * j + HD, g]
                                 ).then_inc(ot_ready, 16)

            def load_mask(b):
                with sp.If(general == 1):
                    sp.wait_ge(maskfix_free, 1)
                    sp.sem_inc(maskfix_free, -1)
                    sp.dma_start(mask_fix[:], mask_dram[b].rearrange("(t p) k -> p t k", p=P)).then_inc(maskfix_in, 16)

            def load_x(b):
                sp.wait_ge(xres_free, 1)
                sp.sem_inc(xres_free, -1)
                sp.dma_start(x1[:], io["x"][b].rearrange("(t p) d -> p t d", p=P)).then_inc(xres_in, 16)

            def store(b):
                sp.wait_ge(out_ready, 1)
                sp.sem_inc(out_ready, -1)
                sp.dma_start(out[b].rearrange("(t p) d -> p t d", p=P), out_sb[:]).then_inc(out_stored, 16)

            sp.dma_start(ks[ROW_MAX:ROWS].rearrange("p g j (e k) -> p (g j e) k", e=2),
                         ones3[:].unsqueeze(1).broadcast_to([ROWS - ROW_MAX, G * HG * 2, SK // 2])).then_inc(rows_set, 16)
            load_group(0, 0)
            load_group(0, 1)
            sp.wait_ge(w_zero, 1)
            sp.sem_inc(w_zero, -1)
            sp.dma_start(wo[:], io["woT"].rearrange("(c p) n -> p c n", p=P)).then_inc(w_in, 16)
            sp.dma_start(wqkv[:], io["wqkvT"].rearrange("(c p) n -> p c n", p=P)).then_inc(w_in, 16)
            wout_rows = io["woutT"].rearrange("(g j d) n -> j d g n", g=G, j=HG)
            for j in range(HG):
                sp.dma_start(wout[32 * j:32 * j + HD], wout_rows[j]).then_inc(w_in, 16)
            sp.dma_start(w1[:, :, 0:DFF], io["w1T"].rearrange("(c p) n -> p c n", p=P)).then_inc(w_in, 16)
            sp.dma_start(w2[:, :, 0:DFF], io["w2T"].rearrange("(c p) n -> p c n", p=P)).then_inc(w_in, 16)
            full = DFF // P
            sp.dma_start(w3[:, 0:full], io["w3T"][0:full * P].rearrange("(c p) n -> p c n", p=P)).then_inc(w_in, 16)
            sp.dma_start(w3[0:DFF - full * P, full], io["w3T"][full * P:DFF]).then_inc(w_in, 16)
            for dst, name in ((wr_b, "w_router"), (g1_b, "g1"), (g2_b, "g2")):
                sp.dma_start(dst[:], io[name].partition_broadcast(P)).then_inc(w_in, 16)
            for g in range(2, G):
                load_group(0, g)
            load_mask(0)
            for b in range(2):
                for g in range(G - 1):
                    compact(g)
                    load_group(b + 1, g)
                load_x(b)
                load_mask(b + 1)
                compact(G - 1)
                load_group(b + 1, G - 1)
            with sp.Fori(2, B - 1) as b:
                for g in range(G - 1):
                    compact(g)
                    load_group(b + 1, g)
                store(b - 2)
                load_x(b)
                load_mask(b + 1)
                compact(G - 1)
                load_group(b + 1, G - 1)
            for g in range(G - 1):
                compact(g)
            store(B - 3)
            load_x(B - 1)
            compact(G - 1)
            store(B - 2)
            store(B - 1)
            sp.wait_ge(out_stored, 16)

        @block.gpsimd
        def _(pool):
            def spread_v(g):
                pool.wait_ge(v_in[g % 2], 16)
                pool.sem_inc(v_in[g % 2], -16)
                pool.wait_ge(va_free, 1)
                pool.sem_inc(va_free, -1)
                nc.gpsimd.tensor_copy(va[:, :, g, :, 0:HD], v_in_sb[g % 2][:].rearrange("p t (h d) -> p t h d", h=HG)
                                      ).then_inc(va_ready, 1)
                pool.drain().then_inc(v_in_free, 1)

            nc.gpsimd.memset(va[:].rearrange("p t g h c -> p (t g h) c")[:, :, HD:32], 1.0)
            nc.gpsimd.memset(v_s[:, :, HD:32], 1.0)
            nc.gpsimd.memset(wout[:], 0.0)
            nc.gpsimd.memset(w1[:, :, DFF:], 0.0)
            nc.gpsimd.memset(w2[:, :, DFF:], 0.0)
            nc.gpsimd.memset(w3[:, DFF // P], 0.0)
            pool.drain().then_inc(w_zero, 1)
            spread_v(0)
            spread_v(1)
            nc.gpsimd.memset(neg_half[:], -0.5)
            nc.gpsimd.memset(before[:], 1.0)
            nc.gpsimd.memset(block_of[:], 1.0)
            nc.gpsimd.memset(causal[:], 0.0)
            nc.gpsimd.iota(iota_r[:], pattern=[[1, CAP]], base=0, channel_multiplier=0,
                           allow_small_or_imprecise_dtypes=True)
            pool.drain()
            for t in range(QT):
                nc.gpsimd.affine_select(out=before[:, t], in_=before[:, t], compare_op=ALU.is_gt, fill=0.0,
                                        base=t * P, pattern=[[-1, S]], channel_multiplier=1)
            nc.gpsimd.affine_select(out=block_of[:], in_=block_of[:], compare_op=ALU.is_ge, fill=0.0,
                                    base=0, pattern=[[-HD, H8]], channel_multiplier=1)
            nc.gpsimd.affine_select(out=causal[:], in_=causal[:], compare_op=ALU.is_ge, fill=-1e30,
                                    base=0, pattern=[[-1, CAP]], channel_multiplier=1)
            pool.drain()
            nc.gpsimd.affine_select(out=block_of[:], in_=block_of[:], compare_op=ALU.is_gt, fill=0.0,
                                    base=HD, pattern=[[HD, H8]], channel_multiplier=-1)
            pool.drain().then_inc(consts, 1)

            def rms(col):
                pool.wait_ge(ms_ready, 1)
                pool.sem_inc(ms_ready, -1)
                nc.gpsimd.tensor_scalar(ms[:, col + 1:col + 2], ms[:, col:col + 1], 1.0 / D, RMS_EPS, ALU.mult, ALU.add)
                pool.drain()
                nc.gpsimd.tensor_tensor(ms[:, col:col + 1], ms[:, col + 1:col + 2], neg_half[:, 0:1], ALU.pow
                                        ).then_inc(rms_ready, 1)

            def norm():
                pool.wait_ge(var2_ready, 1)
                pool.sem_inc(var2_ready, -1)
                nc.gpsimd.tensor_scalar(veps[:], mv[:, :, 1], LN_EPS, None, ALU.add)
                pool.drain()
                nc.gpsimd.tensor_tensor(rstd[:], veps[:], neg_half[:], ALU.pow).then_inc(rstd2_ready, 1)

            def make_base():
                pool.wait_ge(y_ready, 1)
                pool.sem_inc(y_ready, -1)
                pool.wait_ge(base_free, 1)
                pool.sem_inc(base_free, -1)
                nc.gpsimd.tensor_tensor(base[:], x1[:], y[:], ALU.add).then_inc(base_ready, 1)
                pool.drain().then_inc(xres_free, 1)

            def batch(first, last):
                norm()
                spread_v(3)
                rms(0)
                if not first:
                    rms(2)
                if not last:
                    spread_v(0)
                    spread_v(1)
                make_base()
                if not last:
                    spread_v(2)

            for g in (2, 3, 0, 1, 2):
                spread_v(g)
            batch(first=True, last=False)
            with pool.Fori(2, B - 1) as b:
                batch(first=False, last=False)
            batch(first=False, last=True)
            norm()
            rms(0)
            rms(2)
            rms(2)
            make_base()

        def act_step(act, s):
            for pr in range(2):
                act.wait_ge(s_ready[pr], 1)
                act.sem_inc(s_ready[pr], -1)
                nc.scalar.activation(probs[s % 2][:, 2 * pr:2 * pr + 2, :], pair_bank[pr][:], ACT.Exp,
                                     scale=HD ** -0.5).then_inc(s_read[pr], 1)

        def act_ffn(act, stage):
            if stage == "selT":
                act.wait_ge(selT_ready, 1)
                act.sem_inc(selT_ready, -1)
                nc.scalar.activation(sel_t[:], misc[1][:], ACT.Copy).then_inc(misc_free[1], 1)
                act.drain().then_inc(selT_sb, 1)
            elif stage == "spread":
                act.wait_ge(spread_ready, 1)
                act.sem_inc(spread_ready, -1)
                nc.scalar.activation(all_scores[:], misc[1][:], ACT.Copy).then_inc(misc_free[1], 1)
                act.drain().then_inc(all_ready, 1)
            elif stage == "hid2T":
                act.wait_ge(hid2T_ready, 1)
                act.sem_inc(hid2T_ready, -1)
                nc.scalar.activation(hid_t[:], misc[1][:, 0:KC * CAP].rearrange("p (c k) -> p c k", c=KC), ACT.Copy
                                     ).then_inc(misc_free[1], 1)
                act.drain().then_inc(hid2T_sb, 1)
            elif stage == "hidT":
                act.wait_ge(hidT_ready, 1)
                act.sem_inc(hidT_ready, -1)
                nc.scalar.activation(hid_t[:], misc[1][:, 0:KC * CAP].rearrange("p (c k) -> p c k", c=KC), ACT.Copy
                                     ).then_inc(misc_free[1], 1)
                act.drain().then_inc(hidT_sb, 1)
            elif stage == "qv":
                act.wait_ge(qv_ready, 1)
                act.sem_inc(qv_ready, -1)
                nc.scalar.activation(q_t[:], misc[1][:, 0:KC * CAP].rearrange("p (c k) -> p c k", c=KC), ACT.Copy)
                nc.scalar.activation(v_s[:, :, 0:HD], misc[1][:, D:2 * D].rearrange("p (h d) -> p h d", h=H), ACT.Copy).then_inc(misc_free[1], 1)
                act.drain().then_inc(qv_sb, 1)
            elif stage in ("exp0", "exp1"):
                m = int(stage[3])
                act.wait_ge(scm_ready, 1)
                act.sem_inc(scm_ready, -1)
                nc.scalar.activation(sc[:, H8 * m:H8 * m + H8], sc[:, H8 * m:H8 * m + H8], ACT.Exp, scale=HD ** -0.5
                                     ).then_inc(p_ready, 1)
            elif stage.startswith("pT"):
                n = int(stage[2])
                act.wait_ge(pT_ready, 1)
                act.sem_inc(pT_ready, -1)
                nc.scalar.activation(p_t[:, 4 * n:4 * n + 4, :], misc[n % 2][:].rearrange("p (h k) -> p h k", h=4), ACT.Copy
                                     ).then_inc(misc_free[n % 2], 1)
                if n == 3:
                    act.drain().then_inc(pT_sb, 1)
            elif stage in ("u0", "u1"):
                r = int(stage[1])
                act.wait_ge(u_ready, 1)
                act.sem_inc(u_ready, -1)
                act.wait_ge(sig_used, 1)
                act.sem_inc(sig_used, -1)
                nc.scalar.activation(sig[r][:], misc[0][:, 0:3 * P], ACT.Exp, scale=-1.0)
                nc.scalar.activation(up[r][:], misc[0][:, 0:3 * P], ACT.Copy).then_inc(misc_free[0], 1)
            elif stage in ("w0", "w1"):
                r = int(stage[1])
                act.wait_ge(w_ready, 1)
                act.sem_inc(w_ready, -1)
                nc.scalar.activation(gate[:, 3 * r:3 * r + 3], misc[1][:, 0:3 * P].rearrange("p (f k) -> p f k", f=3),
                                     ACT.Copy).then_inc(misc_free[1], 1)
                act.drain().then_inc(sig_ready, 1)

        @block.scalar
        def _(act):
            def batch(parts):
                for s in range(G * KT):
                    act_step(act, s)
                    for part, stage, at in ACT_SLOT:
                        if at == s and part in parts:
                            act_ffn(act, stage)

            batch("")
            batch("A")
            with act.Fori(2, B) as b:
                batch("AB")
            for stage in ACT_END:
                act_ffn(act, stage)

        def normalised(dve, dst, src, free):
            nc.vector.tensor_copy(o_sb[:], src[:]).then_inc(free, 1)
            dve.drain()
            nc.vector.transpose(den[:], o_sb[:])
            dve.drain()
            nc.vector.reciprocal(inv[:], den[:].rearrange("p (c r) -> p c r", r=32)[:, :, HD])
            dve.drain()
            nc.vector.tensor_copy(den[:].rearrange("p (c r) -> p c r", r=32), inv[:].unsqueeze(2).broadcast_to([P, S // 32, 32]))
            dve.drain()
            nc.vector.transpose(den_rows[:], den[:])
            dve.drain()
            return nc.vector.tensor_tensor(dst, o_sb[:], den_rows[:], ALU.mult)

        def group_end(dve, g):
            dve.drain()
            dve.wait_ge(o_ready, 1)
            dve.sem_inc(o_ready, -1)
            dve.sem_inc(group_free, 1)
            dve.sem_inc(va_free, 1)
            normalised(dve, o_pad[:, g], o_bank[g % 2], o_free).then_inc(opad_ready, 1)

        def square_sum(dve, src, col):
            nc.vector.scalar_tensor_tensor(out=prod, in0=src, scalar=1.0, in1=src, op0=ALU.mult, op1=ALU.mult,
                                           accum_out=ms[:, col:col + 1])
            dve.drain().then_inc(ms_ready, 1)

        def dve_ffn(dve, stage):
            dve.drain()
            if stage == "x1":
                dve.wait_ge(xres_in, 16)
                dve.sem_inc(xres_in, -16)
                for pr in range(2):
                    dve.wait_ge(wo_ready, 1)
                    dve.sem_inc(wo_ready, -1)
                    nc.vector.tensor_tensor(x1[:, 2 * pr:2 * pr + 2], x1[:, 2 * pr:2 * pr + 2],
                                            misc[pr][:].rearrange("p (t d) -> p t d", t=2), ALU.add
                                            ).then_inc(misc_free[pr], 1)
                    dve.drain()
                    for t in (2 * pr, 2 * pr + 1):
                        nc.vector.bn_stats(stats[:, t], x1[:, t])
                dve.sem_inc(ot_free, 1)
                dve.drain()
                for t in range(QT):
                    nc.vector.bn_aggr(mv[:, t], stats[:, t])
                dve.drain().then_inc(var2_ready, 1)
            elif stage == "y":
                dve.wait_ge(rstd2_ready, 1)
                dve.sem_inc(rstd2_ready, -1)
                for t in range(QT):
                    nc.vector.tensor_scalar(y[:, t], x1[:, t], mv[:, t, 0:1], rstd[:, t:t + 1], ALU.subtract, ALU.mult)
                dve.drain().then_inc(y_ready, 1)
                for t in range(QT):
                    unused = (den, den_rows)[t // 2][:, (t % 2) * D:(t % 2 + 1) * D]
                    nc.vector.scalar_tensor_tensor(out=unused, in0=y[:, t], scalar=1.0, in1=wr_b[:], op0=ALU.mult,
                                                   op1=ALU.mult, accum_out=score[:, t:t + 1])
                dve.drain().then_inc(score_ready, 1)
            elif stage == "rank":
                dve.wait_ge(all_ready, 1)
                dve.sem_inc(all_ready, -1)
                for t in range(QT + 2):
                    if t < QT:
                        nc.vector.scalar_tensor_tensor(out=ties[t % 2][:], in0=all_scores[:], scalar=score[:, t:t + 1],
                                                       in1=before[:, t], op0=ALU.is_equal, op1=ALU.mult)
                    if 1 <= t <= QT:
                        nc.vector.scalar_tensor_tensor(out=ties[(t - 1) % 2][:], in0=all_scores[:],
                                                       scalar=score[:, t - 1:t], in1=ties[(t - 1) % 2][:],
                                                       op0=ALU.is_gt, op1=ALU.add, accum_out=rank[:, t - 1:t])
                    if t >= 2:
                        nc.vector.tensor_scalar(sel[:, t - 2], iota_r[:], rank[:, t - 2:t - 1], None, ALU.is_equal)
                    if t < QT + 1:
                        dve.drain()
                dve.drain().then_inc(sel_ready, 1)
            elif stage == "hid":
                dve.wait_ge(gather_ready, 1)
                dve.sem_inc(gather_ready, -1)
                nc.vector.tensor_copy(x_sel[:], misc[1][:, 0:D]).then_inc(misc_free[1], 1)
                dve.drain()
                square_sum(dve, x_sel[:], 0)
                dve.wait_ge(rms_ready, 1)
                dve.sem_inc(rms_ready, -1)
                nc.vector.scalar_tensor_tensor(out=hid[:], in0=x_sel[:], scalar=ms[:, 0:1], in1=g1_b[:],
                                               op0=ALU.mult, op1=ALU.mult).then_inc(hid_ready, 1)
            elif stage == "k_block":
                dve.wait_ge(k_ready, 1)
                dve.sem_inc(k_ready, -1)
                for m in range(M2):
                    src = misc[0][:, m * CAP:(m + 1) * CAP]
                    last = nc.vector.tensor_tensor(k_block[:, m], src.unsqueeze(1).broadcast_to([P, H8, CAP]),
                                                   block_of[:].unsqueeze(2).broadcast_to([P, H8, CAP]), ALU.mult)
                    last.then_inc(kb_ready, 1)
                dve.drain().then_inc(misc_free[0], 1)
            elif stage == "masked":
                for n in range(4):
                    dve.wait_ge(sc_ready, 1)
                    dve.sem_inc(sc_ready, -1)
                    nc.vector.tensor_tensor(sc[:, 4 * n:4 * n + 4], misc[n % 2][:].rearrange("p (h k) -> p h k", h=4),
                                            causal[:].unsqueeze(1).broadcast_to([P, 4, CAP]), ALU.add
                                            ).then_inc(misc_free[n % 2], 1)
            elif stage in ("soft0", "soft1"):
                m = int(stage[4])
                heads = slice(H8 * m, H8 * m + H8)
                nc.vector.tensor_reduce(s_max[:, heads], sc[:, heads], op=ALU.max, axis=AX.X)
                dve.drain()
                nc.vector.tensor_tensor(sc[:, heads], sc[:, heads], s_max[:, heads].unsqueeze(2).broadcast_to([P, H8, CAP]),
                                        ALU.subtract).then_inc(scm_ready, 1)
            elif stage == "keep":
                nc.vector.tensor_copy(x_keep[:], x_sel[:])
            elif stage == "os":
                dve.wait_ge(pv_ready, 1)
                dve.sem_inc(pv_ready, -1)
                normalised(dve, os_t[:].rearrange("p g k -> p (g k)"), misc[0], misc_free[0]).then_inc(os_ready, 1)
            elif stage == "hid2":
                dve.wait_ge(att_ready, 1)
                dve.sem_inc(att_ready, -1)
                nc.vector.tensor_copy(att[:], misc[0][:, 0:D]).then_inc(misc_free[0], 1)
                dve.drain()
                nc.vector.tensor_tensor(x_keep[:], x_keep[:], att[:], ALU.add)
                dve.drain()
                square_sum(dve, x_keep[:], 2)
                dve.wait_ge(rms_ready, 1)
                dve.sem_inc(rms_ready, -1)
                nc.vector.scalar_tensor_tensor(out=x_keep[:], in0=x_keep[:], scalar=ms[:, 2:3], in1=g2_b[:],
                                               op0=ALU.mult, op1=ALU.mult).then_inc(hid2_ready, 1)
            elif stage in ("gate0", "gate1"):
                r = int(stage[4])
                dve.wait_ge(sig_ready, 1)
                dve.sem_inc(sig_ready, -1)
                nc.vector.tensor_scalar(sig[r][:], sig[r][:], 1.0, None, ALU.add)
                half = gate[:, 3 * r:3 * r + 3]
                nc.vector.tensor_tensor(half, half, up[r][:].rearrange("p (f k) -> p f k", f=3), ALU.mult)
                dve.drain()
                nc.vector.reciprocal(sig[r][:], sig[r][:])
                dve.drain()
                nc.vector.tensor_tensor(half, half, sig[r][:].rearrange("p (f k) -> p f k", f=3), ALU.mult
                                        ).then_inc(gate_ready, 1)
                dve.drain().then_inc(sig_used, 1)
            elif stage == "delta":
                dve.wait_ge(ff_ready, 1)
                dve.sem_inc(ff_ready, -1)
                nc.vector.tensor_tensor(att[:], att[:], misc[0][:, 0:D], ALU.add).then_inc(misc_free[0], 1)
                dve.drain().then_inc(delta_ready, 1)
            elif stage == "base":
                dve.wait_ge(base_ready, 1)
                dve.sem_inc(base_ready, -1)
            elif stage == "out":
                dve.wait_ge(out_stored, 16)
                dve.sem_inc(out_stored, -16)
                for pr in (1, 0):
                    dve.wait_ge(scat_ready, 1)
                    dve.sem_inc(scat_ready, -1)
                    nc.vector.tensor_tensor(out_sb[:, 2 * pr:2 * pr + 2], base[:, 2 * pr:2 * pr + 2],
                                            misc[pr][:].rearrange("p (t d) -> p t d", t=2), ALU.add
                                            ).then_inc(misc_free[pr], 1)
                dve.drain().then_inc(out_ready, 1)
                dve.sem_inc(base_free, 1)

        @block.vector
        def _(dve):
            nc.vector.tensor_scalar(lower[:], ident[:], -BIG, None, ALU.mult)
            dve.sem_inc(maskfix_free, 1)
            dve.sem_inc(group_free, G)
            dve.sem_inc(va_free, G)
            dve.sem_inc(v_in_free, 2)
            dve.sem_inc(o_free, 2)
            dve.sem_inc(ot_free, 1)
            dve.sem_inc(misc_free[0], 1)
            dve.sem_inc(misc_free[1], 1)
            dve.sem_inc(xres_free, 1)
            dve.sem_inc(sig_used, 2)
            dve.sem_inc(base_free, 1)
            dve.sem_inc(out_stored, 16)
            dve.drain().then_inc(lower_set, 1)
            def batch(parts):
                for part, stage in DVE_ORDER:
                    if part == "group":
                        group_end(dve, stage)
                    elif part in parts:
                        dve_ffn(dve, stage)

            batch("")
            dve.wait_ge(consts, 1)
            dve.sem_inc(consts, -1)
            batch("A")
            with dve.Fori(2, B) as b:
                batch("AB")
            for stage in DVE_END:
                dve_ffn(dve, stage)

        def scores(pe, s, general, first):
            g, t = s // KT, s % KT
            if t == 0:
                pe.wait_ge(group_in[g], 32)
                pe.sem_inc(group_in[g], -32)
            if general and s == 0:
                if not first:
                    pe.wait_ge(s_read[0], 1)
                    pe.sem_inc(s_read[0], -1)
                    pe.wait_ge(s_read[1], 1)
                    pe.sem_inc(s_read[1], -1)
                    pe.sem_inc(maskfix_free, 1)
                pe.wait_ge(maskfix_in, 16)
                pe.sem_inc(maskfix_in, -16)
            for pr in range(2):
                if s > 0 or (not first and not general):
                    pe.wait_ge(s_read[pr], 1)
                    pe.sem_inc(s_read[pr], -1)
                for e in range(2):
                    j = 2 * pr + e
                    last = nc.tensor.matmul(pair_bank[pr][:, e], ks[0:ROWS, g, j, t * P:(t + 1) * P],
                                            qs[0:ROWS, g, j, :], start=True, stop=not general)
                    if general:
                        for n in range(QT):
                            last = nc.tensor.matmul(pair_bank[pr][:, e, n * P:(n + 1) * P],
                                                    mask_fix[:, n, t * P:(t + 1) * P], lower[:],
                                                    start=False, stop=(n == QT - 1))
                last.then_inc(s_ready[pr], 1)

        def values(pe, s):
            g, t = s // KT, s % KT
            if t == 0:
                pe.wait_ge(va_ready, 1)
                pe.sem_inc(va_ready, -1)
                pe.wait_ge(o_free, 1)
                pe.sem_inc(o_free, -1)
            for j in range(HG):
                last = nc.tensor.matmul(o_bank[g % 2][32 * j:32 * j + 32], va[:, t, g, j], probs[s % 2][:, j],
                                        start=(t == 0), stop=(t == KT - 1))
            if t == KT - 1:
                last.then_inc(o_ready, 1)

        def pe_attention(pe, parts, general, first=False):
            for s in range(G * KT):
                scores(pe, s, general, first)
                if s > 0 or not first:
                    values(pe, (s - 1) % (G * KT))
                for part, stage, at in PE_SLOT:
                    if at == s and part in parts:
                        pe_ffn(pe, stage)

        def transposes(dst, srcs):
            for n, src in enumerate(srcs):
                last = nc.tensor.transpose(dst[:, n * P:(n + 1) * P], src, ident[:])
            return last

        def product(dst, pairs):
            for n, (a, c) in enumerate(pairs):
                last = nc.tensor.matmul(dst, a, c, start=(n == 0), stop=(n == len(pairs) - 1))
            return last

        def pe_ffn(pe, stage):
            if stage in ("wo0", "wo1", "wo2", "wo3"):
                t = int(stage[2])
                pr, e = t // 2, t % 2
                if t == 0:
                    pe.wait_ge(ot_ready, 16 * G * HG)
                    pe.sem_inc(ot_ready, -16 * G * HG)
                if e == 0:
                    pe.wait_ge(misc_free[pr], 1)
                    pe.sem_inc(misc_free[pr], -1)
                last = product(misc[pr][:, e * D:(e + 1) * D], [(o_t[:, c, t * P:(t + 1) * P], wo[:, c]) for c in range(KC)])
                if e == 1:
                    last.then_inc(wo_ready, 1)
            elif stage == "spread":
                pe.wait_ge(score_ready, 1)
                pe.sem_inc(score_ready, -1)
                pe.wait_ge(misc_free[1], 1)
                pe.sem_inc(misc_free[1], -1)
                transposes(misc[1], [score[:, t:t + 1].broadcast_to([P, P]) for t in range(QT)]).then_inc(spread_ready, 1)
            elif stage == "gather":
                pe.wait_ge(sel_ready, 1)
                pe.sem_inc(sel_ready, -1)
                pe.wait_ge(misc_free[1], 1)
                pe.sem_inc(misc_free[1], -1)
                product(misc[1][:, 0:D], [(sel[:, t], y[:, t]) for t in range(QT)]).then_inc(gather_ready, 1)
            elif stage == "selT":
                pe.wait_ge(misc_free[1], 1)
                pe.sem_inc(misc_free[1], -1)
                transposes(misc[1], [sel[:, t] for t in range(QT)]).then_inc(selT_ready, 1)
            elif stage == "hid2T":
                pe.wait_ge(hid2_ready, 1)
                pe.sem_inc(hid2_ready, -1)
                pe.wait_ge(misc_free[1], 1)
                pe.sem_inc(misc_free[1], -1)
                transposes(misc[1], [x_keep[:, c * P:(c + 1) * P] for c in range(KC)]).then_inc(hid2T_ready, 1)
            elif stage == "hidT":
                pe.wait_ge(hid_ready, 1)
                pe.sem_inc(hid_ready, -1)
                pe.wait_ge(misc_free[1], 1)
                pe.sem_inc(misc_free[1], -1)
                transposes(misc[1], [hid[:, c * P:(c + 1) * P] for c in range(KC)]).then_inc(hidT_ready, 1)
            elif stage == "q":
                pe.wait_ge(hidT_sb, 1)
                pe.sem_inc(hidT_sb, -1)
                pe.wait_ge(misc_free[1], 1)
                pe.sem_inc(misc_free[1], -1)
                for n in range(2):
                    product(misc[1][:, n * CAP:(n + 1) * CAP],
                            [(wqkv[:, c, n * P:(n + 1) * P], hid_t[:, c]) for c in range(KC)])
            elif stage == "v":
                product(misc[1][:, D:2 * D], [(hid_t[:, c], wqkv[:, c, 2 * D:3 * D]) for c in range(KC)]
                        ).then_inc(qv_ready, 1)
            elif stage in ("k0", "k1"):
                n = int(stage[1])
                if n == 0:
                    pe.wait_ge(misc_free[0], 1)
                    pe.sem_inc(misc_free[0], -1)
                last = product(misc[0][:, n * CAP:(n + 1) * CAP],
                               [(wqkv[:, c, D + n * P:D + (n + 1) * P], hid_t[:, c]) for c in range(KC)])
                if n == 1:
                    last.then_inc(k_ready, 1)
            elif stage in ("sc0", "sc1"):
                m = int(stage[2])
                pe.wait_ge(kb_ready, 1)
                pe.sem_inc(kb_ready, -1)
                if m == 0:
                    pe.wait_ge(qv_sb, 1)
                    pe.sem_inc(qv_sb, -1)
                for e in range(2):
                    pe.wait_ge(misc_free[e], 1)
                    pe.sem_inc(misc_free[e], -1)
                    nc.tensor.matmul(misc[e][:], q_t[:, m], k_block[:, m, 4 * e:4 * e + 4, :], start=True, stop=True
                                     ).then_inc(sc_ready, 1)
            elif stage in ("pT0", "pT1"):
                m = int(stage[2])
                pe.wait_ge(p_ready, 1)
                pe.sem_inc(p_ready, -1)
                for e in range(2):
                    pe.wait_ge(misc_free[e], 1)
                    pe.sem_inc(misc_free[e], -1)
                    h0 = 8 * m + 4 * e
                    transposes(misc[e], [sc[:, h] for h in range(h0, h0 + 4)]).then_inc(pT_ready, 1)
            elif stage in ("pv0", "pv1"):
                r = int(stage[2])
                if r == 0:
                    pe.wait_ge(pT_sb, 1)
                    pe.sem_inc(pT_sb, -1)
                    pe.wait_ge(misc_free[0], 1)
                    pe.sem_inc(misc_free[0], -1)
                for g in range(2 * r, 2 * r + 2):
                    for j in range(HG):
                        last = nc.tensor.matmul(misc[0][32 * j:32 * j + 32, g * CAP:(g + 1) * CAP], v_s[:, HG * g + j],
                                                p_t[:, HG * g + j], start=True, stop=True)
                if r == 1:
                    last.then_inc(pv_ready, 1)
            elif stage.startswith("wout"):
                g = int(stage[4])
                if g == 0:
                    pe.wait_ge(os_ready, 1)
                    pe.sem_inc(os_ready, -1)
                    pe.wait_ge(misc_free[0], 1)
                    pe.sem_inc(misc_free[0], -1)
                last = nc.tensor.matmul(misc[0][:, 0:D], os_t[:, g], wout[:, g], start=(g == 0), stop=(g == G - 1))
                if g == G - 1:
                    last.then_inc(att_ready, 1)
            elif stage in ("u0", "u1", "w0", "w1a", "w1b"):
                r = int(stage[1])
                if stage == "u0":
                    pe.wait_ge(hid2T_sb, 1)
                    pe.sem_inc(hid2T_sb, -1)
                w, i, ready = (w1, 0, u_ready) if stage[0] == "u" else (w2, 1, w_ready)
                tiles = {"w1a": (0, 1), "w1b": (2,)}.get(stage, (0, 1, 2))
                if 0 in tiles:
                    pe.wait_ge(misc_free[i], 1)
                    pe.sem_inc(misc_free[i], -1)
                for f in tiles:
                    last = product(misc[i][:, f * P:(f + 1) * P],
                                   [(w[:, c, (3 * r + f) * P:(3 * r + f + 1) * P], hid_t[:, c]) for c in range(KC)])
                if 2 in tiles:
                    last.then_inc(ready, 1)
            elif stage in ("down0", "down1"):
                r = int(stage[4])
                pe.wait_ge(gate_ready, 1)
                pe.sem_inc(gate_ready, -1)
                if r == 0:
                    pe.wait_ge(misc_free[0], 1)
                    pe.sem_inc(misc_free[0], -1)
                for f in range(3 * r, 3 * r + 3):
                    last = nc.tensor.matmul(misc[0][:, 0:D], gate[:, f], w3[:, f], start=(f == 0), stop=(f == FT - 1))
                if r == 1:
                    last.then_inc(ff_ready, 1)
            elif stage in ("scat1", "scat0"):
                pr = int(stage[4])
                if pr == 1:
                    pe.wait_ge(delta_ready, 1)
                    pe.sem_inc(delta_ready, -1)
                    pe.wait_ge(selT_sb, 1)
                    pe.sem_inc(selT_sb, -1)
                pe.wait_ge(misc_free[pr], 1)
                pe.sem_inc(misc_free[pr], -1)
                for e in range(2):
                    t = 2 * pr + e
                    last = nc.tensor.matmul(misc[pr][:, e * D:(e + 1) * D], sel_t[:, t * P:(t + 1) * P], att[:],
                                            start=True, stop=True)
                last.then_inc(scat_ready, 1)

        @block.tensor
        def _(pe):
            in_general = pe.value_load(flags_i[0:1, 0:1], min_val=0, max_val=1)
            pe.wait_ge(rows_set, 16)
            pe.wait_ge(lower_set, 1)
            pe.sem_inc(lower_set, -1)

            def batches(general):
                pe_attention(pe, "", general, first=True)
                pe.wait_ge(w_in, 16 * N_W)
                pe_attention(pe, "A", general)
                with pe.Fori(2, B) as b:
                    pe_attention(pe, "AB", general)
                pe.wait_ge(s_read[0], 1)
                pe.sem_inc(s_read[0], -1)
                pe.wait_ge(s_read[1], 1)
                pe.sem_inc(s_read[1], -1)
                values(pe, G * KT - 1)

            with pe.If(in_general == 1):
                batches(True)
            with pe.Else():
                batches(False)
            for stage in PE_END:
                pe_ffn(pe, stage)


PE_SLOT = [("B", "pv0", 1), ("B", "pv1", 1), ("B", "selT", 2), ("A", "wo0", 3), ("A", "wo1", 4), ("A", "wo2", 5),
           ("A", "wo3", 6), ("B", "wout0", 7), ("B", "wout1", 8), ("A", "spread", 9), ("B", "wout2", 10),
           ("B", "wout3", 11), ("A", "gather", 13), ("A", "hidT", 15), ("A", "q", 16), ("A", "v", 17), ("A", "k0", 18),
           ("A", "k1", 18), ("B", "hid2T", 18), ("B", "u0", 19), ("B", "w0", 20), ("B", "u1", 21), ("B", "w1a", 22),
           ("B", "w1b", 22), ("A", "sc0", 24), ("A", "sc1", 25), ("B", "down0", 26), ("B", "down1", 27),
           ("B", "scat1", 28), ("B", "scat0", 29), ("A", "pT0", 30), ("A", "pT1", 31)]
ACT_SLOT = [("B", "selT", 2), ("A", "spread", 9), ("A", "hidT", 15), ("A", "qv", 17),
            ("B", "hid2T", 18), ("B", "u0", 19), ("B", "w0", 20), ("B", "u1", 21), ("B", "w1", 22), ("A", "exp0", 27), ("A", "exp1", 28),
            ("A", "pT0", 30), ("A", "pT1", 30), ("A", "pT2", 31), ("A", "pT3", 31)]
DVE_ORDER = [("B", "base"), ("B", "os"), ("A", "x1"), ("A", "y"), ("A", "rank"), ("A", "hid"), ("group", 0),
             ("B", "hid2"), ("A", "k_block"), ("group", 1), ("B", "gate0"), ("B", "gate1"), ("A", "masked"), ("A", "soft0"),
             ("A", "soft1"),
             ("B", "delta"), ("group", 2), ("B", "out"), ("A", "keep"), ("group", 3)]

PE_END = ["pv0", "pv1", "selT", "wo0", "wo1", "wo2", "wo3", "wout0", "wout1", "spread", "wout2", "wout3", "gather",
          "hidT", "q", "v", "k0", "k1", "hid2T", "sc0", "sc1", "u0", "w0", "u1", "w1a", "w1b", "pT0", "pT1", "pv0", "pv1",
          "down0", "down1", "scat1", "scat0", "wout0", "wout1", "wout2", "wout3", "selT", "hid2T",
          "u0", "w0", "u1", "w1a", "w1b", "down0", "down1", "scat1", "scat0"]
ACT_END = ["selT", "spread", "hidT", "qv", "hid2T", "u0", "w0", "u1", "w1", "exp0", "exp1", "pT0", "pT1", "pT2", "pT3",
           "selT", "hid2T", "u0", "w0", "u1", "w1"]
DVE_END = ["base", "os", "x1", "y", "rank", "hid", "hid2", "k_block", "masked", "soft0", "soft1", "gate0", "gate1", "keep", "os",
           "delta", "out", "hid2", "base", "gate0", "gate1", "delta", "out"]


def kernel(**inputs):
    import numpy as np
    import concourse.bacc as bacc
    from concourse import mybir
    from concourse.bass_utils import run_bass_kernel_spmd

    c = np.ascontiguousarray
    a = {k: np.asarray(v) for k, v in inputs.items()}

    def head_minor(w):
        return c(w.reshape(M2, H8, HD, D).transpose(0, 2, 1, 3).reshape(D, D).T)

    arrays = {
        "x": c(a["x"]),
        "ctxT": c(a["ctx_1024"].transpose(0, 2, 1)),
        "mask": c(a["mask_BxSxS2_bk0"]),
        "wqT": head_minor(a["L0_xattn_w_q"]),
        "wkT": head_minor(a["L0_xattn_w_k"]),
        "wvT": c(a["L0_xattn_w_v"].T),
        "woT": c(a["L0_xattn_w_o"].T),
        "w_router": c(a["L0_ffn_w_router"]),
        "wqkvT": c(a["L0_ffn_W_qkv"].T),
        "woutT": c(a["L0_ffn_W_out"].T),
        "g1": c(a["L0_ffn_g1"]),
        "g2": c(a["L0_ffn_g2"]),
        "w1T": c(a["L0_ffn_W1"].T),
        "w2T": c(a["L0_ffn_W2"].T),
        "w3T": c(a["L0_ffn_W3"].T),
    }
    nc = bacc.Bacc("TRN2", target_bir_lowering=False, num_devices=1)
    io = {n: nc.dram_tensor(f"in_{n}", v.shape, mybir.dt.from_np(v.dtype), kind="ExternalInput").ap()
          for n, v in arrays.items()}
    out = nc.dram_tensor("out_dram", (B, S, D), mybir.dt.float32, kind="ExternalOutput").ap()
    program(nc, io, out)
    r = run_bass_kernel_spmd(nc, [{f"in_{n}": v for n, v in arrays.items()}], core_ids=[0])
    return r.results[0]["out_dram"]
```
